# Optimizing a Trainium2 kernel written in Bass

```python
import numpy as np
import jax
import jax.numpy as jnp

def _softmax(x, axis=-1):
    return jax.nn.softmax(x, axis=axis)

def _gelu(x):
    return jax.nn.gelu(x, approximate=True)

def _silu(x):
    return jax.nn.silu(x)

def _sigmoid(x):
    return jax.nn.sigmoid(x)

def _layernorm(x, axis=-1, eps=1e-05):
    m = jnp.mean(x, axis=axis, keepdims=True)
    v = jnp.var(x, axis=axis, keepdims=True)
    return (x - m) / jnp.sqrt(v + eps)

def _scatter_add(tgt, idx, src, axis=0):
    return tgt.at[idx].add(src)

def _segment_sum(src, seg, n):
    return jax.ops.segment_sum(src, seg, n)
kernel_name = 'mk_decoder_preln_d2_seqx_r4_1b1cef'

def setup_inputs(seed: int=0):
    np.random.seed(seed)
    _w = jnp.asarray

    def _rec_inputs():
        import jax
        import jax.numpy as jnp
        _rk = jax.random.key(seed)
        x = 7.22e-05 + 1 * jax.random.normal(jax.random.fold_in(_rk, 1), (4, 512, 512), jnp.float32)
        _lenS = 512 - jax.random.randint(jax.random.fold_in(_rk, 7), (4,), 0, max(1, 512 // 4) + 1, jnp.int32)
        _lenS2 = 512 - jax.random.randint(jax.random.fold_in(_rk, 8), (4,), 0, max(1, 512 // 4) + 1, jnp.int32)
        _ctx_1024P = jax.random.normal(jax.random.fold_in(_rk, 11), (4, 16, 256), jnp.float32)
        _ctx_1024c = jax.random.dirichlet(jax.random.fold_in(_rk, 511), 0.3 * jnp.ones((16,), jnp.float32), (4, 512))
        _ctx_1024t = jnp.einsum('bsk,bkd->bsd', _ctx_1024c, _ctx_1024P)
        _ctx_1024t = _ctx_1024t * jax.lax.rsqrt(jnp.mean(jnp.square(_ctx_1024t)) + 1e-12) * 0.953939
        ctx_1024 = 2.81802e-05 + 1.00001 * (_ctx_1024t + 0.3 * jax.random.normal(jax.random.fold_in(_rk, 611), (4, 512, 256), jnp.float32))
        return (x, ctx_1024)
    x, ctx_1024 = _rec_inputs()

    def _L0_attn_setup():
        import jax, jax.numpy as jnp
        import numpy as np
        D_MODEL = 512
        N_HEAD = 16
        MLP_HIDDEN = 1408
        NORMALIZER = 16.0

        def rmsnorm(x, w, eps=1e-05):
            return x * jax.lax.rsqrt(jnp.mean(x * x, axis=-1, keepdims=True) + eps) * w

        def _reference_tuple_inner(x, Wq, Wk, Wkg1, Wkg2, bkg2, Wv, Wg, bg, Wo, ln1_w, ln2_w, W1, W3, W2):
            B, L, d = x.shape
            H = N_HEAD
            hd = d // H
            kd = d // 2 // H
            scaling = (d // H) ** (-0.5)
            xn = rmsnorm(x, ln1_w)
            q = xn @ Wq
            k = xn @ Wk * scaling
            gk = jax.nn.log_sigmoid(xn @ Wkg1 @ Wkg2 + bkg2) / NORMALIZER
            v = xn @ Wv
            g = xn @ Wg + bg
            split = lambda t, dh: t.reshape(B, L, H, dh).transpose(1, 0, 2, 3)
            qh, kh, gh = (split(q, kd), split(k, kd), split(gk, kd))
            vh = split(v, hd)
            S0 = jnp.zeros((B, H, kd, hd), x.dtype)

            def step(S, inp):
                qt, kt, vt, gt = inp
                S = S * jnp.exp(gt)[..., None] + kt[..., None] * vt[..., None, :]
                ot = jnp.einsum('bhk,bhkd->bhd', qt, S)
                return (S, ot)
            Sf, o = jax.lax.scan(step, S0, (qh, kh, vh, gh))
            mu = jnp.mean(o, axis=-1, keepdims=True)
            var = jnp.var(o, axis=-1, keepdims=True)
            o = (o - mu) * jax.lax.rsqrt(var + 1e-05)
            o = o.transpose(1, 0, 2, 3).reshape(B, L, d)
            o = jax.nn.silu(g) * o
            x = x + o @ Wo
            xn2 = rmsnorm(x, ln2_w)
            x = x + jax.nn.silu(xn2 @ W1) * (xn2 @ W3) @ W2
            return (x, Sf)
        key = jax.random.key(seed)
        d, B, L, Hd = (D_MODEL, 2, 1024, MLP_HIDDEN)
        ks = jax.random.split(key, 12)
        w = lambda k, shape, s=0.02: jax.random.normal(k, shape, jnp.float32) * s
        return {'x': jax.random.normal(ks[0], (B, L, d), jnp.float32), 'Wq': w(ks[1], (d, d // 2)), 'Wk': w(ks[2], (d, d // 2)), 'Wkg1': w(ks[3], (d, 16)), 'Wkg2': w(ks[4], (16, d // 2)), 'bkg2': jnp.zeros((d // 2,), jnp.float32), 'Wv': w(ks[5], (d, d)), 'Wg': w(ks[6], (d, d)), 'bg': jnp.zeros((d,), jnp.float32), 'Wo': w(ks[7], (d, d)), 'ln1_w': jnp.ones((d,), jnp.float32), 'ln2_w': jnp.ones((d,), jnp.float32), 'W1': w(ks[8], (d, Hd)), 'W3': w(ks[9], (d, Hd)), 'W2': w(ks[10], (Hd, d))}
    _L0_attn_all = _L0_attn_setup()
    _L0_attn_in = {k: v for k, v in _L0_attn_all.items() if k in ('Wq', 'Wk', 'Wkg1', 'Wkg2', 'bkg2', 'Wv', 'Wg', 'bg', 'Wo', 'ln1_w', 'ln2_w', 'W1', 'W3', 'W2')}
    del _L0_attn_all

    def _L0_xattn_setup():
        import jax, jax.numpy as jnp
        import numpy as np
        key = jax.random.key(seed)
        ks = jax.random.split(key, 6)
        B, L, N, C, D = (8, 128, 512, 256, 128)
        return {'teacher_logits': jax.random.normal(ks[0], (B, L, N), dtype=jnp.float32), 'teacher_features': jax.random.normal(ks[1], (B, N, C), dtype=jnp.float32), 'Wq': jax.random.normal(ks[2], (D, C), dtype=jnp.float32) * (1.0 / np.sqrt(C)), 'bq': jnp.zeros((D,), dtype=jnp.float32), 'Wk': jax.random.normal(ks[3], (D, C), dtype=jnp.float32) * (1.0 / np.sqrt(C)), 'bk': jnp.zeros((D,), dtype=jnp.float32)}
    _L0_xattn_all = _L0_xattn_setup()
    _L0_xattn_in = {k: v for k, v in _L0_xattn_all.items() if k in ('Wq', 'bq', 'Wk', 'bk')}
    del _L0_xattn_all

    def _L0_ffn_setup():
        import jax, jax.numpy as jnp
        import numpy as np
        TOPK = 2
        key = jax.random.key(seed)
        ks = jax.random.split(key, 6)
        B, T, H, S, r, ad = (2, 1024, 512, 32, 16, 32)
        h = jax.random.normal(ks[0], (B, T, H), dtype=jnp.float32)
        Wr = jax.random.normal(ks[1], (S, H), dtype=jnp.float32) * 0.02
        U = jax.random.normal(ks[2], (S, H, r), dtype=jnp.float32) * 0.02
        V = jax.random.normal(ks[3], (S, r, H), dtype=jnp.float32) * 0.02
        attr = jax.random.normal(ks[4], (S, ad), dtype=jnp.float32) * 0.02
        Wa = jax.random.normal(ks[5], (1, ad), dtype=jnp.float32) * 0.02
        return {'h': h, 'Wr': Wr, 'U': U, 'V': V, 'attr': attr, 'Wa': Wa}
    _L0_ffn_all = _L0_ffn_setup()
    _L0_ffn_in = {k: v for k, v in _L0_ffn_all.items() if k in ('Wr', 'U', 'V', 'attr', 'Wa')}
    del _L0_ffn_all

    def _L1_attn_setup():
        import jax, jax.numpy as jnp
        import numpy as np
        from jax import lax
        H = 16
        D = 128
        HID = 512
        CONV_K = 4
        CHUNK = 64
        EPS = 1e-06

        def silu(x):
            return x * jax.nn.sigmoid(x)

        def short_conv(x, w):
            B, T, C = x.shape
            K = w.shape[1]
            xp = jnp.pad(x, ((0, 0), (K - 1, 0), (0, 0)))
            y = sum((xp[:, j:j + T, :] * w[None, None, :, j] for j in range(K)))
            return silu(y)

        def l2norm(x):
            return x * lax.rsqrt(jnp.sum(x * x, -1, keepdims=True) + EPS)

        def rmsnorm(x, w):
            return x * lax.rsqrt(jnp.mean(x * x, -1, keepdims=True) + EPS) * w

        def kda_scan(q, k, v, g, beta):
            B, T, _, _ = q.shape
            NC = T // CHUNK

            def tm(a):
                a = jnp.moveaxis(a, 1, 0)
                return a.reshape((NC, CHUNK) + a.shape[1:])

            def step(S, inp):
                qt, kt, vt, gt, bt = inp
                S = S * jnp.exp(gt)[..., :, None]
                u = (vt - jnp.einsum('bhk,bhkv->bhv', kt, S)) * bt[..., None]
                S = S + kt[..., None] * u[..., None, :]
                ot = jnp.einsum('bhk,bhkv->bhv', qt, S)
                return (S, ot)

            @jax.checkpoint
            def chunk_body(S, inp):
                return lax.scan(step, S, inp)
            S0 = jnp.zeros((B, H, D, D), dtype=q.dtype)
            _, o = lax.scan(chunk_body, S0, (tm(q), tm(k), tm(v), tm(g), tm(beta)))
            o = o.reshape(T, B, H, D)
            return jnp.moveaxis(o, 0, 1)
        key = jax.random.key(seed)
        ks = jax.random.split(key, 16)
        s_h = 1.0 / np.sqrt(HID)
        s_d = 1.0 / np.sqrt(D)
        inp = {'hidden_states': jax.random.normal(ks[0], (2, 1024, HID), dtype=jnp.float32), 'Wq': jax.random.normal(ks[1], (HID, H * D), dtype=jnp.float32) * s_h, 'Wk': jax.random.normal(ks[2], (HID, H * D), dtype=jnp.float32) * s_h, 'Wv': jax.random.normal(ks[3], (HID, H * D), dtype=jnp.float32) * s_h, 'conv_q_w': jax.random.normal(ks[4], (H * D, CONV_K), dtype=jnp.float32) * 0.5, 'conv_k_w': jax.random.normal(ks[5], (H * D, CONV_K), dtype=jnp.float32) * 0.5, 'conv_v_w': jax.random.normal(ks[6], (H * D, CONV_K), dtype=jnp.float32) * 0.5, 'A_log': jnp.log(jax.random.uniform(ks[7], (1, 1, H, 1), dtype=jnp.float32, minval=1.0, maxval=16.0)), 'Wfa': jax.random.normal(ks[8], (HID, D), dtype=jnp.float32) * s_h, 'Wfb': jax.random.normal(ks[9], (D, H * D), dtype=jnp.float32) * s_d, 'dt_bias': jax.random.normal(ks[10], (H * D,), dtype=jnp.float32) * 0.5, 'Wb': jax.random.normal(ks[11], (HID, H), dtype=jnp.float32) * s_h, 'Wga': jax.random.normal(ks[12], (HID, D), dtype=jnp.float32) * s_h, 'Wgb': jax.random.normal(ks[13], (D, H * D), dtype=jnp.float32) * s_d, 'o_norm_w': jnp.ones((D,), dtype=jnp.float32), 'Wo': jax.random.normal(ks[14], (H * D, HID), dtype=jnp.float32) * s_h}
        return inp
    _L1_attn_all = _L1_attn_setup()
    _L1_attn_in = {k: v for k, v in _L1_attn_all.items() if k in ('Wq', 'Wk', 'Wv', 'conv_q_w', 'conv_k_w', 'conv_v_w', 'A_log', 'Wfa', 'Wfb', 'dt_bias', 'Wb', 'Wga', 'Wgb', 'o_norm_w', 'Wo')}
    del _L1_attn_all

    def _L1_xattn_setup():
        import jax, jax.numpy as jnp
        import numpy as np
        B, S1, S2, DCA = (2, 512, 256, 16)
        QDIM, KDIM, H = (512, 256, 16)
        HD = QDIM // H
        SCALE = HD ** (-0.5)
        EPS = 1e-06
        DCA_WEIGHT = 1.0

        def _ln(t, w, b):
            m = jnp.mean(t, axis=-1, keepdims=True)
            v = jnp.var(t, axis=-1, keepdims=True)
            return (t - m) * jax.lax.rsqrt(v + EPS) * w + b

        def _attn(q, k, v):
            s = jnp.einsum('bhqd,bhkd->bhqk', q, k) * SCALE
            p = jax.nn.softmax(s, axis=-1)
            return jnp.einsum('bhqk,bhkd->bhqd', p, v)
        key = jax.random.key(seed)
        ks = jax.random.split(key, 8)
        w = lambda k, shape: jax.random.normal(k, shape, jnp.float32) * 0.02
        return {'x': jax.random.normal(ks[0], (B, S1, QDIM), jnp.float32), 'y': jax.random.normal(ks[1], (B, S2 + DCA, KDIM), jnp.float32), 'Wq': w(ks[2], (QDIM, QDIM)), 'bq': jnp.zeros((QDIM,), jnp.float32), 'Wk': w(ks[3], (KDIM, QDIM)), 'bk': jnp.zeros((QDIM,), jnp.float32), 'Wv': w(ks[4], (KDIM, QDIM)), 'bv': jnp.zeros((QDIM,), jnp.float32), 'Wkv_dca': w(ks[5], (KDIM, 2 * QDIM)), 'bkv_dca': jnp.zeros((2 * QDIM,), jnp.float32), 'qn_w': jnp.ones((HD,), jnp.float32), 'qn_b': jnp.zeros((HD,), jnp.float32), 'kn_w': jnp.ones((HD,), jnp.float32), 'kn_b': jnp.zeros((HD,), jnp.float32), 'kn_dca_w': jnp.ones((HD,), jnp.float32), 'kn_dca_b': jnp.zeros((HD,), jnp.float32), 'Wo': w(ks[6], (QDIM, QDIM)), 'bo': jnp.zeros((QDIM,), jnp.float32)}
    _L1_xattn_all = _L1_xattn_setup()
    _L1_xattn_in = {k: v for k, v in _L1_xattn_all.items() if k in ('Wq', 'bq', 'Wk', 'bk', 'Wv', 'bv', 'Wkv_dca', 'bkv_dca', 'qn_w', 'qn_b', 'kn_w', 'kn_b', 'kn_dca_w', 'kn_dca_b', 'Wo', 'bo')}
    del _L1_xattn_all

    def _L1_ffn_setup():
        import jax, jax.numpy as jnp
        import numpy as np
        BS, SLEN, DIM, HID, E, TOPK = (4, 512, 512, 448, 8, 2)
        key = jax.random.key(seed)
        ks = jax.random.split(key, 9)
        s = 0.02
        return {'x': jax.random.normal(ks[0], (BS, SLEN, DIM), jnp.float32), 'gate_w': jax.random.normal(ks[1], (DIM, E), jnp.float32) * s, 'w1': jax.random.normal(ks[2], (E, DIM, HID), jnp.float32) * s, 'w2': jax.random.normal(ks[3], (E, HID, DIM), jnp.float32) * s, 'w3': jax.random.normal(ks[4], (E, DIM, HID), jnp.float32) * s, 'sw1': jax.random.normal(ks[5], (DIM, HID), jnp.float32) * s, 'sw2': jax.random.normal(ks[6], (HID, DIM), jnp.float32) * s, 'sw3': jax.random.normal(ks[7], (DIM, HID), jnp.float32) * s, 'expert_bias': jnp.zeros((E,), jnp.float32)}
    _L1_ffn_all = _L1_ffn_setup()
    _L1_ffn_in = {k: v for k, v in _L1_ffn_all.items() if k in ('gate_w', 'w1', 'w2', 'w3', 'sw1', 'sw2', 'sw3', 'expert_bias')}
    del _L1_ffn_all
    return {'x': x, 'ctx_1024': ctx_1024, 'L0_attn_Wq': _L0_attn_in['Wq'], 'L0_attn_Wk': _L0_attn_in['Wk'], 'L0_attn_Wkg1': _L0_attn_in['Wkg1'], 'L0_attn_Wkg2': _L0_attn_in['Wkg2'], 'L0_attn_bkg2': _L0_attn_in['bkg2'], 'L0_attn_Wv': _L0_attn_in['Wv'], 'L0_attn_Wg': _L0_attn_in['Wg'], 'L0_attn_bg': _L0_attn_in['bg'], 'L0_attn_Wo': _L0_attn_in['Wo'], 'L0_attn_ln1_w': _L0_attn_in['ln1_w'], 'L0_attn_ln2_w': _L0_attn_in['ln2_w'], 'L0_attn_W1': _L0_attn_in['W1'], 'L0_attn_W3': _L0_attn_in['W3'], 'L0_attn_W2': _L0_attn_in['W2'], 'L0_xattn_Wq': _L0_xattn_in['Wq'], 'L0_xattn_bq': _L0_xattn_in['bq'], 'L0_xattn_Wk': _L0_xattn_in['Wk'], 'L0_xattn_bk': _L0_xattn_in['bk'], 'L0_ffn_Wr': _L0_ffn_in['Wr'], 'L0_ffn_U': _L0_ffn_in['U'], 'L0_ffn_V': _L0_ffn_in['V'], 'L0_ffn_attr': _L0_ffn_in['attr'], 'L0_ffn_Wa': _L0_ffn_in['Wa'], 'L1_attn_Wq': _L1_attn_in['Wq'], 'L1_attn_Wk': _L1_attn_in['Wk'], 'L1_attn_Wv': _L1_attn_in['Wv'], 'L1_attn_conv_q_w': _L1_attn_in['conv_q_w'], 'L1_attn_conv_k_w': _L1_attn_in['conv_k_w'], 'L1_attn_conv_v_w': _L1_attn_in['conv_v_w'], 'L1_attn_A_log': _L1_attn_in['A_log'], 'L1_attn_Wfa': _L1_attn_in['Wfa'], 'L1_attn_Wfb': _L1_attn_in['Wfb'], 'L1_attn_dt_bias': _L1_attn_in['dt_bias'], 'L1_attn_Wb': _L1_attn_in['Wb'], 'L1_attn_Wga': _L1_attn_in['Wga'], 'L1_attn_Wgb': _L1_attn_in['Wgb'], 'L1_attn_o_norm_w': _L1_attn_in['o_norm_w'], 'L1_attn_Wo': _L1_attn_in['Wo'], 'L1_xattn_Wq': _L1_xattn_in['Wq'], 'L1_xattn_bq': _L1_xattn_in['bq'], 'L1_xattn_Wk': _L1_xattn_in['Wk'], 'L1_xattn_bk': _L1_xattn_in['bk'], 'L1_xattn_Wv': _L1_xattn_in['Wv'], 'L1_xattn_bv': _L1_xattn_in['bv'], 'L1_xattn_Wkv_dca': _L1_xattn_in['Wkv_dca'], 'L1_xattn_bkv_dca': _L1_xattn_in['bkv_dca'], 'L1_xattn_qn_w': _L1_xattn_in['qn_w'], 'L1_xattn_qn_b': _L1_xattn_in['qn_b'], 'L1_xattn_kn_w': _L1_xattn_in['kn_w'], 'L1_xattn_kn_b': _L1_xattn_in['kn_b'], 'L1_xattn_kn_dca_w': _L1_xattn_in['kn_dca_w'], 'L1_xattn_kn_dca_b': _L1_xattn_in['kn_dca_b'], 'L1_xattn_Wo': _L1_xattn_in['Wo'], 'L1_xattn_bo': _L1_xattn_in['bo'], 'L1_ffn_gate_w': _L1_ffn_in['gate_w'], 'L1_ffn_w1': _L1_ffn_in['w1'], 'L1_ffn_w2': _L1_ffn_in['w2'], 'L1_ffn_w3': _L1_ffn_in['w3'], 'L1_ffn_sw1': _L1_ffn_in['sw1'], 'L1_ffn_sw2': _L1_ffn_in['sw2'], 'L1_ffn_sw3': _L1_ffn_in['sw3'], 'L1_ffn_expert_bias': _L1_ffn_in['expert_bias']}

def reference(x, ctx_1024, L0_attn_Wq, L0_attn_Wk, L0_attn_Wkg1, L0_attn_Wkg2, L0_attn_bkg2, L0_attn_Wv, L0_attn_Wg, L0_attn_bg, L0_attn_Wo, L0_attn_ln1_w, L0_attn_ln2_w, L0_attn_W1, L0_attn_W3, L0_attn_W2, L0_xattn_Wq, L0_xattn_bq, L0_xattn_Wk, L0_xattn_bk, L0_ffn_Wr, L0_ffn_U, L0_ffn_V, L0_ffn_attr, L0_ffn_Wa, L1_attn_Wq, L1_attn_Wk, L1_attn_Wv, L1_attn_conv_q_w, L1_attn_conv_k_w, L1_attn_conv_v_w, L1_attn_A_log, L1_attn_Wfa, L1_attn_Wfb, L1_attn_dt_bias, L1_attn_Wb, L1_attn_Wga, L1_attn_Wgb, L1_attn_o_norm_w, L1_attn_Wo, L1_xattn_Wq, L1_xattn_bq, L1_xattn_Wk, L1_xattn_bk, L1_xattn_Wv, L1_xattn_bv, L1_xattn_Wkv_dca, L1_xattn_bkv_dca, L1_xattn_qn_w, L1_xattn_qn_b, L1_xattn_kn_w, L1_xattn_kn_b, L1_xattn_kn_dca_w, L1_xattn_kn_dca_b, L1_xattn_Wo, L1_xattn_bo, L1_ffn_gate_w, L1_ffn_w1, L1_ffn_w2, L1_ffn_w3, L1_ffn_sw1, L1_ffn_sw2, L1_ffn_sw3, L1_ffn_expert_bias):
    import jax
    import jax.numpy as jnp

    def _L0_attn_ref(x, Wq, Wk, Wkg1, Wkg2, bkg2, Wv, Wg, bg, Wo, ln1_w, ln2_w, W1, W3, W2):
        import jax, jax.numpy as jnp
        import numpy as np
        D_MODEL = 512
        N_HEAD = 16
        MLP_HIDDEN = 1408
        NORMALIZER = 16.0

        def rmsnorm(x, w, eps=1e-05):
            return x * jax.lax.rsqrt(jnp.mean(x * x, axis=-1, keepdims=True) + eps) * w

        def _reference_tuple_inner(x, Wq, Wk, Wkg1, Wkg2, bkg2, Wv, Wg, bg, Wo, ln1_w, ln2_w, W1, W3, W2):
            B, L, d = x.shape
            H = N_HEAD
            hd = d // H
            kd = d // 2 // H
            scaling = (d // H) ** (-0.5)
            xn = rmsnorm(x, ln1_w)
            q = xn @ Wq
            k = xn @ Wk * scaling
            gk = jax.nn.log_sigmoid(xn @ Wkg1 @ Wkg2 + bkg2) / NORMALIZER
            v = xn @ Wv
            g = xn @ Wg + bg
            split = lambda t, dh: t.reshape(B, L, H, dh).transpose(1, 0, 2, 3)
            qh, kh, gh = (split(q, kd), split(k, kd), split(gk, kd))
            vh = split(v, hd)
            S0 = jnp.zeros((B, H, kd, hd), x.dtype)

            def step(S, inp):
                qt, kt, vt, gt = inp
                S = S * jnp.exp(gt)[..., None] + kt[..., None] * vt[..., None, :]
                ot = jnp.einsum('bhk,bhkd->bhd', qt, S)
                return (S, ot)
            Sf, o = jax.lax.scan(step, S0, (qh, kh, vh, gh))
            mu = jnp.mean(o, axis=-1, keepdims=True)
            var = jnp.var(o, axis=-1, keepdims=True)
            o = (o - mu) * jax.lax.rsqrt(var + 1e-05)
            o = o.transpose(1, 0, 2, 3).reshape(B, L, d)
            o = jax.nn.silu(g) * o
            x = x + o @ Wo
            xn2 = rmsnorm(x, ln2_w)
            x = x + jax.nn.silu(xn2 @ W1) * (xn2 @ W3) @ W2
            return (x, Sf)
        return _reference_tuple_inner(x, Wq, Wk, Wkg1, Wkg2, bkg2, Wv, Wg, bg, Wo, ln1_w, ln2_w, W1, W3, W2)[0]

    def _L0_xattn_ref(teacher_logits, teacher_features, Wq, bq, Wk, bk):
        import jax, jax.numpy as jnp
        import numpy as np
        query = jnp.einsum('bnc,dc->bnd', teacher_features, Wq) + bq
        key = jnp.einsum('bnc,dc->bnd', teacher_features, Wk) + bk
        energy = jnp.einsum('bnd,bmd->bnm', query, key)
        attention = jax.nn.softmax(energy, axis=-1)
        x_m = jnp.einsum('bln,bmn->blm', teacher_logits, attention)
        return x_m

    def _L0_ffn_ref(h, Wr, U, V, attr, Wa):
        import jax, jax.numpy as jnp
        import numpy as np
        TOPK = 2
        S = Wr.shape[0]
        sc = jnp.einsum('bth,sh->bts', h, Wr)
        _, idx = jax.lax.top_k(sc, TOPK)
        m = jax.nn.one_hot(idx, S, dtype=sc.dtype).sum(axis=-2)
        g = jax.nn.softmax(sc, axis=-1) * m
        g = g / (g.sum(axis=-1, keepdims=True) + 1e-08)
        hU = jnp.einsum('bth,shr->btsr', h, U)
        out = jnp.einsum('bts,btsr,srh->bth', g, hU, V)
        aw = jax.nn.sigmoid(attr @ Wa[0])
        gate = (g @ aw)[..., None]
        return out * (0.9 + 0.2 * gate)

    def _L1_attn_ref(hidden_states, Wq, Wk, Wv, conv_q_w, conv_k_w, conv_v_w, A_log, Wfa, Wfb, dt_bias, Wb, Wga, Wgb, o_norm_w, Wo):
        import jax, jax.numpy as jnp
        import numpy as np
        from jax import lax
        H = 16
        D = 128
        HID = 512
        CONV_K = 4
        CHUNK = 64
        EPS = 1e-06

        def silu(x):
            return x * jax.nn.sigmoid(x)

        def short_conv(x, w):
            B, T, C = x.shape
            K = w.shape[1]
            xp = jnp.pad(x, ((0, 0), (K - 1, 0), (0, 0)))
            y = sum((xp[:, j:j + T, :] * w[None, None, :, j] for j in range(K)))
            return silu(y)

        def l2norm(x):
            return x * lax.rsqrt(jnp.sum(x * x, -1, keepdims=True) + EPS)

        def rmsnorm(x, w):
            return x * lax.rsqrt(jnp.mean(x * x, -1, keepdims=True) + EPS) * w

        def kda_scan(q, k, v, g, beta):
            B, T, _, _ = q.shape
            NC = T // CHUNK

            def tm(a):
                a = jnp.moveaxis(a, 1, 0)
                return a.reshape((NC, CHUNK) + a.shape[1:])

            def step(S, inp):
                qt, kt, vt, gt, bt = inp
                S = S * jnp.exp(gt)[..., :, None]
                u = (vt - jnp.einsum('bhk,bhkv->bhv', kt, S)) * bt[..., None]
                S = S + kt[..., None] * u[..., None, :]
                ot = jnp.einsum('bhk,bhkv->bhv', qt, S)
                return (S, ot)

            @jax.checkpoint
            def chunk_body(S, inp):
                return lax.scan(step, S, inp)
            S0 = jnp.zeros((B, H, D, D), dtype=q.dtype)
            _, o = lax.scan(chunk_body, S0, (tm(q), tm(k), tm(v), tm(g), tm(beta)))
            o = o.reshape(T, B, H, D)
            return jnp.moveaxis(o, 0, 1)
        B, T, _ = hidden_states.shape
        q = short_conv(hidden_states @ Wq, conv_q_w)
        k = short_conv(hidden_states @ Wk, conv_k_w)
        v = short_conv(hidden_states @ Wv, conv_v_w)
        g = (hidden_states @ Wfa @ Wfb).reshape(B, T, H, D)
        g = -jnp.exp(A_log) * jax.nn.softplus(g + dt_bias.reshape(1, 1, H, D))
        beta = jax.nn.sigmoid(hidden_states @ Wb)
        q = l2norm(q.reshape(B, T, H, D)) * D ** (-0.5)
        k = l2norm(k.reshape(B, T, H, D))
        v = v.reshape(B, T, H, D)
        o = kda_scan(q, k, v, g, beta)
        go = (hidden_states @ Wga @ Wgb).reshape(B, T, H, D)
        o = rmsnorm(o, o_norm_w) * jax.nn.sigmoid(go)
        o = o.reshape(B, T, H * D) @ Wo
        return o

    def _L1_xattn_ref(x, y, Wq, bq, Wk, bk, Wv, bv, Wkv_dca, bkv_dca, qn_w, qn_b, kn_w, kn_b, kn_dca_w, kn_dca_b, Wo, bo):
        import jax, jax.numpy as jnp
        import numpy as np
        B, S1, S2, DCA = (2, 512, 256, 16)
        QDIM, KDIM, H = (512, 256, 16)
        HD = QDIM // H
        SCALE = HD ** (-0.5)
        EPS = 1e-06
        DCA_WEIGHT = 1.0

        def _ln(t, w, b):
            m = jnp.mean(t, axis=-1, keepdims=True)
            v = jnp.var(t, axis=-1, keepdims=True)
            return (t - m) * jax.lax.rsqrt(v + EPS) * w + b

        def _attn(q, k, v):
            s = jnp.einsum('bhqd,bhkd->bhqk', q, k) * SCALE
            p = jax.nn.softmax(s, axis=-1)
            return jnp.einsum('bhqk,bhkd->bhqd', p, v)
        b, s1, _ = x.shape
        y_dca = y[:, -DCA:, :]
        y_main = y[:, :-DCA, :]
        kv_dca = (y_dca @ Wkv_dca + bkv_dca).reshape(b, DCA, 2, H, HD)
        k_dca = _ln(kv_dca[:, :, 0], kn_dca_w, kn_dca_b)
        v_dca = kv_dca[:, :, 1]
        s2 = y_main.shape[1]
        q = _ln((x @ Wq + bq).reshape(b, s1, H, HD), qn_w, qn_b)
        kv = jnp.concatenate([y_main @ Wk + bk, y_main @ Wv + bv], axis=-1)
        kv = kv.reshape(b, s2, H, 2 * HD)
        k = _ln(kv[..., :HD], kn_w, kn_b)
        v = kv[..., HD:]
        qT = q.transpose(0, 2, 1, 3)
        ctx = _attn(qT, k.transpose(0, 2, 1, 3), v.transpose(0, 2, 1, 3))
        ctx = ctx.transpose(0, 2, 1, 3).reshape(b, s1, QDIM)
        ctx_dca = _attn(qT, k_dca.transpose(0, 2, 1, 3), v_dca.transpose(0, 2, 1, 3))
        ctx_dca = ctx_dca.transpose(0, 2, 1, 3).reshape(b, s1, QDIM)
        ctx = ctx + DCA_WEIGHT * ctx_dca
        return ctx @ Wo + bo

    def _L1_ffn_ref(x, gate_w, w1, w2, w3, sw1, sw2, sw3, expert_bias):
        import jax, jax.numpy as jnp
        import numpy as np
        BS, SLEN, DIM, HID, E, TOPK = (4, 512, 512, 448, 8, 2)
        bs, slen, dim = x.shape
        T = bs * slen
        xf = x.reshape(T, dim)
        scores = jax.nn.softmax((xf @ gate_w).astype(jnp.float32), axis=-1)
        _, sel = jax.lax.top_k(scores + expert_bias[None, :], TOPK)
        top_scores = jnp.take_along_axis(scores, sel, axis=1)
        flat_sel = sel.reshape(-1)
        counts = jnp.bincount(flat_sel, length=E).astype(jnp.int32)
        order = jnp.argsort(flat_sel, stable=True)
        top_scores_sorted = top_scores.reshape(-1)[order]
        token_idx = order // TOPK
        routed_in = xf[token_idx] * top_scores_sorted[:, None]
        h = jax.nn.silu(jax.lax.ragged_dot(routed_in, w1, counts)) * jax.lax.ragged_dot(routed_in, w3, counts)
        routed_out = jax.lax.ragged_dot(h, w2, counts)
        out = jax.nn.silu(xf @ sw1) * (xf @ sw3) @ sw2
        out = out.at[token_idx].add(routed_out)
        return out.reshape(bs, slen, dim)
    x = x + _L0_attn_ref(_layernorm(x, axis=-1), L0_attn_Wq, L0_attn_Wk, L0_attn_Wkg1, L0_attn_Wkg2, L0_attn_bkg2, L0_attn_Wv, L0_attn_Wg, L0_attn_bg, L0_attn_Wo, L0_attn_ln1_w, L0_attn_ln2_w, L0_attn_W1, L0_attn_W3, L0_attn_W2)
    x = x + _L0_xattn_ref(_layernorm(x, axis=-1), ctx_1024, L0_xattn_Wq, L0_xattn_bq, L0_xattn_Wk, L0_xattn_bk)
    x = x + _L0_ffn_ref(_layernorm(x, axis=-1), L0_ffn_Wr, L0_ffn_U, L0_ffn_V, L0_ffn_attr, L0_ffn_Wa)
    x = x + _L1_attn_ref(_layernorm(x, axis=-1), L1_attn_Wq, L1_attn_Wk, L1_attn_Wv, L1_attn_conv_q_w, L1_attn_conv_k_w, L1_attn_conv_v_w, L1_attn_A_log, L1_attn_Wfa, L1_attn_Wfb, L1_attn_dt_bias, L1_attn_Wb, L1_attn_Wga, L1_attn_Wgb, L1_attn_o_norm_w, L1_attn_Wo)
    x = x + _L1_xattn_ref(_layernorm(x, axis=-1), ctx_1024, L1_xattn_Wq, L1_xattn_bq, L1_xattn_Wk, L1_xattn_bk, L1_xattn_Wv, L1_xattn_bv, L1_xattn_Wkv_dca, L1_xattn_bkv_dca, L1_xattn_qn_w, L1_xattn_qn_b, L1_xattn_kn_w, L1_xattn_kn_b, L1_xattn_kn_dca_w, L1_xattn_kn_dca_b, L1_xattn_Wo, L1_xattn_bo)
    x = x + _L1_ffn_ref(_layernorm(x, axis=-1), L1_ffn_gate_w, L1_ffn_w1, L1_ffn_w2, L1_ffn_w3, L1_ffn_sw1, L1_ffn_sw2, L1_ffn_sw3, L1_ffn_expert_bias)
    return x

_drawn_inputs = setup_inputs


def setup_inputs(seed=0):
    import zlib

    import numpy as np

    out = dict(_drawn_inputs(seed))
    spreads = {'L0_attn_bkg2': (0.0, 0.8),
     'L0_attn_bg': (0.0, 0.572),
     'L0_attn_ln1_w': (1.0, 0.577),
     'L0_attn_ln2_w': (1.0, 0.6),
     'L0_xattn_bq': (0.0, 0.1),
     'L0_xattn_bk': (0.0, 2.0),
     'L1_attn_o_norm_w': (1.0, 0.2),
     'L1_xattn_bq': (0.0, 0.8),
     'L1_xattn_bk': (0.0, 0.628),
     'L1_xattn_bv': (0.0, 0.592),
     'L1_xattn_bkv_dca': (0.0, 0.418),
     'L1_xattn_qn_w': (1.0, 0.6),
     'L1_xattn_qn_b': (0.0, 0.8),
     'L1_xattn_kn_w': (1.0, 0.6),
     'L1_xattn_kn_b': (0.0, 2.0),
     'L1_xattn_kn_dca_w': (1.0, 0.6),
     'L1_xattn_kn_dca_b': (0.0, 2.0),
     'L1_xattn_bo': (0.0, 0.1),
     'L1_ffn_expert_bias': (0.0, 0.8)}
    factors = {'L0_attn_Wkg1': 8.0,
     'L0_attn_Wkg2': 8.0,
     'L0_ffn_Wr': 4.307,
     'L0_ffn_U': 4.145,
     'L0_ffn_V': 4.166,
     'L0_ffn_attr': 8.0,
     'L0_ffn_Wa': 24.802,
     'L1_xattn_Wq': 2.885,
     'L1_ffn_gate_w': 8.0,
     'L1_ffn_w1': 8.0,
     'L1_ffn_w2': 8.0,
     'L1_ffn_w3': 8.0,
     'L1_ffn_sw1': 2.979,
     'L1_ffn_sw2': 2.915,
     'L1_ffn_sw3': 2.912}
    for name, (base, spread) in spreads.items():
        noise = np.random.default_rng([zlib.crc32(name.encode()), seed]).standard_normal(out[name].shape)
        drawn = base * np.exp(spread * noise) if base else spread * noise
        out[name] = jnp.asarray(drawn.astype(out[name].dtype))
    for name, factor in factors.items():
        out[name] = (out[name] * factor).astype(out[name].dtype)
    return out
```

```python
import math
from contextlib import ExitStack

import concourse.bass as bass
from concourse import mybir

ALU = mybir.AluOpType
ACT = mybir.ActivationFunctionType
AX_X = mybir.AxisListType.X
F32 = mybir.dt.float32
U32 = mybir.dt.uint32
P = 128
B, L, D = 4, 512, 512
TJ = L // P
KD = D // P
NT = B * TJ
LEVELS = [1, 2, 4, 8, 16, 32, 64]


class Signals:

    def __init__(self, nc, ctx, names, keys=None):
        self.nc = nc
        self.sems = [ctx.enter_context(nc.semaphore(n)) for n in names]
        self.of = dict(zip(keys or names, self.sems))

    def __getitem__(self, name):
        return self.of[name]

    def clear(self):
        nums = sorted(s.num for s in self.sems)
        run = [nums[0], nums[0]]
        for n in nums[1:] + [None]:
            if n == run[1] + 1:
                run[1] = n
                continue
            self.nc.sync.sem_clear(range(run[0], run[1] + 1))
            run = [n, n]

    def fresh(self):
        self.clear()
        self.nc.all_engine_barrier()


class Chip:
    pass


def rsqrt_small(act, S, src, dst, ready, done):
    act.wait_ge(S[ready], 1)
    act.activation(dst, src, ACT.Ln)
    act.drain()
    act.activation(dst, dst, ACT.Exp, scale=-0.5)
    act.drain().then_inc(S[done], 1)


def layernorm_T(nc, C, S, b, xT, w=None):
    x, xn, ps = C.x, C.xn, C.ps
    with nc.Block() as blk:
        @blk.vector
        def _(dve):
            for j in range(TJ):
                dve.bn_stats(C.st[:, j, :], x[:, TJ * b + j, :])
            dve.drain()
            for j in range(TJ):
                dve.bn_aggr(C.mv[:, j, :], C.st[:, j, :])
            dve.drain()
            dve.tensor_scalar(C.var[:, :], C.mv[:, :, 1], 1e-5, None, ALU.add)
            dve.drain().then_inc(S["ln_var"], 1)
            dve.wait_ge(S["ln_rstd"], 1)
            for j in range(TJ):
                dve.tensor_scalar(xn[:, j, :], x[:, TJ * b + j, :], C.mv[:, j, 0:1], C.rstd[:, j:j + 1],
                                  ALU.subtract, ALU.mult).then_inc(S["ln_xn"], 1)

        @blk.scalar
        def _(act):
            rsqrt_small(act, S, C.var[:, :], C.rstd[:, :], "ln_var", "ln_rstd")
            if w is None:
                for k in range(KD):
                    act.wait_ge(S["ln_tr"], k + 1)
                    act.copy(xT[:, k, :], ps[:, k, :])

        @blk.tensor
        def _(pe):
            if w is None:
                pe.wait_ge(S["ln_xn"], TJ)
                for k in range(KD):
                    for j in range(TJ):
                        mm = pe.transpose(ps[:, k, P * j:P * j + P], xn[:, j, P * k:P * k + P], C.ident[:, :])
                    mm.then_inc(S["ln_tr"], 1)
    if w is not None:
        rmsnorm_T(nc, C, S, xn, xT, w, "r1")


def rmsnorm_T(nc, C, S, src, xT, w, tag):
    ps = C.ps
    with nc.Block() as blk:
        @blk.scalar
        def _(act):
            for j in range(TJ):
                act.activation(C.xr[:, j, :], src[:, j, :], ACT.Square, accum_out=C.ss[:, j:j + 1])
            act.drain()
            act.activation(C.var[:, :], C.ss[:, :], ACT.Ln, scale=1.0 / D, bias=C.eps5[:, 0:1])
            act.drain()
            act.activation(C.rstd[:, :], C.var[:, :], ACT.Exp, scale=-0.5).then_inc(S[tag + "_rstd"], 1)
            for k in range(KD):
                act.wait_ge(S[tag + "_tr"], k + 1)
                act.activation(xT[:, k, :], ps[:, k, :], ACT.Copy, scale=w[:, k:k + 1])

        @blk.vector
        def _(dve):
            dve.wait_ge(S[tag + "_rstd"], 1)
            for j in range(TJ):
                dve.tensor_scalar(C.xr[:, j, :], src[:, j, :], C.rstd[:, j:j + 1], None,
                                  ALU.mult).then_inc(S[tag + "_xr"], 1)

        @blk.tensor
        def _(pe):
            pe.wait_ge(S[tag + "_xr"], TJ)
            for k in range(KD):
                for j in range(TJ):
                    mm = pe.transpose(ps[:, k, P * j:P * j + P], C.xr[:, j, P * k:P * k + P], C.ident[:, :])
                mm.then_inc(S[tag + "_tr"], 1)


def halves(ap, h):
    v = ap.rearrange("p (n a r) -> p n a r", a=2, r=h)
    return v[:, :, 0, :], v[:, :, 1, :]


LN_SIGNALS = ["ln_var", "ln_rstd", "ln_xn", "ln_tr"]


def load_all(nc, S, pairs, name):
    with nc.Block() as blk:
        @blk.sync
        def _(sp):
            for dst, src in pairs[0::2]:
                sp.dma_start(dst, src).then_inc(S[name], 16)
            sp.wait_ge(S[name], 16 * len(pairs))

        @blk.scalar
        def _(act):
            for dst, src in pairs[1::2]:
                act.dma_start(dst, src).then_inc(S[name], 16)


def rows(ap):
    return ap.rearrange("(k p) n -> p k n", p=P)


def everywhere(ap, p=P):
    return ap.rearrange("(a n) -> a n", a=1).broadcast_to((p, ap.shape[0]))


TILE_SIGNALS = ["gp", "qk", "qk_sb", "abs", "softplus", "summed", "decay", "products", "diag", "diag_sb",
                "q_scaled", "k_scaled", "spread", "pairs", "masked", "kt", "kt_sb", "dstate", "state", "o", "o_sb"]


def gla_layer(nc, C, W):
    H, KH, VH, F = 16, 16, 32, 1408
    FM = F // P
    x, ps, ident = C.x, C.ps, C.ident
    with ExitStack() as ctx:
        def sb(name, shape, dt=F32):
            return ctx.enter_context(nc.sbuf_tensor("g_" + name, shape, dt))

        S = Signals(nc, ctx, ["g_ld"])
        Sb = Signals(nc, ctx, LN_SIGNALS + ["r1_rstd", "r1_tr", "r1_xr", "r2_rstd", "r2_tr", "r2_xr", "m_h", "m_s",
                                            "m_g", "m_y", "m_x"])
        Sc = Signals(nc, ctx, ["c_gp", "c_p", "c_v", "c_vb"])
        St_ = [Signals(nc, ctx, [f"t{u}_{n}" for n in TILE_SIGNALS], TILE_SIGNALS) for u in range(2)]
        Sn = Signals(nc, ctx, ["n_sq", "n_rs", "n_sg", "n_o", "n_tr", "n_trc", "n_y", "n_g"])
        xa = sb("xa", [P, TJ, D])
        C.xn = xa
        C.xr = sb("xr", [P, TJ, D])
        ln1 = sb("ln1", [P, KD])
        ln2 = sb("ln2", [P, KD])
        xT = sb("xT", [P, KD, L])
        ctx2 = ExitStack()

        def sa(name, shape, dt=F32):
            return ctx2.enter_context(nc.sbuf_tensor("ga_" + name, shape, dt))
        o_all = sb("o_all", [P, NT, D])
        with ctx2:
            wq = sa("wq", [P, KD, D])
            wk = sa("wk", [P, KD, D])
            wkg1 = sa("wkg1", [P, KD, KH])
            wkg2 = sa("wkg2", [KH, D])
            bkg = sa("bkg", [P, KD])
            bkgn = sa("bkgn", [P, KD])
            wv = sa("wv", [P, KD, D])
            wg = sa("wg", [P, KD, D])
            bg = sa("bg", [P, D])
            wo = sa("wo", [P, KD, D])
            masku = sa("masku", [P, 7, 64], U32)
            bdm = sa("bdm", [P, P])
            lr = sa("lr", [KH, L])
            kS = sa("kS", [P, 2, L])
            qS = sa("qS", [P, 2, L])
            dec = sa("dec", [P, 2, L])
            dec2 = sa("dec2", [P, 2, L])
            v = sa("v", [P, TJ, D])
            g = sa("g", [P, TJ, D])
            A_ = sa("A", [P, 2, 16, P])
            o = sa("o", [P, TJ, D])
            kt = sa("kt", [P, 2, TJ, P])
            qb = sa("qb", [P, 2, TJ, 4, 64])
            work = C.xr[:, :, :].rearrange("p (a u) (c s) -> p a u c s", u=2, s=P)
            tmp, state = work[:, 0], work[:, 1]
            mom = sa("mom", [P, 2, TJ * H])

            pad = lambda t: t.rearrange("p k (h c) -> p k h c", c=32)
            S.fresh()
            with nc.Block() as blk:
                @blk.vector
                def _(dve):
                    dve.memset(wq[:, :, :], 0.0)
                    dve.memset(wk[:, :, :], 0.0)
                    dve.memset(wkg2[:, :], 0.0)
                    dve.memset(qb[:, :, :, :, :], 0.0)
                    dve.memset(bkg[:, :], 0.0)
            pairs = [(pad(w[:, :, :])[:, k, :, 0:KH],
                      W[n].rearrange("(k p) (h c) -> p k h c", p=P, c=KH)[:, k])
                     for w, n in ((wq, "L0_attn_Wq"), (wk, "L0_attn_Wk")) for k in range(KD)]
            pairs += [(wkg2[:, :].rearrange("p (h c) -> p h c", c=32)[:, :, 0:KH],
                       W["L0_attn_Wkg2"].rearrange("p (h c) -> p h c", c=KH))]
            pairs += [(bkg[32 * i:32 * i + KH, :], W["L0_attn_bkg2"][i]) for i in range(4)]
            pairs += [(wkg1[:, :, :], rows(W["L0_attn_Wkg1"])), (wv[:, :, :], rows(W["L0_attn_Wv"])),
                      (wg[:, :, :], rows(W["L0_attn_Wg"])), (wo[:, :, :], rows(W["L0_attn_Wo"])),
                      (bg[:, :], everywhere(W["L0_attn_bg"])), (ln1[:, :], W["L0_attn_ln1_w"]),
                      (ln2[:, :], W["L0_attn_ln2_w"]), 
                      (masku[:, :, :], W["c_masku"]), (bdm[:, :], W["c_heads"])]
            load_all(nc, S, pairs, "g_ld")
            with nc.Block() as blk:
                @blk.vector
                def _(dve):
                    dve.tensor_scalar(bkgn[:, :], bkg[:, :], -1.0, None, ALU.mult)

            with nc.Fori(0, B) as b:
                Sb.fresh()
                layernorm_T(nc, C, Sb, b, xT, ln1)
                Sc.fresh()
                with nc.Block() as blk:
                    @blk.tensor
                    def _(pe):
                        for k in range(KD):
                            mm = pe.matmul(ps[0:KH, 7, :], wkg1[:, k, :], xT[:, k, :], start=(k == 0),
                                           stop=(k == KD - 1))
                        mm.then_inc(Sc["c_gp"], 1)
                        for j in range(TJ):
                            for n, w in ((2 * (j % 2), wv), (2 * (j % 2) + 1, wg)):
                                if j >= 2:
                                    pe.wait_ge(Sc["c_v" if w is wv else "c_vb"], j - 1)
                                for k in range(KD):
                                    mm = pe.matmul(ps[:, n, :], xT[:, k, P * j:P * j + P], w[:, k, :],
                                                   start=(k == 0), stop=(k == KD - 1))
                                mm.then_inc(Sc["c_p"], 1)

                    @blk.scalar
                    def _(act):
                        act.wait_ge(Sc["c_gp"], 1)
                        act.copy(lr[:, :], ps[0:KH, 7, :])
                        for j in range(TJ):
                            act.wait_ge(Sc["c_p"], 2 * j + 1)
                            act.copy(v[:, j, :], ps[:, 2 * (j % 2), :]).then_inc(Sc["c_v"], 1)
                        for j in range(TJ):
                            act.wait_ge(Sc["c_vb"], j + 1)
                            act.activation(g[:, j, :], g[:, j, :], ACT.Silu)

                    @blk.vector
                    def _(dve):
                        for j in range(TJ):
                            dve.wait_ge(Sc["c_p"], 2 * j + 2)
                            dve.tensor_tensor(g[:, j, :], ps[:, 2 * (j % 2) + 1, :], bg[:, :], ALU.add
                                              ).then_inc(Sc["c_vb"], 1)
                for t0 in range(0, KD, 2):
                    for s in St_:
                        s.clear()
                    nc.all_engine_barrier()
                    with nc.Block() as blk:
                        def hs(u):
                            return slice(P * (t0 + u), P * (t0 + u) + P)

                        def pair_bank(u, l, m):
                            return 4 * u + 2 * (l % 2) + m

                        @blk.tensor
                        def _(pe):
                            for u in range(2):
                                s = St_[u]
                                pe.matmul(ps[:, 4 * u, :], wkg2[:, hs(u)], lr[:, :], start=True, stop=True
                                          ).then_inc(s["gp"], 1)
                                for n, w in ((1, wq), (2, wk)):
                                    for k in range(KD):
                                        mm = pe.matmul(ps[:, 4 * u + n, :], w[:, k, hs(u)], xT[:, k, :],
                                                       start=(k == 0), stop=(k == KD - 1))
                                    mm.then_inc(s["qk"], 1)
                            for u in range(2):
                                s = St_[u]
                                pe.wait_ge(s["products"], 1)
                                for c in range(TJ):
                                    mm = pe.matmul(ps[:, 4 * u + 3, 4 * c:4 * c + 4], tmp[:, u, c, :],
                                                   bdm[:, 0:P:32], start=True, stop=True)
                                mm.then_inc(s["diag"], 1)
                            for l, w in enumerate(LEVELS):
                                for u in range(2):
                                    s = St_[u]
                                    pe.wait_ge(s["spread"], l + 1)
                                    if l == 0:
                                        pe.wait_ge(s["summed"], 1)
                                        pe.wait_ge(s["qk_sb"], 2)
                                    else:
                                        pe.wait_ge(s["k_scaled"], l)
                                    if l == 1:
                                        pe.wait_ge(s["diag_sb"], 1)
                                    if l >= 2:
                                        pe.wait_ge(s["masked"], 2 * (l - 1))
                                    for c in range(TJ):
                                        a = 256 * (c % 2)
                                        mm = pe.matmul(ps[:, pair_bank(u, l, c // 2), a:a + 256],
                                                       kS[:, u, P * c:P * c + P],
                                                       qb[:, u, c, :, :].rearrange("p i t -> p (i t)"),
                                                       start=True, stop=True)
                                    mm.then_inc(s["pairs"], 1)
                            for u in range(2):
                                s = St_[u]
                                pe.wait_ge(s["k_scaled"], len(LEVELS))
                                pe.wait_ge(s["q_scaled"], len(LEVELS) + 1)
                                pe.wait_ge(s["masked"], 2 * len(LEVELS))
                                for c in range(TJ):
                                    mm = pe.transpose(ps[:, 4 * u, P * c:P * c + P], kS[:, u, P * c:P * c + P],
                                                      ident[:, :])
                                mm.then_inc(s["kt"], 1)
                            for c in range(TJ):
                                for u in range(2):
                                    s = St_[u]
                                    if c == 0:
                                        pe.wait_ge(s["kt_sb"], 1)
                                    if c < TJ - 1:
                                        if c >= 1:
                                            pe.wait_ge(s["state"], c)
                                        pe.matmul(ps[:, 4 * u + 3, 0:P], kt[:, u, c, :], v[:, c, hs(u)],
                                                  start=True, stop=True).then_inc(s["dstate"], 1)
                                    oc = ps[:, 4 * u + 1 + c % 2, 0:P]
                                    if c >= 2:
                                        pe.wait_ge(s["o_sb"], c - 1)
                                    if c >= 1:
                                        pe.wait_ge(s["state"], c)
                                        pe.matmul(oc, qS[:, u, P * c:P * c + P], state[:, u, c - 1, :], start=True,
                                                  stop=False, skip_group_check=True)
                                    for i in range(4):
                                        a = P * (t0 + u) + VH * i
                                        mm = pe.matmul(oc[:, VH * i:VH * i + VH], A_[:, u, 4 * c + i, :],
                                                       v[:, c, a:a + VH], start=(c == 0), stop=(i == 3),
                                                       skip_group_check=True)
                                    mm.then_inc(s["o"], 1)

                        @blk.scalar
                        def _(act):
                            for u in range(2):
                                act.wait_ge(St_[u]["gp"], 1)
                                act.activation(dec2[:, u, :], ps[:, 4 * u, :], ACT.Abs, bias=bkg[:, t0 + u:t0 + u + 1])
                                act.drain().then_inc(St_[u]["abs"], 1)
                                act.activation(dec2[:, u, :], dec2[:, u, :], ACT.Exp, scale=-1.0)
                            act.drain()
                            for u in range(2):
                                act.activation(dec2[:, u, :], dec2[:, u, :], ACT.Ln, bias=1.0
                                               ).then_inc(St_[u]["softplus"], 1)
                            for u in range(2):
                                s = St_[u]
                                act.wait_ge(s["qk"], 1)
                                act.copy(qS[:, u, :], ps[:, 4 * u + 1, :]).then_inc(s["qk_sb"], 1)
                                act.wait_ge(s["qk"], 2)
                                act.mul(kS[:, u, :], ps[:, 4 * u + 2, :], float(VH) ** -0.5).then_inc(s["qk_sb"], 1)
                            for u in range(2):
                                act.wait_ge(St_[u]["summed"], 1)
                                act.activation(dec[:, u, :], dec[:, u, :], ACT.Exp, scale=-1.0 / 16.0
                                               ).then_inc(St_[u]["decay"], 1)
                            for l, w in enumerate(LEVELS):
                                for u in range(2):
                                    s = St_[u]
                                    act.wait_ge(s["q_scaled"], l + 1)
                                    if l:
                                        act.wait_ge(s["pairs"], l)
                                    for i in range(4):
                                        r = slice(32 * i, 32 * i + 32)
                                        act.copy(qb[r, u, :, i, :].rearrange("p c (n r) -> p c n r", r=w),
                                                 halves(qS[r, u, :], w)[1].rearrange("p (c n) r -> p c n r", c=TJ))
                                    act.drain().then_inc(s["spread"], 1)
                            for u in range(2):
                                act.wait_ge(St_[u]["kt"], 1)
                                act.copy(kt[:, u, :, :].rearrange("p c s -> p (c s)"), ps[:, 4 * u, :]
                                         ).then_inc(St_[u]["kt_sb"], 1)
                            for c in range(TJ):
                                for u in range(2):
                                    act.wait_ge(St_[u]["o"], c + 1)
                                    act.copy(o[:, c, hs(u)], ps[:, 4 * u + 1 + c % 2, 0:P]).then_inc(St_[u]["o_sb"], 1)

                        @blk.vector
                        def _(dve):
                            for u in range(2):
                                dve.wait_ge(St_[u]["abs"], 1)
                                dve.tensor_scalar(dec[:, u, :], ps[:, 4 * u, :], -1.0, bkgn[:, t0 + u:t0 + u + 1],
                                                  ALU.mult, ALU.add)
                                dve.drain()
                                dve.tensor_scalar(dec[:, u, :], dec[:, u, :], 0.0, None, ALU.max)
                            dve.drain()
                            for u in range(2):
                                dve.wait_ge(St_[u]["softplus"], 1)
                                dve.tensor_tensor(dec[:, u, :], dec[:, u, :], dec2[:, u, :], ALU.add
                                                  ).then_inc(St_[u]["summed"], 1)
                            for u in range(2):
                                dve.wait_ge(St_[u]["qk_sb"], 2)
                                dve.tensor_tensor(tmp[:, u, :, :].rearrange("p c s -> p (c s)"), qS[:, u, :],
                                                  kS[:, u, :], ALU.mult).then_inc(St_[u]["products"], 1)
                            for u in range(2):
                                dve.wait_ge(St_[u]["diag"], 1)
                                dve.tensor_tensor(A_[:, u, :, :],
                                                  ps[:, 4 * u + 3, 0:16].unsqueeze(2).broadcast_to((P, 16, P)),
                                                  ident[:, :].unsqueeze(1).broadcast_to((P, 16, P)), ALU.mult
                                                  ).then_inc(St_[u]["diag_sb"], 1)
                            dve.drain()
                            for l, w in enumerate(LEVELS):
                                for u in range(2):
                                    dve.wait_ge(St_[u]["pairs"], l + 1)
                                    for m in range(2):
                                        Av = A_[:, u, 8 * m:8 * m + 8, :].rearrange("p c (n a r) -> p c n a r",
                                                                                    a=2, r=w)
                                        dve.copy_predicated(
                                            Av[:, :, :, 1, :],
                                            masku[:, l, :].unsqueeze(1).broadcast_to((P, 8, 64)).rearrange(
                                                "p c (n r) -> p c n r", r=w),
                                            ps[:, pair_bank(u, l, m), :].rearrange("p (c n r) -> p c n r", c=8, r=w)
                                        ).then_inc(St_[u]["masked"], 1)
                                dve.drain()
                            Dc = dec2 if len(LEVELS) % 2 else dec
                            for c in range(TJ - 1):
                                for u in range(2):
                                    s = St_[u]
                                    dve.wait_ge(s["dstate"], c + 1)
                                    to = state[:, u, c, :]
                                    if c == 0:
                                        dve.tensor_tensor(to, ps[:, 4 * u + 3, 0:P], bdm[:, :], ALU.mult)
                                    else:
                                        dve.tensor_tensor(tmp[:, u, c, :], ps[:, 4 * u + 3, 0:P], bdm[:, :], ALU.mult)
                                        dve.drain()
                                        dve.scalar_tensor_tensor(to, state[:, u, c - 1, :], Dc[:, u, c:c + 1],
                                                                 tmp[:, u, c, :], ALU.mult, ALU.add)
                                    dve.drain().then_inc(s["state"], 1)

                        @blk.gpsimd
                        def _(pool):
                            for u in range(2):
                                pool.wait_ge(St_[u]["decay"], 1)
                                pool.wait_ge(St_[u]["products"], 1)
                                pool.tensor_tensor(qS[:, u, :], qS[:, u, :], dec[:, u, :], ALU.mult)
                                pool.drain().then_inc(St_[u]["q_scaled"], 1)
                            src = dec
                            for l, w in enumerate(LEVELS):
                                dst = dec2 if l % 2 == 0 else dec
                                nblk = L // (2 * w)
                                for u in range(2):
                                    pr = src[:, u, 0:2 * nblk].rearrange("p (n a) -> p n a", a=2)
                                    q2 = halves(qS[:, u, :], w)[1]
                                    pool.wait_ge(St_[u]["spread"], l + 1)
                                    pool.tensor_tensor(q2, q2, pr[:, :, 0:1].broadcast_to((P, nblk, w)), ALU.mult)
                                    pool.tensor_tensor(dst[:, u, 0:nblk], pr[:, :, 0], pr[:, :, 1], ALU.mult)
                                    pool.drain().then_inc(St_[u]["q_scaled"], 1)
                                for u in range(2):
                                    pr = src[:, u, 0:2 * nblk].rearrange("p (n a) -> p n a", a=2)
                                    k1 = halves(kS[:, u, :], w)[0]
                                    pool.wait_ge(St_[u]["pairs"], l + 1)
                                    pool.tensor_tensor(k1, k1, pr[:, :, 1:2].broadcast_to((P, nblk, w)), ALU.mult)
                                    pool.drain().then_inc(St_[u]["k_scaled"], 1)
                                src = dst
                Sn.fresh()
                with nc.Block() as blk:
                    ov = o[:, :, :].rearrange("p j (h d) -> p (j h) d", d=VH)
                    rv = C.xr[:, :, :].rearrange("p j (h d) -> p (j h) d", d=VH)

                    def each(m):
                        return mom[:, m, :].unsqueeze(2).broadcast_to((P, TJ * H, VH))

                    @blk.vector
                    def _(dve):
                        dve.tensor_reduce(mom[:, 0, :], ov, AX_X, ALU.add)
                        dve.drain()
                        dve.tensor_scalar(mom[:, 0, :], mom[:, 0, :], 1.0 / VH, None, ALU.mult)
                        dve.drain()
                        dve.tensor_tensor(ov, ov, each(0), ALU.subtract)
                        dve.drain()
                        dve.tensor_tensor(rv, ov, ov, ALU.mult)
                        dve.drain()
                        dve.tensor_reduce(mom[:, 1, :], rv, AX_X, ALU.add)
                        dve.drain().then_inc(Sn["n_sq"], 1)
                        dve.wait_ge(Sn["n_rs"], 1)
                        dve.tensor_tensor(ov, ov, each(1), ALU.mult)
                        dve.drain()
                        dve.tensor_tensor(o[:, :, :], o[:, :, :], g[:, :, :], ALU.mult)
                        dve.drain().then_inc(Sn["n_o"], 1)
                        for j in range(TJ):
                            dve.wait_ge(Sn["n_y"], j + 1)
                            dve.tensor_tensor(o_all[:, bass.ds(TJ * b + j, 1), :].rearrange("p a d -> p (a d)"),
                                              xa[:, j, :], ps[:, 4 + j, :], ALU.add)

                    @blk.scalar
                    def _(act):
                        act.wait_ge(Sn["n_sq"], 1)
                        act.activation(mom[:, 1, :], mom[:, 1, :], ACT.Ln, scale=1.0 / VH, bias=C.eps5[:, 0:1])
                        act.drain()
                        act.activation(mom[:, 1, :], mom[:, 1, :], ACT.Exp, scale=-0.5)
                        act.drain().then_inc(Sn["n_rs"], 1)
                        for k in range(KD):
                            act.wait_ge(Sn["n_tr"], k + 1)
                            act.copy(xT[:, k, :], ps[:, k, :]).then_inc(Sn["n_trc"], 1)

                    @blk.tensor
                    def _(pe):
                        pe.wait_ge(Sn["n_o"], 1)
                        for k in range(KD):
                            for j in range(TJ):
                                mm = pe.transpose(ps[:, k, P * j:P * j + P], o[:, j, P * k:P * k + P], ident[:, :])
                            mm.then_inc(Sn["n_tr"], 1)
                        pe.wait_ge(Sn["n_trc"], KD)
                        for j in range(TJ):
                            for k in range(KD):
                                mm = pe.matmul(ps[:, 4 + j, :], xT[:, k, P * j:P * j + P], wo[:, k, :],
                                               start=(k == 0), stop=(k == KD - 1))
                            mm.then_inc(Sn["n_y"], 1)

        w1 = sb("w1", [P, KD, F])
        w3 = sb("w3", [P, KD, F])
        w2 = sb("w2", [P, FM, D])
        sl = sb("sl", [P, 2, L])
        hT = sb("hT", [P, FM, L])
        S.fresh()
        load_all(nc, S, [(w1[:, :, :], rows(W["L0_attn_W1"])), (w3[:, :, :], rows(W["L0_attn_W3"])),
                         (w2[:, :, :], rows(W["L0_attn_W2"]))], "g_ld")
        with nc.Fori(0, B) as b:
            Sb.fresh()
            with nc.Block() as blk:
                @blk.vector
                def _(dve):
                    dve.tensor_copy(xa[:, :, :], o_all[:, bass.ds(TJ * b, TJ), :])
                    for j in range(TJ):
                        xj = x[:, bass.ds(TJ * b + j, 1), :]
                        dve.tensor_tensor(xj, xj, o_all[:, bass.ds(TJ * b + j, 1), :], ALU.add)
            rmsnorm_T(nc, C, Sb, xa, xT, ln2, "r2")
            with nc.Block() as blk:
                @blk.tensor
                def _(pe):
                    for m in range(FM):
                        for n, w in ((0, w1), (1, w3)):
                            if m >= 2:
                                pe.wait_ge(Sb["m_g" if n else "m_s"], m - 1)
                            for k in range(KD):
                                mm = pe.matmul(ps[:, 2 * (m % 2) + n, :], w[:, k, P * m:P * m + P], xT[:, k, :],
                                               start=(k == 0), stop=(k == KD - 1))
                            mm.then_inc(Sb["m_h"], 1)
                    pe.wait_ge(Sb["m_g"], FM)
                    for j in range(TJ):
                        for m in range(FM):
                            mm = pe.matmul(ps[:, 4 + j, :], hT[:, m, P * j:P * j + P], w2[:, m, :],
                                           start=(m == 0), stop=(m == FM - 1))
                        mm.then_inc(Sb["m_y"], 1)

                @blk.scalar
                def _(act):
                    for m in range(FM):
                        act.wait_ge(Sb["m_h"], 2 * m + 1)
                        if m >= 2:
                            act.wait_ge(Sb["m_g"], m - 1)
                        act.activation(sl[:, m % 2, :], ps[:, 2 * (m % 2), :], ACT.Silu).then_inc(Sb["m_s"], 1)

                @blk.vector
                def _(dve):
                    for m in range(FM):
                        dve.wait_ge(Sb["m_h"], 2 * m + 2)
                        dve.wait_ge(Sb["m_s"], m + 1)
                        dve.tensor_tensor(hT[:, m, :], sl[:, m % 2, :], ps[:, 2 * (m % 2) + 1, :], ALU.mult
                                          ).then_inc(Sb["m_g"], 1)
                    for j in range(TJ):
                        dve.wait_ge(Sb["m_y"], j + 1)
                        xj = x[:, bass.ds(TJ * b + j, 1), :].rearrange("p a d -> p (a d)")
                        dve.tensor_tensor(xj, xj, ps[:, 4 + j, :], ALU.add)


def context_mix(nc, C, W):
    CK = 2
    x, ps, ident = C.x, C.ps, C.ident
    with ExitStack() as ctx:
        def sb(name, shape, dt=F32):
            return ctx.enter_context(nc.sbuf_tensor("m_" + name, shape, dt))

        S = Signals(nc, ctx, ["m_ld"])
        Sb = Signals(nc, ctx, LN_SIGNALS + ["m_ctx", "m_qk", "m_qkc", "m_e", "m_max", "m_exp", "m_p", "m_at", "m_atc",
                                            "m_yy"])
        C.xn = sb("xn", [P, TJ, D])
        xT = sb("xT", [P, KD, L])
        wq = sb("wq", [P, CK, P])
        wk = sb("wk", [P, CK, P])
        bq = sb("bq", [P, 1])
        bk = sb("bk", [P, 1])
        cT = sb("cT", [P, CK, L])
        qT = sb("qT", [P, L])
        kT = sb("kT", [P, L])
        att = sb("att", [P, TJ, L])
        attT = sb("attT", [P, TJ, L])
        mx = sb("mx", [P, TJ])
        sm = sb("sm", [P, TJ])
        S.fresh()
        load_all(nc, S, [(wq[:, :, :], rows(W["L0_xattn_Wq"])), (wk[:, :, :], rows(W["L0_xattn_Wk"])),
                         (bq[:, :], W["L0_xattn_bq"]), (bk[:, :], W["L0_xattn_bk"])], "m_ld")
        with nc.Fori(0, B) as b:
            Sb.fresh()
            layernorm_T(nc, C, Sb, b, xT)
            with nc.Block() as blk:
                @blk.sync
                def _(sp):
                    sp.dma_start(cT[:, :, :], W["ctx_1024"].rearrange("b (k p) n -> b p k n", p=P)[
                        bass.ds(b, 1)].rearrange("a p k n -> (a p) k n")).then_inc(Sb["m_ctx"], 16)

                @blk.tensor
                def _(pe):
                    pe.wait_ge(Sb["m_ctx"], 16)
                    for n, w in ((4, wq), (5, wk)):
                        for k in range(CK):
                            mm = pe.matmul(ps[:, n, :], w[:, k, :], cT[:, k, :], start=(k == 0), stop=(k == CK - 1))
                        mm.then_inc(Sb["m_qk"], 1)
                    pe.wait_ge(Sb["m_qkc"], 2)
                    for m in range(TJ):
                        pe.matmul(ps[:, m, :], qT[:, P * m:P * m + P], kT[:, :], start=True, stop=True
                                  ).then_inc(Sb["m_e"], 1)
                    pe.wait_ge(Sb["m_p"], TJ)
                    for n in range(TJ):
                        for m in range(TJ):
                            mm = pe.transpose(ps[:, 4 + n, P * m:P * m + P], att[:, m, P * n:P * n + P], ident[:, :])
                        mm.then_inc(Sb["m_at"], 1)
                    pe.wait_ge(Sb["m_atc"], TJ)
                    for j in range(TJ):
                        for n in range(TJ):
                            mm = pe.matmul(ps[:, j, :], xT[:, n, P * j:P * j + P], attT[:, n, :],
                                           start=(n == 0), stop=(n == TJ - 1))
                        mm.then_inc(Sb["m_yy"], 1)

                @blk.scalar
                def _(act):
                    act.wait_ge(Sb["m_qk"], 1)
                    act.activation(qT[:, :], ps[:, 4, :], ACT.Identity, bias=bq[:, 0:1]).then_inc(Sb["m_qkc"], 1)
                    act.wait_ge(Sb["m_qk"], 2)
                    act.activation(kT[:, :], ps[:, 5, :], ACT.Identity, bias=bk[:, 0:1]).then_inc(Sb["m_qkc"], 1)
                    for m in range(TJ):
                        act.wait_ge(Sb["m_max"], m + 1)
                        act.activation(att[:, m, :], ps[:, m, :], ACT.Exp, bias=mx[:, m:m + 1],
                                       accum_out=sm[:, m:m + 1])
                        act.drain().then_inc(Sb["m_exp"], 1)
                    for n in range(TJ):
                        act.wait_ge(Sb["m_at"], n + 1)
                        act.copy(attT[:, n, :], ps[:, 4 + n, :]).then_inc(Sb["m_atc"], 1)

                @blk.vector
                def _(dve):
                    for m in range(TJ):
                        dve.wait_ge(Sb["m_e"], m + 1)
                        dve.tensor_reduce(mx[:, m:m + 1], ps[:, m, :], AX_X, ALU.max, negate=True)
                        dve.drain().then_inc(Sb["m_max"], 1)
                    for m in range(TJ):
                        dve.wait_ge(Sb["m_exp"], m + 1)
                        dve.reciprocal(sm[:, m:m + 1], sm[:, m:m + 1])
                        dve.drain()
                        dve.tensor_scalar(att[:, m, :], att[:, m, :], sm[:, m:m + 1], None, ALU.mult
                                          ).then_inc(Sb["m_p"], 1)
                    for j in range(TJ):
                        dve.wait_ge(Sb["m_yy"], j + 1)
                        xj = x[:, bass.ds(TJ * b + j, 1), :].rearrange("p a d -> p (a d)")
                        dve.tensor_tensor(xj, xj, ps[:, j, :], ALU.add)


def top_two(dve, vals, top, idx, idxf, iota, sel, n):
    dve.max(top, vals)
    dve.drain()
    dve.max_index(idx, top, vals)
    dve.drain()
    dve.tensor_copy(idxf, idx[:, 0:2])
    dve.drain()
    dve.tensor_scalar(sel, iota[:, 0:n], idxf[:, 0:1], None, ALU.is_equal)
    dve.drain()
    dve.scalar_tensor_tensor(sel, iota[:, 0:n], idxf[:, 1:2], sel, ALU.is_equal, ALU.add)
    dve.drain()


def low_rank_ffn(nc, C, W):
    NS, R, AD = 32, 16, 32
    x, ps, ident = C.x, C.ps, C.ident
    with ExitStack() as ctx:
        def sb(name, shape, dt=F32):
            return ctx.enter_context(nc.sbuf_tensor("f_" + name, shape, dt))

        S = Signals(nc, ctx, ["f_ld", "f_aw"])
        Sb = Signals(nc, ctx, LN_SIGNALS + ["f_sc", "f_scc", "f_max", "f_exp", "f_hu", "f_hg", "f_tr", "f_trc", "f_y"])
        C.xn = sb("xn", [P, TJ, D])
        xT = sb("xT", [P, KD, L])
        wr = sb("wr", [P, KD, NS])
        U = sb("U", [P, KD, NS * R])
        V = sb("V", [P, KD, D])
        attr = sb("attr", [P, NS, AD])
        wa = sb("wa", [P, AD])
        aw = sb("aw", [P, NS])
        iota = sb("iota", [P, NS])
        sc = sb("sc", [P, TJ, NS])
        top = sb("top", [P, TJ, 8])
        idx = sb("idx", [P, TJ, 8], U32)
        idxf = sb("idxf", [P, TJ, 2])
        sel = sb("sel", [P, TJ, NS])
        e = sb("e", [P, TJ, NS])
        nmx = sb("nmx", [P, TJ])
        sm = sb("sm", [P, TJ])
        gs = sb("gs", [P, TJ])
        gate = sb("gate", [P, TJ])
        hg = sb("hg", [P, TJ, NS * R])
        hgT = sb("hgT", [P, KD, L])
        S.fresh()
        load_all(nc, S, [(wr[:, :, :], rows(W["L0_ffn_Wr"])), (U[:, :, :], rows(W["L0_ffn_U"])),
                         (V[:, :, :], rows(W["L0_ffn_V"])),
                         (attr[:, :, :].rearrange("p s a -> p (s a)"), everywhere(W["L0_ffn_attr"].rearrange("s a -> (s a)"))),
                         (wa[:, :], everywhere(W["L0_ffn_Wa"].rearrange("o a -> (o a)"))),
                         (iota[:, :], everywhere(W["c_iota"]))], "f_ld")
        with nc.Block() as blk:
            @blk.vector
            def _(dve):
                dve.tensor_tensor(attr[:, :, :], attr[:, :, :], wa[:, :].unsqueeze(1).broadcast_to((P, NS, AD)), ALU.mult)
                dve.drain()
                dve.tensor_reduce(aw[:, :], attr[:, :, :], AX_X, ALU.add)
                dve.drain().then_inc(S["f_aw"], 1)

            @blk.scalar
            def _(act):
                act.wait_ge(S["f_aw"], 1)
                act.activation(aw[:, :], aw[:, :], ACT.Sigmoid)
        with nc.Fori(0, B) as b:
            Sb.fresh()
            layernorm_T(nc, C, Sb, b, xT)
            with nc.Block() as blk:
                @blk.tensor
                def _(pe):
                    for j in range(TJ):
                        for k in range(KD):
                            mm = pe.matmul(ps[:, 0, NS * j:NS * j + NS], xT[:, k, P * j:P * j + P], wr[:, k, :],
                                           start=(k == 0), stop=(k == KD - 1))
                    mm.then_inc(Sb["f_sc"], 1)
                    for j in range(TJ):
                        for k in range(KD):
                            mm = pe.matmul(ps[:, 4 + j, :], xT[:, k, P * j:P * j + P], U[:, k, :],
                                           start=(k == 0), stop=(k == KD - 1))
                        mm.then_inc(Sb["f_hu"], 1)
                    pe.wait_ge(Sb["f_hg"], TJ)
                    for k in range(KD):
                        for j in range(TJ):
                            mm = pe.transpose(ps[:, k, P * j:P * j + P], hg[:, j, P * k:P * k + P], ident[:, :])
                        mm.then_inc(Sb["f_tr"], 1)
                    pe.wait_ge(Sb["f_trc"], KD)
                    for j in range(TJ):
                        for k in range(KD):
                            mm = pe.matmul(ps[:, 4 + j, :], hgT[:, k, P * j:P * j + P], V[:, k, :],
                                           start=(k == 0), stop=(k == KD - 1))
                        mm.then_inc(Sb["f_y"], 1)

                @blk.scalar
                def _(act):
                    act.wait_ge(Sb["f_sc"], 1)
                    act.copy(sc[:, :, :], ps[:, 0, 0:TJ * NS].rearrange("p (j s) -> p j s", s=NS)
                             ).then_inc(Sb["f_scc"], 1)
                    act.wait_ge(Sb["f_max"], 1)
                    for j in range(TJ):
                        act.activation(e[:, j, :], sc[:, j, :], ACT.Exp, bias=nmx[:, j:j + 1], accum_out=sm[:, j:j + 1])
                    act.drain().then_inc(Sb["f_exp"], 1)
                    for k in range(KD):
                        act.wait_ge(Sb["f_tr"], k + 1)
                        act.copy(hgT[:, k, :], ps[:, k, :]).then_inc(Sb["f_trc"], 1)

                @blk.vector
                def _(dve):
                    dve.wait_ge(Sb["f_scc"], 1)
                    dve.tensor_reduce(nmx[:, :], sc[:, :, :], AX_X, ALU.max, negate=True)
                    dve.drain().then_inc(Sb["f_max"], 1)
                    for j in range(TJ):
                        top_two(dve, sc[:, j, :], top[:, j, :], idx[:, j, :], idxf[:, j, :], iota, sel[:, j, :], NS)
                    dve.wait_ge(Sb["f_exp"], 1)
                    dve.reciprocal(sm[:, :], sm[:, :])
                    dve.drain()
                    dve.tensor_tensor(e[:, :, :], e[:, :, :], sm[:, :].unsqueeze(2).broadcast_to((P, TJ, NS)), ALU.mult)
                    dve.drain()
                    dve.tensor_tensor(e[:, :, :], e[:, :, :], sel[:, :, :], ALU.mult)
                    dve.drain()
                    dve.tensor_reduce(gs[:, :], e[:, :, :], AX_X, ALU.add)
                    dve.drain()
                    dve.tensor_scalar(gs[:, :], gs[:, :], 1e-8, None, ALU.add)
                    dve.drain()
                    dve.reciprocal(gs[:, :], gs[:, :])
                    dve.drain()
                    dve.tensor_tensor(e[:, :, :], e[:, :, :], gs[:, :].unsqueeze(2).broadcast_to((P, TJ, NS)), ALU.mult)
                    dve.drain()
                    for j in range(TJ):
                        dve.wait_ge(Sb["f_hu"], j + 1)
                        dve.tensor_tensor(hg[:, j, :].rearrange("p (s r) -> p s r", r=R),
                                          ps[:, 4 + j, :].rearrange("p (s r) -> p s r", r=R),
                                          e[:, j, :].unsqueeze(2).broadcast_to((P, NS, R)), ALU.mult
                                          ).then_inc(Sb["f_hg"], 1)
                    dve.tensor_tensor(sel[:, :, :], e[:, :, :], aw[:, :].unsqueeze(1).broadcast_to((P, TJ, NS)), ALU.mult)
                    dve.drain()
                    dve.tensor_reduce(gate[:, :], sel[:, :, :], AX_X, ALU.add)
                    dve.drain()
                    dve.tensor_scalar(gate[:, :], gate[:, :], 0.2, 0.9, ALU.mult, ALU.add)
                    dve.drain()
                    for j in range(TJ):
                        dve.wait_ge(Sb["f_y"], j + 1)
                        xj = x[:, bass.ds(TJ * b + j, 1), :].rearrange("p a d -> p (a d)")
                        dve.scalar_tensor_tensor(xj, ps[:, 4 + j, :], gate[:, j:j + 1], xj, ALU.mult, ALU.add)


def delta_attention(nc, C, W):
    LAST = len(LEVELS) - 1
    H, NCH = 16, NT
    TOK = B * L
    x, ps, ident = C.x, C.ps, C.ident
    with ExitStack() as ctx:
        def sb(name, shape, dt=F32):
            return ctx.enter_context(nc.sbuf_tensor("d_" + name, shape, dt))

        S = Signals(nc, ctx, ["d_ld", "d_scr"] + LN_SIGNALS)
        Sp = Signals(nc, ctx, ["p_w", "p_raw", "p_pad", "p_conv", "p_silu", "p_sq", "p_ss", "p_nk", "p_gate",
                               "p_abs", "p_max", "p_sp", "p_sum", "p_dec", "p_go", "p_th", "p_beta", "p_gfree",
                               "p_go_free", "p_khat", "p_kn", "p_q2", "p_vt", "p_vs", "p_dg", "p_dgm"])
        Sl = Signals(nc, ctx, ["l_pairs", "l_masked", "l_scaled", "l_y", "l_yc", "l_upd", "l_new", "l_tr", "l_trc",
                               "l_kt", "l_ktc"])
        Sr = Signals(nc, ctx, ["r_ks", "r_w", "r_u", "r_uc", "r_o", "r_oc", "r_st", "r_new", "r_ms", "r_var",
                               "r_rs", "r_on", "r_ot", "r_og", "r_y", "r_yx", "r_nxt"])
        xT = sb("xT", [P, KD, TOK])
        f1T = sb("f1T", [P, TOK])
        g1T = sb("g1T", [P, TOK])
        beta_t = sb("beta_t", [P, NCH, H])
        negA = sb("negA", [P, H])
        dtb = sb("dtb", [P, H])
        cw = sb("cw", [P, 3, H, 4])
        onw = sb("onw", [P, 1])
        load_all(nc, S, [
            (negA[:, :], everywhere(W["L1_attn_A_log"].rearrange("a b h d -> (a b h d)"))),
            (dtb[:, :], W["L1_attn_dt_bias"]),
            (cw[:, 0], rows(W["L1_attn_conv_q_w"])),
            (cw[:, 1], rows(W["L1_attn_conv_k_w"])),
            (cw[:, 2], rows(W["L1_attn_conv_v_w"])),
            (onw[:, :], W["L1_attn_o_norm_w"]),
        ], "d_ld")

        with ExitStack() as pre:
            xTb = pre.enter_context(nc.sbuf_tensor("d_xTb", [P, KD, L], F32))
            C.xn = pre.enter_context(nc.sbuf_tensor("d_xn", [P, TJ, D], F32))
            wfa = pre.enter_context(nc.sbuf_tensor("d_wfa", [P, KD, P], F32))
            wga = pre.enter_context(nc.sbuf_tensor("d_wga", [P, KD, P], F32))
            wb = pre.enter_context(nc.sbuf_tensor("d_wb", [P, KD, H], F32))
            betaT = pre.enter_context(nc.sbuf_tensor("d_betaT", [H, TOK], F32))
            S.fresh()
            load_all(nc, S, [(wfa[:, :, :], rows(W["L1_attn_Wfa"])), (wga[:, :, :], rows(W["L1_attn_Wga"])),
                             (wb[:, :, :], rows(W["L1_attn_Wb"]))], "d_ld")
            with nc.Fori(0, B) as b:
                S.fresh()
                layernorm_T(nc, C, S, b, xTb)
                with nc.Block() as blk:
                    @blk.tensor
                    def _(pe):
                        for n, (w, m) in enumerate(((wfa, P), (wga, P), (wb, H))):
                            for k in range(KD):
                                mm = pe.matmul(ps[0:m, n, :], w[:, k, :], xTb[:, k, :],
                                               start=(k == 0), stop=(k == KD - 1))
                        for j in range(TJ):
                            for k in range(KD):
                                mm = pe.matmul(ps[:, 3, H * j:H * j + H], xTb[:, k, P * j:P * j + P], wb[:, k, :],
                                               start=(k == 0), stop=(k == KD - 1))
                        mm.then_inc(S["ln_tr"], 1)

                    @blk.scalar
                    def _(act):
                        act.wait_ge(S["ln_tr"], KD + 1)
                        act.copy(f1T[:, bass.ds(L * b, L)], ps[:, 0, :])
                        act.copy(g1T[:, bass.ds(L * b, L)], ps[:, 1, :])
                        act.activation(betaT[:, bass.ds(L * b, L)], ps[0:H, 2, :], ACT.Sigmoid)
                        act.activation(beta_t[:, bass.ds(TJ * b, TJ), :],
                                       ps[:, 3, 0:TJ * H].rearrange("p (j h) -> p j h", h=H), ACT.Sigmoid)

                    @blk.vector
                    def _(dve):
                        for k in range(KD):
                            dve.tensor_copy(xT[:, k, bass.ds(L * b, L)], xTb[:, k, :])
            S.fresh()
            with nc.Block() as blk:
                @blk.sync
                def _(sp):
                    sp.dma_start(C.scratch[0:H, :], betaT[:, :]).then_inc(S["d_scr"], 16)
                    sp.wait_ge(S["d_scr"], 16)

                @blk.scalar
                def _(act):
                    act.activation(negA[:, :], negA[:, :], ACT.Exp)
                    act.drain().then_inc(S["ln_var"], 1)

                @blk.vector
                def _(dve):
                    dve.wait_ge(S["ln_var"], 1)
                    dve.tensor_scalar(negA[:, :], negA[:, :], -1.0, None, ALU.mult)

        wqkv = sb("wqkv", [P, 3, KD, P])
        wfg = sb("wfg", [P, 2, P])
        wo = sb("wo", [P, D])
        raw = sb("raw", [P, 3, 3 + L])
        conv = sb("conv", [P, 3, L])
        KQ = sb("KQ", [P, 2, TOK])
        kS = sb("kS", [P, TOK])
        vb = sb("vb", [P, TOK])
        sg = sb("sg", [P, TOK])
        dec = sb("dec", [P, TOK])
        N_ = sb("N", [P, NCH, P])
        T_ = sb("T", [P, NCH, P])
        A_ = sb("A", [P, NCH, P])
        M_ = sb("M", [P, NCH, P])
        Y_ = sb("Y", [P, NCH, P])
        dec2 = sb("dec2", [P, TOK // 2])
        maskf = sb("maskf", [P, 7, 64])
        masku = sb("masku", [P, 7, 64], U32)
        rowm = sb("rowm", [P, 7])
        sumq = sb("sumq", [P, NCH])
        fac = sb("fac", [P, 3, NCH])
        T1f = dec2[:, 0:L]
        Fs = N_[:, :, :].rearrange("p c s -> p (c s)")

        S.fresh()
        load_all(nc, S, [(maskf[:, :, :], W["c_mask"]), (masku[:, :, :], W["c_masku"]), (rowm[:, :], W["c_rowm"])],
                 "d_ld")
        with nc.Fori(0, H) as h:
            Sp.fresh()
            with nc.Block() as blk:
                @blk.sync
                def _(sp):
                    for n, w in enumerate(("Wq", "Wk", "Wv")):
                        sp.dma_start(wqkv[:, n], rows(W["L1_attn_" + w])[:, :, bass.ds(P * h, P)]
                                     ).then_inc(Sp["p_w"], 16)
                    sp.dma_start(wfg[:, 0, :], W["L1_attn_Wfb"][:, bass.ds(P * h, P)]).then_inc(Sp["p_w"], 16)
                    sp.dma_start(wfg[:, 1, :], W["L1_attn_Wgb"][:, bass.ds(P * h, P)]).then_inc(Sp["p_w"], 16)
                    sp.dma_start(wo[:, :], W["L1_attn_Wo"][bass.ds(P * h, P), :]).then_inc(Sp["p_w"], 16)
                    sp.dma_start(M_[:, :, :].rearrange("p c s -> p (c s)"),
                                 C.scratch[bass.ds(h, 1), :].broadcast_to((P, TOK))).then_inc(Sp["p_beta"], 16)
                    sp.wait_ge(Sp["p_beta"], 16)
                    sp.wait_ge(Sp["p_w"], 96)

                @blk.tensor
                def _(pe):
                    pe.wait_ge(Sp["p_w"], 96)
                    for b in range(B):
                        for n in range(3):
                            if b >= 1:
                                pe.wait_ge(Sp["p_raw"], 3 * (b - 1) + n + 1)
                            for k in range(KD):
                                mm = pe.matmul(ps[:, n, :], wqkv[:, n, k, :], xT[:, k, L * b:L * b + L],
                                               start=(k == 0), stop=(k == KD - 1))
                            mm.then_inc(Sp["p_pad"], 1)
                        if b >= 1:
                            pe.wait_ge(Sp["p_th"], b)
                        pe.matmul(ps[:, 3, :], wfg[:, 1, :], g1T[:, L * b:L * b + L],
                                  start=True, stop=True).then_inc(Sp["p_go"], 1)
                    for b in range(B):
                        pe.matmul(ps[:, 4 + b, :], wfg[:, 0, :], f1T[:, L * b:L * b + L],
                                  start=True, stop=True).then_inc(Sp["p_gate"], 1)
                    for b in range(B):
                        pe.wait_ge(Sp["p_sq"], b + 1)
                        pe.matmul(ps[:, b, :], C.ones[:, :], Fs[:, L * b:L * b + L],
                                  start=True, stop=True).then_inc(Sp["p_ss"], 1)

                @blk.scalar
                def _(act):
                    for b in range(B):
                        for n in range(3):
                            act.wait_ge(Sp["p_pad"], 3 * b + n + 1)
                            if b >= 1:
                                act.wait_ge(Sp["p_conv"], 3 * (b - 1) + n + 1)
                            act.copy(raw[:, n, 3:3 + L], ps[:, n, :]).then_inc(Sp["p_raw"], 1)
                        act.wait_ge(Sp["p_go"], b + 1)
                        act.activation(sg[:, L * b:L * b + L], ps[:, 3, :], ACT.Tanh, scale=0.5
                                       ).then_inc(Sp["p_th"], 1)
                        for n, dst in enumerate((KQ[:, 1, L * b:L * b + L], kS[:, L * b:L * b + L],
                                                 vb[:, L * b:L * b + L])):
                            act.wait_ge(Sp["p_conv"], 3 * b + n + 1)
                            act.activation(dst, conv[:, n, :], ACT.Silu).then_inc(Sp["p_silu"], 1)
                    act.drain()
                    for b in range(B):
                        act.activation(Fs[:, L * b:L * b + L], kS[:, L * b:L * b + L], ACT.Square
                                       ).then_inc(Sp["p_sq"], 1)
                    for b in range(B):
                        act.activation(T_[:, TJ * b:TJ * b + TJ, :].rearrange("p c s -> p (c s)"),
                                       KQ[:, 1, L * b:L * b + L], ACT.Square).then_inc(Sp["p_q2"], 1)
                    def seq(t, b):
                        return t[:, L * b:L * b + L]
                    rk = Y_[:, :, :].rearrange("p c s -> p (c s)")
                    for b in range(B):
                        act.wait_ge(Sp["p_gate"], b + 1)
                        act.activation(seq(dec, b), ps[:, 4 + b, :], ACT.Abs, bias=dtb[:, bass.ds(h, 1)]
                                       ).then_inc(Sp["p_abs"], 1)
                    act.drain()
                    act.activation(dec[:, :], dec[:, :], ACT.Exp, scale=-1.0)
                    act.drain()
                    for b in range(B):
                        act.activation(seq(dec, b), seq(dec, b), ACT.Ln, bias=1.0).then_inc(Sp["p_sp"], 1)
                    for b in range(B):
                        act.wait_ge(Sp["p_ss"], b + 1)
                        act.activation(seq(rk, b), ps[:, b, :], ACT.Ln, bias=C.eps6[:, 0:1])
                    act.drain()
                    for b in range(B):
                        act.activation(seq(rk, b), seq(rk, b), ACT.Exp, scale=-0.5).then_inc(Sp["p_nk"], 1)
                        act.wait_ge(Sp["p_sum"], b + 1)
                        act.activation(seq(dec, b), seq(dec, b), ACT.Exp, scale=negA[:, bass.ds(h, 1)]
                                       ).then_inc(Sp["p_dec"], 1)

                @blk.vector
                def _(dve):
                    dve.memset(raw[:, :, 0:3], 0.0)
                    dve.drain()
                    for b in range(B):
                        for n in range(3):
                            dve.wait_ge(Sp["p_raw"], 3 * b + n + 1)
                            if b >= 1:
                                dve.wait_ge(Sp["p_silu"], 3 * (b - 1) + n + 1)
                            dve.tensor_scalar(conv[:, n, :], raw[:, n, 3:3 + L], cw[:, n, bass.ds(h, 1), 3],
                                              None, ALU.mult)
                            for t in range(3):
                                dve.drain()
                                mm = dve.scalar_tensor_tensor(conv[:, n, :], raw[:, n, t:t + L],
                                                              cw[:, n, bass.ds(h, 1), t], conv[:, n, :],
                                                              ALU.mult, ALU.add)
                            dve.drain().then_inc(Sp["p_conv"], 1)
                    dve.wait_ge(Sp["p_silu"], 3 * B)
                    for b in range(B):
                        cv = conv[:, b, :] if b < 3 else T1f
                        dve.wait_ge(Sp["p_abs"], b + 1)
                        dve.tensor_scalar(cv, ps[:, 4 + b, :], dtb[:, bass.ds(h, 1)], 0.0, ALU.add, ALU.max)
                    dve.drain()
                    for b in range(B):
                        cv = conv[:, b, :] if b < 3 else T1f
                        dve.wait_ge(Sp["p_sp"], b + 1)
                        dve.tensor_tensor(dec[:, L * b:L * b + L], cv, dec[:, L * b:L * b + L], ALU.add
                                          ).then_inc(Sp["p_sum"], 1)

                @blk.gpsimd
                def _(pool):
                    pool.wait_ge(Sp["p_th"], B)
                    pool.tensor_scalar(sg[:, :], sg[:, :], 0.5, 0.5, ALU.mult, ALU.add)
                    Mf = M_[:, :, :].rearrange("p c s -> p (c s)")
                    Yf = Y_[:, :, :].rearrange("p c s -> p (c s)")
                    for b in range(B):
                        sl = slice(L * b, L * b + L)
                        pool.wait_ge(Sp["p_beta"], 16)
                        pool.wait_ge(Sp["p_nk"], b + 1)
                        pool.wait_ge(Sp["p_sq"], B)
                        pool.tensor_tensor(kS[:, sl], kS[:, sl], Yf[:, sl], ALU.mult)
                        pool.drain()
                        pool.wait_ge(Sp["p_dec"], b + 1)
                        pool.tensor_tensor(Yf[:, sl], Mf[:, sl], dec[:, sl], ALU.mult)
                        pool.drain()
                        pool.tensor_tensor(KQ[:, 0, sl], kS[:, sl], Yf[:, sl], ALU.mult)

            with nc.Block() as blk:
                @blk.tensor
                def _(pe):
                    for c in range(NCH):
                        mm = pe.matmul(ps[:, 0, 2 * c:2 * c + 2], T_[:, c, :], C.ones[:, 0:2], start=True, stop=True)
                    mm.then_inc(Sp["p_dg"], 1)
                    for c in range(NCH):
                        mm = pe.transpose(ps[:, 1 + c // 4, P * (c % 4):P * (c % 4) + P], vb[:, P * c:P * c + P],
                                          ident[:, :])
                    mm.then_inc(Sp["p_vt"], 1)
                    for b in range(B):
                        if b >= 3:
                            pe.wait_ge(Sp["p_dgm"], b - 2)
                        for c in range(TJ * b, TJ * b + TJ):
                            mm = pe.matmul(ps[:, 5 + b % 3, P * (c % 4):P * (c % 4) + P], kS[:, P * c:P * c + P],
                                           KQ[:, 1, P * c:P * c + P], start=True, stop=True)
                        mm.then_inc(Sp["p_dg"], 1)

                @blk.scalar
                def _(act):
                    act.wait_ge(Sp["p_dg"], 1)
                    act.copy(sumq[:, :], ps[:, 0, 0:2 * NCH].rearrange("p (c a) -> p c a", a=2)[:, :, 0])
                    act.wait_ge(Sp["p_vt"], 1)
                    for c in range(NCH):
                        act.activation(vb[:, P * c:P * c + P], ps[:, 1 + c // 4, P * (c % 4):P * (c % 4) + P],
                                       ACT.Copy, scale=beta_t[:, c, bass.ds(h, 1)])

                @blk.vector
                def _(dve):
                    for b in range(B):
                        dve.wait_ge(Sp["p_dg"], b + 2)
                        dve.tensor_tensor(A_[:, TJ * b:TJ * b + TJ, :],
                                          ps[:, 5 + b % 3, :].rearrange("p (c s) -> p c s", s=P),
                                          ident[:, :].unsqueeze(1).broadcast_to((P, TJ, P)), ALU.mult
                                          ).then_inc(Sp["p_dgm"], 1)
                    dve.wait_ge(Sp["p_dg"], 1)
                    dve.memset(M_[:, :, :], 0.0)
                    dve.memset(Y_[:, :, :], 0.0)

                @blk.gpsimd
                def _(pool):
                    pool.wait_ge(Sp["p_dg"], B + 1)
                    for b in range(B):
                        sl = slice(L * b, L * b + L)
                        pool.tensor_tensor(KQ[:, 1, sl], KQ[:, 1, sl], dec[:, sl], ALU.mult)

            Sl.fresh()
            with nc.Block() as blk:
                def second(ap, w):
                    return ap.rearrange("p c (n a r) -> p c n a r", a=2, r=w)[:, :, :, 1, :]

                def packed(ap, w):
                    return ap.rearrange("p c (n r) -> p c n r", r=w)

                def blocks(w):
                    return range(0, P, 2 * w)

                def of(t, b):
                    return t[:, TJ * b:TJ * b + TJ, :].rearrange("p c s -> p (c s)")

                @blk.tensor
                def _(pe):
                    def strips(w):
                        g = P // 2 if 4 <= w <= 16 else P
                        return [slice(n, n + g) for n in range(0, P, g)]

                    def pairs(l, w):
                        for b in range(B):
                            if l >= 1:
                                pe.wait_ge(Sl["l_scaled"], B * (l - 1) + b + 1)
                                pe.wait_ge(Sl["l_masked"], B * (l - 1) + b + 1)
                            if l >= 3:
                                pe.wait_ge(Sl["l_trc"], B * (l - 3) + b + 1)
                            for c in range(TJ):
                                cc = P * (TJ * b + c)
                                bank = ps[:, b, P * c:P * c + P].rearrange("p (q s) -> p q s", q=2)
                                for r in strips(w):
                                    t2 = KQ[:, :, cc + r.start:cc + r.stop].rearrange(
                                        "p q (n a r) -> p q n a r", a=2, r=w)[:, :, :, 1, :]
                                    mm = pe.matmul(bank[r, :, r.start // 2:r.stop // 2],
                                                   kS[:, cc + r.start:cc + r.stop], t2, start=True, stop=True)
                            mm.then_inc(Sl["l_pairs"], 1)

                    pairs(0, LEVELS[0])
                    for b in range(B):
                        pe.wait_ge(Sl["l_masked"], b + 1)
                        for c in range(TJ):
                            mm = pe.transpose(ps[:, 4 + b, P * c:P * c + P], M_[:, TJ * b + c, :], ident[:, :])
                        mm.then_inc(Sl["l_y"], 1)
                    pairs(1, LEVELS[1])
                    for l in range(1, LAST + 1):
                        w = LEVELS[l]
                        for b in range(B):
                            pe.wait_ge(Sl["l_masked"], B * l + b + 1)
                            pe.wait_ge(Sl["l_new"], B * (l - 1) + b + 1)
                            for c in range(TJ):
                                cc, a = TJ * b + c, P * c
                                if w < 32:
                                    for r in strips(w):
                                        mm = pe.matmul(ps[r, 4 + b, a + r.start:a + r.stop], M_[r, cc, r],
                                                       T_[r, cc, r], start=True, stop=True)
                                else:
                                    for n in blocks(w):
                                        one, two = slice(n, n + w), slice(n + w, n + 2 * w)
                                        mm = pe.matmul(ps[two, 4 + b, a + n:a + n + w], M_[one, cc, two],
                                                       T_[one, cc, one], start=True, stop=True)
                            mm.then_inc(Sl["l_y"], 1)
                        if l >= 2:
                            for b in range(B):
                                for c in range(TJ):
                                    mm = pe.transpose(ps[:, b, P * c:P * c + P], T_[:, TJ * b + c, :], ident[:, :])
                                mm.then_inc(Sl["l_tr"], 1)
                        if l < LAST:
                            pairs(l + 1, LEVELS[l + 1])
                        else:
                            for b in range(B):
                                pe.wait_ge(Sl["l_scaled"], B * l + b + 1)
                                pe.wait_ge(Sl["l_trc"], B * (l - 2) + b + 1)
                                for c in range(TJ):
                                    cc = TJ * b + c
                                    mm = pe.transpose(ps[:, b, P * c:P * c + P], kS[:, P * cc:P * cc + P],
                                                      ident[:, :])
                                mm.then_inc(Sl["l_kt"], 1)
                        for b in range(B):
                            pe.wait_ge(Sl["l_yc"], B * (l - 1) + b + 1)
                            if l >= 2:
                                pe.wait_ge(Sl["l_trc"], B * (l - 2) + b + 1)
                            for c in range(TJ):
                                cc, a = TJ * b + c, P * c
                                if w < 32:
                                    for r in strips(w):
                                        mm = pe.matmul(ps[r, 4 + b, a + r.start:a + r.stop], N_[r, cc, r],
                                                       Y_[r, cc, r], start=True, stop=True)
                                elif l < LAST:
                                    for n in blocks(w):
                                        one, two = slice(n, n + w), slice(n + w, n + 2 * w)
                                        mm = pe.matmul(ps[two, 4 + b, a + n:a + n + w], N_[two, cc, two],
                                                       Y_[two, cc, one], start=True, stop=True)
                                else:
                                    mm = pe.matmul(ps[0:w, 4 + b, a + w:a + 2 * w], Y_[w:, cc, 0:w],
                                                   N_[w:, cc, w:], start=True, stop=True)
                            mm.then_inc(Sl["l_upd"], 1)

                @blk.vector
                def _(dve):
                    def mask(l, w):
                        for b in range(B):
                            cs = slice(TJ * b, TJ * b + TJ)
                            bank = ps[:, b, :].rearrange("p (c q s) -> p c q s", c=TJ, q=2)
                            dve.wait_ge(Sl["l_pairs"], B * l + b + 1)
                            if l >= 1:
                                dve.wait_ge(Sl["l_y"], B * (l - 1) + b + 1)
                            dve.tensor_tensor(second(M_[:, cs, :], w), packed(bank[:, :, 0, :], w),
                                              packed(maskf[:, l, :].unsqueeze(1).broadcast_to((P, TJ, 64)), w),
                                              ALU.mult)
                            dve.copy_predicated(second(A_[:, cs, :], w),
                                                packed(masku[:, l, :].unsqueeze(1).broadcast_to((P, TJ, 64)), w),
                                                packed(bank[:, :, 1, :], w)).then_inc(Sl["l_masked"], 1)

                    mask(0, LEVELS[0])
                    dve.drain()
                    eye = ident[:, :].unsqueeze(1).broadcast_to((P, TJ, P))
                    for b in range(B):
                        cs = slice(TJ * b, TJ * b + TJ)
                        dve.tensor_tensor(N_[:, cs, :], eye, M_[:, cs, :], ALU.subtract)
                        dve.wait_ge(Sl["l_y"], b + 1)
                        dve.tensor_tensor(T_[:, cs, :], eye, ps[:, 4 + b, :].rearrange("p (c s) -> p c s", c=TJ),
                                          ALU.subtract).then_inc(Sl["l_new"], 1)
                    dve.drain()
                    mask(1, LEVELS[1])
                    for l in range(1, LAST + 1):
                        w = LEVELS[l]
                        if l < LAST:
                            dve.drain()
                            mask(l + 1, LEVELS[l + 1])
                        for b in range(B):
                            cs = slice(TJ * b, TJ * b + TJ)
                            bank = ps[:, 4 + b, :].rearrange("p (c s) -> p c s", c=TJ)
                            dve.wait_ge(Sl["l_upd"], B * (l - 1) + b + 1)
                            if w < 32:
                                Tf = halves(of(T_, b), w)[0]
                                op = dve.tensor_tensor(Tf, Tf, halves(ps[:, 4 + b, :], w)[0], ALU.subtract)
                            elif l < LAST:
                                for n in blocks(w):
                                    two = slice(n + w, n + 2 * w)
                                    op = dve.tensor_scalar(T_[two, cs, n:n + w], bank[two, :, n:n + w], -1.0, None,
                                                           ALU.mult)
                            else:
                                op = dve.tensor_scalar(N_[0:w, cs, w:], bank[0:w, :, w:], -1.0, None, ALU.mult)
                            op.then_inc(Sl["l_new"], 1)
                        dve.drain()

                @blk.scalar
                def _(act):
                    for l in range(1, LAST + 1):
                        w = LEVELS[l]
                        for b in range(B):
                            cs = slice(TJ * b, TJ * b + TJ)
                            bank = ps[:, 4 + b, :].rearrange("p (c s) -> p c s", c=TJ)
                            act.wait_ge(Sl["l_y"], B * l + b + 1)
                            if w < 32:
                                op = act.activation(halves(of(Y_, b), w)[0], halves(ps[:, 4 + b, :], w)[0], ACT.Copy,
                                                    scale=rowm[:, l:l + 1])
                            else:
                                for n in blocks(w):
                                    two = slice(n + w, n + 2 * w)
                                    op = act.copy(Y_[two, cs, n:n + w], bank[two, :, n:n + w])
                            op.then_inc(Sl["l_yc"], 1)
                        if l >= 2:
                            h = LEVELS[l - 1]
                            for b in range(B):
                                act.wait_ge(Sl["l_tr"], B * (l - 2) + b + 1)
                                act.copy(halves(of(N_, b), h)[1], halves(ps[:, b, :], h)[1]
                                         ).then_inc(Sl["l_trc"], 1)
                    for b in range(B):
                        act.wait_ge(Sl["l_kt"], b + 1)
                        act.copy(M_[:, TJ * b:TJ * b + TJ, :].rearrange("p c s -> p (c s)"), ps[:, b, :])

                @blk.gpsimd
                def _(pool):
                    src = dec
                    for l, w in enumerate(LEVELS):
                        dst = dec2 if l % 2 == 0 else dec
                        nblk = L // (2 * w)
                        for b in range(B):
                            sl = slice(L * b, L * b + L)
                            n0 = b * 2 * nblk
                            pr = src[:, n0:n0 + 2 * nblk].rearrange("p (n a) -> p n a", a=2)
                            D1, D2 = pr[:, :, 0:1], pr[:, :, 1:2]
                            kq2 = KQ[:, :, sl].rearrange("p q (n a r) -> p q n a r", a=2, r=w)[:, :, :, 1, :]
                            kf = halves(kS[:, sl], w)[0]
                            pool.wait_ge(Sl["l_pairs"], B * l + b + 1)
                            for q in range(2):
                                pool.tensor_tensor(kq2[:, q], kq2[:, q], D1.broadcast_to((P, nblk, w)), ALU.mult)
                            pool.tensor_tensor(kf, kf, D2.broadcast_to((P, nblk, w)), ALU.mult)
                            pool.tensor_tensor(dst[:, b * nblk:b * nblk + nblk], pr[:, :, 0], pr[:, :, 1], ALU.mult)
                            pool.drain().then_inc(Sl["l_scaled"], 1)
                        src = dst
            Dc = dec2 if len(LEVELS) % 2 else dec

            Sr.fresh()
            St = dec[:, 2 * L:2 * L + B * P] if Dc is dec2 else dec2[:, 0:B * P]
            with nc.Block() as blk:
                def W_(b):
                    return conv[:, 0, P * b:P * b + P]

                def U_(b):
                    return conv[:, 1, P * b:P * b + P]

                @blk.tensor
                def _(pe):
                    for c in range(TJ):
                        if c >= 1:
                            for b in range(B):
                                cc = TJ * b + c
                                pe.wait_ge(Sr["r_new"], B * (c - 1) + b + 1)
                                pe.matmul(ps[:, b, 0:P], KQ[:, 0, P * cc:P * cc + P],
                                          St[:, P * b:P * b + P], start=True, stop=True).then_inc(Sr["r_ks"], 1)
                        for b in range(B):
                            cc = TJ * b + c
                            pe.wait_ge(Sr["r_w"], B * c + b + 1)
                            pe.matmul(ps[:, b, P:2 * P], N_[:, cc, :], W_(b), start=True, stop=True
                                      ).then_inc(Sr["r_u"], 1)
                        for b in range(B):
                            cc = TJ * b + c
                            o = ps[:, 4 + b, 0:P]
                            if c >= 1:
                                pe.wait_ge(Sr["r_oc"], B * (c - 1) + b + 1)
                            if c >= 1:
                                pe.matmul(o, KQ[:, 1, P * cc:P * cc + P], St[:, P * b:P * b + P],
                                          start=True, stop=False)
                            pe.wait_ge(Sr["r_uc"], B * c + b + 1)
                            pe.matmul(o, A_[:, cc, :], U_(b), start=(c == 0), stop=True).then_inc(Sr["r_o"], 1)
                            if c < TJ - 1:
                                pe.matmul(ps[:, b, 2 * P:3 * P], M_[:, cc, :], U_(b), start=True, stop=True
                                          ).then_inc(Sr["r_st"], 1)
                    for b in range(B):
                        pe.wait_ge(Sr["r_on"], b + 1)
                        for c in range(TJ):
                            mm = pe.transpose(ps[:, b % 2, P * c:P * c + P], Y_[:, TJ * b + c, :], ident[:, :])
                        mm.then_inc(Sr["r_ot"], 1)
                        pe.wait_ge(Sr["r_og"], b + 1)
                        for c in range(TJ):
                            if b >= 1:
                                pe.wait_ge(Sr["r_yx"], TJ * (b - 1) + c + 1)
                            pe.matmul(ps[:, 4 + c, :], kS[:, P * (TJ * b + c):P * (TJ * b + c) + P], wo[:, :],
                                      start=True, stop=True).then_inc(Sr["r_y"], 1)

                @blk.vector
                def _(dve):
                    for c in range(TJ):
                        for b in range(B):
                            cc = TJ * b + c
                            if c >= 1:
                                dve.wait_ge(Sr["r_u"], B * (c - 1) + b + 1)
                                dve.wait_ge(Sr["r_ks"], B * (c - 1) + b + 1)
                                dve.tensor_tensor(W_(b), vb[:, P * cc:P * cc + P], ps[:, b, 0:P],
                                                  ALU.subtract).then_inc(Sr["r_w"], 1)
                            else:
                                dve.tensor_copy(W_(b), vb[:, P * cc:P * cc + P]).then_inc(Sr["r_w"], 1)
                        if c < TJ - 1:
                            for b in range(B):
                                cc = TJ * b + c
                                dve.wait_ge(Sr["r_st"], B * c + b + 1)
                                s = St[:, P * b:P * b + P]
                                if c >= 1:
                                    dve.scalar_tensor_tensor(s, s, Dc[:, cc:cc + 1], ps[:, b, 2 * P:3 * P],
                                                             ALU.mult, ALU.add).then_inc(Sr["r_new"], 1)
                                else:
                                    dve.tensor_copy(s, ps[:, b, 2 * P:3 * P]).then_inc(Sr["r_new"], 1)
                    dve.wait_ge(Sr["r_ms"], 1)
                    dve.tensor_tensor(fac[:, 1, :], fac[:, 1, :], fac[:, 0, :], ALU.mult)
                    dve.drain()
                    dve.tensor_tensor(fac[:, 1, :], fac[:, 1, :], fac[:, 0, :], ALU.mult)
                    dve.drain().then_inc(Sr["r_var"], 1)
                    dve.wait_ge(Sr["r_rs"], 1)
                    dve.tensor_tensor(fac[:, 1, :], fac[:, 1, :], fac[:, 0, :], ALU.mult)
                    dve.drain()
                    for b in range(B):
                        o = Y_[:, TJ * b:TJ * b + TJ, :]
                        dve.tensor_tensor(o, o, fac[:, 1, TJ * b:TJ * b + TJ].unsqueeze(2).broadcast_to((P, TJ, P)),
                                          ALU.mult).then_inc(Sr["r_on"], 1)
                    for b in range(B):
                        dve.wait_ge(Sr["r_ot"], b + 1)
                        dve.scalar_tensor_tensor(kS[:, L * b:L * b + L], ps[:, b % 2, :], onw[:, 0:1],
                                                 sg[:, L * b:L * b + L], ALU.mult, ALU.mult
                                                 ).then_inc(Sr["r_og"], 1)
                        for c in range(TJ):
                            dve.wait_ge(Sr["r_y"], TJ * b + c + 1)
                            dve.tensor_tensor(x[:, TJ * b + c, :], x[:, TJ * b + c, :], ps[:, 4 + c, :],
                                              ALU.add).then_inc(Sr["r_yx"], 1)

                @blk.scalar
                def _(act):
                    for c in range(TJ):
                        for b in range(B):
                            act.wait_ge(Sr["r_u"], B * c + b + 1)
                            if c >= 1:
                                act.wait_ge(Sr["r_o"], B * (c - 1) + b + 1)
                                act.wait_ge(Sr["r_st"], B * (c - 1) + b + 1)
                            act.copy(U_(b), ps[:, b, P:2 * P]).then_inc(Sr["r_uc"], 1)
                        for b in range(B):
                            act.wait_ge(Sr["r_o"], B * c + b + 1)
                            act.copy(Y_[:, TJ * b + c, :], ps[:, 4 + b, 0:P]
                                     ).then_inc(Sr["r_oc"], 1)
                    act.drain()
                    for cc in range(NCH):
                        act.activation(A_[:, cc, :], Y_[:, cc, :], ACT.Square, accum_out=fac[:, 1, cc:cc + 1])
                    act.activation(fac[:, 2, :], sumq[:, :], ACT.Ln, bias=C.eps6[:, 0:1])
                    act.drain()
                    act.activation(fac[:, 0, :], fac[:, 2, :], ACT.Exp, scale=-0.5, bias=C.lnsd[:, 0:1])
                    act.drain().then_inc(Sr["r_ms"], 1)
                    act.wait_ge(Sr["r_var"], 1)
                    act.activation(fac[:, 2, :], fac[:, 1, :], ACT.Ln, scale=1.0 / P, bias=C.eps6[:, 0:1])
                    act.drain()
                    act.activation(fac[:, 1, :], fac[:, 2, :], ACT.Exp, scale=-0.5)
                    act.drain().then_inc(Sr["r_rs"], 1)


def cross_attention(nc, C, W):
    H, HD, DCA, CK, NM = 16, 32, 16, 2, L - 16
    G = TJ * H
    x, ps, ident = C.x, C.ps, C.ident
    with ExitStack() as ctx:
        def sb(name, shape, dt=F32):
            return ctx.enter_context(nc.sbuf_tensor("a_" + name, shape, dt))

        S = Signals(nc, ctx, ["a_ld"])
        Sb = Signals(nc, ctx, LN_SIGNALS + ["a_ctx", "a_q", "a_qb", "a_k", "a_kb", "a_d", "a_db", "a_sq", "a_rs",
                                            "a_n", "a_tr", "a_trc"])
        Sh = Signals(nc, ctx, ["h_s", "h_max", "h_exp", "h_pt", "h_ptc", "h_o", "h_sum", "h_on", "h_ot", "h_otc",
                               "h_y", "h_free"])
        C.xn = sb("xn", [P, TJ, D])
        xT = sb("xT", [P, KD, L])
        wq = sb("wq", [P, KD, D])
        wkv = sb("wkv", [P, CK, 2 * D])
        wdc = sb("wdc", [P, CK, 2 * D])
        wo = sb("wo", [P, KD, D])
        bq = sb("bq", [P, D])
        bkv = sb("bkv", [P, 2 * D])
        bdc = sb("bdc", [P, 2 * D])
        bo = sb("bo", [P, D])
        nw = sb("nw", [P, 6])
        isd = sb("isd", [P, 2])
        cT = sb("cT", [P, CK, L])
        q = sb("q", [P, TJ, D])
        k = sb("k", [P, TJ, D])
        v = sb("v", [P, TJ, D])
        v2 = sb("v2", [P, H, 2 * HD])
        kv3 = sb("kv3", [P, 2 * D])
        sq = sb("sq", [P, TJ, D])
        mom = sb("mom", [P, 2, 2, G])
        qT = sb("qT", [P, KD, L])
        kT = sb("kT", [P, KD, L])
        nm = sb("nm", [P, 2, H, 2])
        sm = sb("sm", [P, 2, H])
        pr = sb("pr", [P, 2, L])
        pT = sb("pT", [P, 2, L])
        o = sb("o", [P, TJ, D])
        S.fresh()
        load_all(nc, S, [
            (wq[:, :, :], rows(W["L1_xattn_Wq"])), (wo[:, :, :], rows(W["L1_xattn_Wo"])),
            (wkv[:, :, 0:D], rows(W["L1_xattn_Wk"])), (wkv[:, :, D:2 * D], rows(W["L1_xattn_Wv"])),
            (wdc[:, :, :], rows(W["L1_xattn_Wkv_dca"])), (bq[:, :], everywhere(W["L1_xattn_bq"])),
            (bkv[:, 0:D], everywhere(W["L1_xattn_bk"])), (bkv[:, D:2 * D], everywhere(W["L1_xattn_bv"])),
            (bdc[:, :], everywhere(W["L1_xattn_bkv_dca"])), (bo[:, :], everywhere(W["L1_xattn_bo"])),
            (isd[:, :], W["c_isd"])]
            + [(nw[HD * i:HD * i + HD, n:n + 1], W["L1_xattn_" + name])
               for n, name in enumerate(("qn_w", "qn_b", "kn_w", "kn_b", "kn_dca_w", "kn_dca_b"))
               for i in range(4)], "a_ld")
        with nc.Fori(0, B) as b:
            Sb.fresh()
            layernorm_T(nc, C, Sb, b, xT)
            with nc.Block() as blk:
                def heads(ap):
                    return ap.rearrange("p j (h d) -> p (j h) d", d=HD)

                @blk.sync
                def _(sp):
                    sp.dma_start(cT[:, :, :], W["ctx_1024"].rearrange("b (k p) n -> b p k n", p=P)[
                        bass.ds(b, 1)].rearrange("a p k n -> (a p) k n")).then_inc(Sb["a_ctx"], 16)

                @blk.tensor
                def _(pe):
                    for j in range(TJ):
                        for kk in range(KD):
                            mm = pe.matmul(ps[:, j, :], xT[:, kk, P * j:P * j + P], wq[:, kk, :],
                                           start=(kk == 0), stop=(kk == KD - 1))
                        mm.then_inc(Sb["a_q"], 1)
                    pe.wait_ge(Sb["a_ctx"], 16)
                    for j in range(TJ):
                        if j >= 2:
                            pe.wait_ge(Sb["a_kb"], j - 1)
                        for n in range(2):
                            for kk in range(CK):
                                mm = pe.matmul(ps[:, 4 + 2 * (j % 2) + n, :], cT[:, kk, P * j:P * j + P],
                                               wkv[:, kk, D * n:D * n + D], start=(kk == 0), stop=(kk == CK - 1))
                        mm.then_inc(Sb["a_k"], 1)
                    pe.wait_ge(Sb["a_qb"], 2)
                    for n in range(2):
                        for kk in range(CK):
                            mm = pe.matmul(ps[:, n, :], cT[:, kk, P * (TJ - 1):L], wdc[:, kk, D * n:D * n + D],
                                           start=(kk == 0), stop=(kk == CK - 1))
                    mm.then_inc(Sb["a_d"], 1)
                    for n, src in enumerate((q, k)):
                        pe.wait_ge(Sb["a_n"], n + 1)
                        for kk in range(KD):
                            if n == 1:
                                pe.wait_ge(Sb["a_trc"], kk + 1)
                            for j in range(TJ):
                                mm = pe.transpose(ps[:, kk, P * j:P * j + P], src[:, j, P * kk:P * kk + P], ident[:, :])
                            mm.then_inc(Sb["a_tr"], 1)

                @blk.vector
                def _(dve):
                    for j in range(TJ):
                        dve.wait_ge(Sb["a_q"], j + 1)
                        dve.tensor_tensor(q[:, j, :], ps[:, j, :], bq[:, :], ALU.add).then_inc(Sb["a_qb"], 1)
                    bh = bkv[:, :].rearrange("p (h e) -> p h e", e=2 * HD)
                    for j in range(TJ):
                        dve.wait_ge(Sb["a_k"], j + 1)
                        last = j == TJ - 1
                        kvp = ps[:, 4 + 2 * (j % 2):6 + 2 * (j % 2), :].rearrange("p n (h e) -> p (n h) e", e=2 * HD)
                        dve.tensor_tensor(k[:, j, :].rearrange("p (h d) -> p h d", d=HD), kvp[:, :, 0:HD],
                                          bh[:, :, 0:HD], ALU.add)
                        dst = v2[:, :, 0:HD] if last else v[:, j, :].rearrange("p (h d) -> p h d", d=HD)
                        dve.tensor_tensor(dst, kvp[:, :, HD:], bh[:, :, HD:], ALU.add).then_inc(Sb["a_kb"], 1)
                    dve.wait_ge(Sb["a_d"], 1)
                    for n in range(2):
                        dve.tensor_tensor(kv3[:, D * n:D * n + D], ps[:, n, :], bdc[:, D * n:D * n + D], ALU.add)
                    dve.drain()
                    dve.tensor_scalar(kv3[:, :], kv3[:, :], isd[:, 1:2], None, ALU.mult)
                    dve.tensor_scalar(v2[:, :, 0:HD], v2[:, :, 0:HD], isd[:, 0:1], None, ALU.mult)
                    dve.drain()
                    dve.scalar_tensor_tensor(k[:, TJ - 1, :], k[:, TJ - 1, :], isd[:, 0:1], kv3[:, 0:D],
                                             ALU.mult, ALU.add)
                    dve.tensor_copy(v2[:, :, HD:], kv3[:, D:2 * D].rearrange("p (h d) -> p h d", d=HD))
                    for n, t in enumerate((q, k)):
                        tv = heads(t[:, :, :])
                        m = lambda i: mom[:, n, i, :].unsqueeze(2).broadcast_to((P, G, HD))
                        dve.drain()
                        dve.tensor_reduce(mom[:, n, 0, :], tv, AX_X, ALU.add)
                        dve.drain()
                        dve.tensor_scalar(mom[:, n, 0, :], mom[:, n, 0, :], 1.0 / HD, None, ALU.mult)
                        dve.drain()
                        dve.tensor_tensor(tv, tv, m(0), ALU.subtract)
                        dve.drain()
                        dve.tensor_tensor(heads(sq[:, :, :]), tv, tv, ALU.mult)
                        dve.drain()
                        dve.tensor_reduce(mom[:, n, 1, :], heads(sq[:, :, :]), AX_X, ALU.add)
                        dve.drain().then_inc(Sb["a_sq"], 1)
                        dve.wait_ge(Sb["a_rs"], n + 1)
                        dve.tensor_tensor(tv, tv, m(1), ALU.mult)
                        dve.drain().then_inc(Sb["a_n"], 1)

                @blk.scalar
                def _(act):
                    for n in range(2):
                        act.wait_ge(Sb["a_sq"], n + 1)
                        act.activation(mom[:, n, 1, :], mom[:, n, 1, :], ACT.Ln, scale=1.0 / HD, bias=C.eps6[:, 0:1])
                        act.drain()
                        act.activation(mom[:, n, 1, :], mom[:, n, 1, :], ACT.Exp, scale=-0.5)
                        act.drain().then_inc(Sb["a_rs"], 1)
                        for kk in range(KD):
                            act.wait_ge(Sb["a_tr"], KD * n + kk + 1)
                            if n == 0:
                                act.activation(qT[:, kk, :], ps[:, kk, :], ACT.Identity, scale=nw[:, 0:1],
                                               bias=nw[:, 1:2]).then_inc(Sb["a_trc"], 1)
                            else:
                                act.activation(kT[:, kk, 0:NM], ps[:, kk, 0:NM], ACT.Identity, scale=nw[:, 2:3],
                                               bias=nw[:, 3:4])
                                act.activation(kT[:, kk, NM:L], ps[:, kk, NM:L], ACT.Identity, scale=nw[:, 4:5],
                                               bias=nw[:, 5:6])
            for j in range(TJ):
                Sh.fresh()
                with nc.Block() as blk:
                    @blk.tensor
                    def _(pe):
                        def scores(h):
                            r = slice(HD * (h % 4), HD * (h % 4) + HD)
                            if h >= 2:
                                pe.wait_ge(Sh["h_exp"], h - 1)
                            pe.matmul(ps[:, h % 2, :], qT[r, h // 4, P * j:P * j + P], kT[r, h // 4, :],
                                      start=True, stop=True).then_inc(Sh["h_s"], 1)

                        def turn(h):
                            pe.wait_ge(Sh["h_exp"], h + 1)
                            if h >= 2:
                                pe.wait_ge(Sh["h_ptc"], h - 1)
                            for t in range(TJ):
                                mm = pe.transpose(ps[:, 2 + h % 2, P * t:P * t + P], pr[:, h % 2, P * t:P * t + P],
                                                  ident[:, :])
                            mm.then_inc(Sh["h_pt"], 1)

                        def mix(h):
                            pe.wait_ge(Sh["h_ptc"], h + 1)
                            bank = ps[:, 4 + h // 8, 64 * (h % 8):64 * (h % 8) + 64]
                            pe.matmul(bank, pT[:, h % 2, P * (TJ - 1):L], v2[:, h, :], start=True, stop=False,
                                      skip_group_check=True)
                            for t in range(TJ - 1):
                                mm = pe.matmul(bank[:, 0:HD], pT[:, h % 2, P * t:P * t + P],
                                               v[:, t, HD * h:HD * h + HD], start=False, stop=(t == TJ - 2),
                                               skip_group_check=True)
                            mm.then_inc(Sh["h_o"], 1)

                        scores(0)
                        for h in range(H):
                            if h + 1 < H:
                                scores(h + 1)
                            turn(h)
                            if h >= 1:
                                mix(h - 1)
                        mix(H - 1)
                        pe.wait_ge(Sh["h_on"], 1)
                        for kk in range(KD):
                            mm = pe.transpose(ps[:, 6, P * kk:P * kk + P], o[:, 0, P * kk:P * kk + P], ident[:, :])
                        mm.then_inc(Sh["h_ot"], 1)
                        pe.wait_ge(Sh["h_otc"], 1)
                        for kk in range(KD):
                            mm = pe.matmul(ps[:, 7, :], o[:, 1, P * kk:P * kk + P], wo[:, kk, :],
                                           start=(kk == 0), stop=(kk == KD - 1))
                        mm.then_inc(Sh["h_y"], 1)

                    @blk.vector
                    def _(dve):
                        for h in range(H + 1):
                            if h < H:
                                dve.wait_ge(Sh["h_s"], h + 1)
                                dve.tensor_reduce(nm[:, 0, h, 0:1], ps[:, h % 2, 0:NM], AX_X, ALU.max)
                                dve.tensor_reduce(nm[:, 0, h, 1:2], ps[:, h % 2, NM:L], AX_X, ALU.max)
                                dve.drain()
                                dve.tensor_scalar(nm[:, 1, h, :], nm[:, 0, h, :], -float(HD) ** -0.5, None, ALU.mult)
                                dve.drain().then_inc(Sh["h_max"], 1)
                            if h >= 1:
                                g = h - 1
                                dve.wait_ge(Sh["h_pt"], g + 1)
                                if g >= 2:
                                    dve.wait_ge(Sh["h_o"], g - 1)
                                dve.tensor_copy(pT[:, g % 2, :], ps[:, 2 + g % 2, :]).then_inc(Sh["h_ptc"], 1)
                        dve.wait_ge(Sh["h_exp"], H)
                        dve.reciprocal(sm[:, :, :], sm[:, :, :])
                        dve.drain()
                        dve.wait_ge(Sh["h_o"], H)
                        for n in range(2):
                            ov = ps[:, 4 + n, :].rearrange("p (h s d) -> p h s d", s=2, d=HD)
                            for s in range(2):
                                dst = o[:, 2 * s, 256 * n:256 * n + 256].rearrange("p (h d) -> p h d", d=HD)
                                dve.tensor_tensor(dst, ov[:, :, s, :], sm[:, s, 8 * n:8 * n + 8].unsqueeze(2)
                                                  .broadcast_to((P, 8, HD)), ALU.mult)
                        dve.drain()
                        dve.tensor_tensor(o[:, 0, :], o[:, 0, :], o[:, 2, :], ALU.add)
                        dve.drain().then_inc(Sh["h_on"], 1)
                        xj = x[:, bass.ds(TJ * b + j, 1), :].rearrange("p a d -> p (a d)")
                        dve.tensor_tensor(xj, xj, bo[:, :], ALU.add)
                        dve.drain()
                        dve.wait_ge(Sh["h_y"], 1)
                        dve.tensor_tensor(xj, xj, ps[:, 7, :], ALU.add)

                    @blk.scalar
                    def _(act):
                        for h in range(H):
                            act.wait_ge(Sh["h_max"], h + 1)
                            if h >= 2:
                                act.wait_ge(Sh["h_pt"], h - 1)
                            for s, (a, z) in enumerate(((0, NM), (NM, L))):
                                act.activation(pr[:, h % 2, a:z], ps[:, h % 2, a:z], ACT.Exp,
                                               bias=nm[:, 1, h, s:s + 1], scale=float(HD) ** -0.5,
                                               accum_out=sm[:, s, h:h + 1])
                            act.drain().then_inc(Sh["h_exp"], 1)
                        act.wait_ge(Sh["h_ot"], 1)
                        act.copy(o[:, 1, :], ps[:, 6, :]).then_inc(Sh["h_otc"], 1)


def expert_ffn(nc, C, W):
    E, F, TOK = 8, 448, B * L
    FM, FP = 4, 112
    x, ps, ident = C.x, C.ps, C.ident
    with ExitStack() as ctx:
        def sb(name, shape, dt=F32):
            return ctx.enter_context(nc.sbuf_tensor("e_" + name, shape, dt))

        S = Signals(nc, ctx, ["e_ld", "e_scr"])
        Sb = Signals(nc, ctx, LN_SIGNALS + ["e_sc", "e_scc", "e_max", "e_exp", "e_g", "e_gt"])
        Se = Signals(nc, ctx, ["ex_w", "ex_s", "ex_in", "ex_h", "ex_sl", "ex_g", "ex_y", "ex_yx"])
        Sw = Signals(nc, ctx, ["ex_w2"])
        C.xn = sb("xn", [P, TJ, D])
        xT = sb("xT", [P, KD, TOK])
        xTb = sb("xTb", [P, KD, L])
        gw = sb("gw", [P, KD, E])
        eb = sb("eb", [P, E])
        iota = sb("iota", [P, 32])
        sc = sb("sc", [P, TJ, E])
        top = sb("top", [P, TJ, 8])
        idx = sb("idx", [P, TJ, 8], U32)
        idxf = sb("idxf", [P, TJ, 2])
        sel = sb("sel", [P, TJ, E])
        e = sb("e", [P, TJ, E])
        bi = sb("bi", [P, TJ, E])
        nmx = sb("nmx", [P, TJ])
        sm = sb("sm", [P, TJ])
        gT = sb("gT", [E, TOK])
        w1 = sb("w1", [P, KD, F])
        w3 = sb("w3", [P, KD, F])
        w2 = sb("w2", [FP, FM, D])
        sbc = sb("sbc", [P, TOK])
        sl = sb("sl", [FP, 2, L])
        hT = sb("hT", [FP, 2, FM, L])
        xs = sb("xs", [P, 2, KD, L])
        S.fresh()
        load_all(nc, S, [(gw[:, :, :], rows(W["L1_ffn_gate_w"])), (eb[:, :], everywhere(W["L1_ffn_expert_bias"])),
                         (iota[:, :], everywhere(W["c_iota"]))], "e_ld")
        with nc.Fori(0, B) as b:
            Sb.fresh()
            layernorm_T(nc, C, Sb, b, xTb)
            with nc.Block() as blk:
                @blk.tensor
                def _(pe):
                    for j in range(TJ):
                        for k in range(KD):
                            mm = pe.matmul(ps[:, 0, E * j:E * j + E], xTb[:, k, P * j:P * j + P], gw[:, k, :],
                                           start=(k == 0), stop=(k == KD - 1))
                    mm.then_inc(Sb["e_sc"], 1)
                    pe.wait_ge(Sb["e_g"], 1)
                    for j in range(TJ):
                        mm = pe.transpose(ps[0:E, 1, P * j:P * j + P], e[:, j, :], ident[:, :])
                    mm.then_inc(Sb["e_gt"], 1)

                @blk.scalar
                def _(act):
                    act.wait_ge(Sb["e_sc"], 1)
                    act.copy(sc[:, :, :], ps[:, 0, 0:TJ * E].rearrange("p (j s) -> p j s", s=E)
                             ).then_inc(Sb["e_scc"], 1)
                    act.wait_ge(Sb["e_max"], 1)
                    for j in range(TJ):
                        act.activation(e[:, j, :], sc[:, j, :], ACT.Exp, bias=nmx[:, j:j + 1], accum_out=sm[:, j:j + 1])
                    act.drain().then_inc(Sb["e_exp"], 1)
                    act.wait_ge(Sb["e_gt"], 1)
                    act.copy(gT[:, bass.ds(L * b, L)], ps[0:E, 1, :])

                @blk.vector
                def _(dve):
                    for k in range(KD):
                        dve.tensor_copy(xT[:, k, bass.ds(L * b, L)], xTb[:, k, :])
                    dve.wait_ge(Sb["e_scc"], 1)
                    dve.tensor_reduce(nmx[:, :], sc[:, :, :], AX_X, ALU.max, negate=True)
                    dve.drain().then_inc(Sb["e_max"], 1)
                    dve.wait_ge(Sb["e_exp"], 1)
                    dve.reciprocal(sm[:, :], sm[:, :])
                    dve.drain()
                    dve.tensor_tensor(e[:, :, :], e[:, :, :], sm[:, :].unsqueeze(2).broadcast_to((P, TJ, E)), ALU.mult)
                    dve.drain()
                    dve.tensor_tensor(bi[:, :, :], e[:, :, :], eb[:, :].unsqueeze(1).broadcast_to((P, TJ, E)), ALU.add)
                    dve.drain()
                    for j in range(TJ):
                        top_two(dve, bi[:, j, :], top[:, j, :], idx[:, j, :], idxf[:, j, :], iota, sel[:, j, :], E)
                    dve.tensor_tensor(e[:, :, :], e[:, :, :], sel[:, :, :], ALU.mult)
                    dve.drain().then_inc(Sb["e_g"], 1)
        S.fresh()
        with nc.Block() as blk:
            @blk.sync
            def _(sp):
                sp.dma_start(C.scratch[0:E, :], gT[:, :]).then_inc(S["e_scr"], 16)
                sp.wait_ge(S["e_scr"], 16)

        def expert(w1d, w3d, w2d, scores):
            Se.fresh()
            with nc.Block() as blk:
                @blk.sync
                def _(sp):
                    sp.dma_start(w1[:, :, :], w1d).then_inc(Se["ex_w"], 16)
                    sp.dma_start(w3[:, :, :], w3d).then_inc(Se["ex_w"], 16)
                    sp.dma_start(w2[:, :, :], w2d).then_inc(Sw["ex_w2"], 16)
                    if scores is not None:
                        sp.dma_start(sbc[:, :], scores.broadcast_to((P, TOK))).then_inc(Se["ex_s"], 16)
                    sp.wait_ge(Se["ex_w"], 32)
                    sp.wait_ge(Sw["ex_w2"], 16)

                if scores is not None:
                    @blk.gpsimd
                    def _(pool):
                        pool.wait_ge(Se["ex_s"], 16)
                        for b in range(B):
                            if b >= 2:
                                pool.wait_ge(Se["ex_h"], 2 * FM * (b - 1))
                            for k in range(KD):
                                pool.tensor_tensor(xs[:, b % 2, k, :], xT[:, k, L * b:L * b + L],
                                                   sbc[:, L * b:L * b + L], ALU.mult).then_inc(Se["ex_in"], 1)

                @blk.tensor
                def _(pe):
                    pe.wait_ge(Se["ex_w"], 32)
                    pe.wait_ge(Sw["ex_w2"], 16)

                    def out(b):
                        pe.wait_ge(Se["ex_g"], FM * (b + 1))
                        for j in range(TJ):
                            if b >= 1:
                                pe.wait_ge(Se["ex_yx"], TJ * (b - 1) + j + 1)
                            for m in range(FM):
                                mm = pe.matmul(ps[:, 4 + j, :], hT[:, b % 2, m, P * j:P * j + P], w2[:, m, :],
                                               start=(m == 0), stop=(m == FM - 1))
                            mm.then_inc(Se["ex_y"], 1)

                    for b in range(B):
                        for m in range(FM):
                            i = FM * b + m
                            for n, w in ((0, w1), (1, w3)):
                                if i >= 2:
                                    pe.wait_ge(Se["ex_g" if n else "ex_sl"], i - 1)
                                for k in range(KD):
                                    if scores is not None:
                                        pe.wait_ge(Se["ex_in"], KD * b + k + 1)
                                        rhs = xs[:, b % 2, k, :]
                                    else:
                                        rhs = xT[:, k, L * b:L * b + L]
                                    mm = pe.matmul(ps[0:FP, 2 * (i % 2) + n, :], w[:, k, FP * m:FP * m + FP], rhs,
                                                   start=(k == 0), stop=(k == KD - 1))
                                mm.then_inc(Se["ex_h"], 1)
                        if b >= 1:
                            out(b - 1)
                    out(B - 1)

                @blk.scalar
                def _(act):
                    for i in range(FM * B):
                        act.wait_ge(Se["ex_h"], 2 * i + 1)
                        if i >= 2:
                            act.wait_ge(Se["ex_g"], i - 1)
                        act.activation(sl[:, i % 2, :], ps[0:FP, 2 * (i % 2), :], ACT.Silu).then_inc(Se["ex_sl"], 1)

                @blk.vector
                def _(dve):
                    def add(b):
                        for j in range(TJ):
                            dve.wait_ge(Se["ex_y"], TJ * b + j + 1)
                            dve.tensor_tensor(x[:, TJ * b + j, :], x[:, TJ * b + j, :], ps[:, 4 + j, :], ALU.add
                                              ).then_inc(Se["ex_yx"], 1)

                    for b in range(B):
                        for m in range(FM):
                            i = FM * b + m
                            dve.wait_ge(Se["ex_h"], 2 * i + 2)
                            dve.wait_ge(Se["ex_sl"], i + 1)
                            if m == 0 and b >= 2:
                                dve.wait_ge(Se["ex_y"], TJ * (b - 1))
                            dve.tensor_tensor(hT[:, b % 2, m, :], sl[:, i % 2, :], ps[0:FP, 2 * (i % 2) + 1, :],
                                              ALU.mult).then_inc(Se["ex_g"], 1)
                        if b >= 1:
                            add(b - 1)
                    add(B - 1)

        def tall(ap):
            return ap.rearrange("(m p) n -> p m n", p=FP)
        Sw.fresh()
        expert(rows(W["L1_ffn_sw1"]), rows(W["L1_ffn_sw3"]), tall(W["L1_ffn_sw2"]), None)
        with nc.Fori(0, E) as ex:
            Sw.fresh()

            def of(name):
                return W[name][bass.ds(ex, 1)].rearrange("a m n -> (a m) n")
            expert(rows(of("L1_ffn_w1")), rows(of("L1_ffn_w3")), tall(of("L1_ffn_w2")), C.scratch[bass.ds(ex, 1), :])


def program(nc, W, out, scratch, stages):
    with ExitStack() as ctx:
        C = Chip()
        sb = lambda name, shape: ctx.enter_context(nc.sbuf_tensor(name, shape, F32))
        C.x = sb("x", [P, NT, D])
        C.ident = sb("ident", [P, P])
        C.ones = sb("ones", [P, P])
        C.st = sb("st", [P, TJ, 6])
        C.mv = sb("mv", [P, TJ, 2])
        C.var = sb("var", [P, TJ])
        C.ss = sb("ss", [P, TJ])
        C.rstd = sb("rstd", [P, TJ])
        C.eps5 = sb("eps5", [P, 1])
        C.eps6 = sb("eps6", [P, 1])
        C.lnsd = sb("lnsd", [P, 1])
        C.ps = ctx.enter_context(nc.psum_tensor("ps", [P, 8, 512], F32))
        C.scratch = scratch
        S = Signals(nc, ctx, ["x_in", "x_out"])
        xv = W["x"].rearrange("b (j p) d -> p (b j) d", p=P)
        ov = out.rearrange("b (j p) d -> p (b j) d", p=P)
        with nc.Block() as blk:
            @blk.sync
            def _(sp):
                for b in range(B):
                    sp.dma_start(C.x[:, TJ * b:TJ * b + TJ, :], xv[:, TJ * b:TJ * b + TJ, :]).then_inc(S["x_in"], 16)
                sp.dma_start(C.ident[:, :], W["c_ident"]).then_inc(S["x_in"], 16)
                sp.wait_ge(S["x_in"], 16 * (B + 1))

            @blk.vector
            def _(dve):
                dve.memset(C.ones[:, :], 1.0)
                dve.memset(C.eps5[:, :], 1e-5)
                dve.memset(C.eps6[:, :], 1e-6)
                dve.memset(C.lnsd[:, :], LOG_RSQRT_P)
        for stage in stages:
            stage(nc, C, W)
        with nc.Block() as blk:
            @blk.sync
            def _(sp):
                for b in range(B):
                    sp.dma_start(ov[:, TJ * b:TJ * b + TJ, :], C.x[:, TJ * b:TJ * b + TJ, :]).then_inc(S["x_out"], 16)
                sp.wait_ge(S["x_out"], 16 * B)


def shape_constants():
    import numpy as np
    mask = np.zeros((P, len(LEVELS), P // 2), np.float32)
    second = np.zeros((P, len(LEVELS)), np.float32)
    for l, w in enumerate(LEVELS):
        second[:, l] = np.arange(P) // w % 2
        t = np.arange(P).reshape(-1, 2, w)[:, 1, :].reshape(-1)
        mask[:, l, :] = (np.arange(P)[:, None] // (2 * w) == t[None, :] // (2 * w)) & (second[:, l:l + 1] == 0)
    heads = np.kron(np.eye(4), np.ones((32, 32))).astype(np.float32)
    return {"c_heads": heads, "c_ident": np.eye(P, dtype=np.float32), "c_mask": mask, "c_masku": mask.astype(np.uint32),
            "c_rowm": second, "c_rown": second - 1, "c_iota": np.arange(32, dtype=np.float32),
            "c_isd": np.stack([np.arange(P) < P - 16, np.arange(P) >= P - 16], 1).astype(np.float32)}


def kernel(**inputs):
    import numpy as np
    import concourse.bacc as bacc
    from concourse.bass_utils import run_bass_kernel_spmd as run

    nc = bacc.Bacc("TRN2", target_bir_lowering=False, num_devices=1)
    arrays = {n: np.ascontiguousarray(layout(n, np.asarray(a))) for n, a in inputs.items()}
    arrays.update(shape_constants())
    W = {n: nc.dram_tensor("in_" + n, a.shape, mybir.dt.from_np(a.dtype), kind="ExternalInput").ap()
         for n, a in arrays.items()}
    out = nc.dram_tensor("out_0", (B, L, D), F32, kind="ExternalOutput").ap()
    scratch = nc.dram_tensor("scratch", (16, B * L), F32).ap()
    program(nc, W, out, scratch, STAGES)
    r = run(nc, [{"in_" + n: a for n, a in arrays.items()}], core_ids=[0])
    return r.results[0]["out_0"]


def layout(name, a):
    if name == "ctx_1024":
        return a.transpose(0, 2, 1)
    if name in ("L0_xattn_Wq", "L0_xattn_Wk", "L0_ffn_Wr"):
        return a.T
    if name in PER_CHANNEL:
        return a.reshape(-1, min(P, a.size)).T
    if name == "L0_attn_bkg2":
        return a.reshape(KD, 4, 16).transpose(1, 2, 0)
    if name == "L0_ffn_U":
        return a.transpose(1, 0, 2).reshape(D, -1)
    if name == "L0_ffn_V":
        return a.reshape(-1, D)
    return a


PER_CHANNEL = ("L0_attn_ln1_w", "L0_attn_ln2_w", "L0_xattn_bq", "L0_xattn_bk", "L1_attn_dt_bias", "L1_attn_o_norm_w",
               "L1_xattn_qn_w", "L1_xattn_qn_b", "L1_xattn_kn_w", "L1_xattn_kn_b", "L1_xattn_kn_dca_w",
               "L1_xattn_kn_dca_b")
LOG_RSQRT_P = -0.5 * math.log(P)
STAGES = [gla_layer, context_mix, low_rank_ffn, delta_attention, cross_attention, expert_ffn]
```

```python
import math
from contextlib import ExitStack

import concourse.bass as bass
from concourse import mybir

ALU = mybir.AluOpType
ACT = mybir.ActivationFunctionType
AX_X = mybir.AxisListType.X
F32 = mybir.dt.float32
U32 = mybir.dt.uint32
P = 128
B, L, D = 4, 512, 512
TJ = L // P
KD = D // P
NT = B * TJ
LEVELS = [1, 2, 4, 8, 16, 32, 64]


class Signals:

    def __init__(self, nc, ctx, names, keys=None):
        self.nc = nc
        self.sems = [ctx.enter_context(nc.semaphore(n)) for n in names]
        self.of = dict(zip(keys or names, self.sems))

    def __getitem__(self, name):
        return self.of[name]

    def clear(self):
        nums = sorted(s.num for s in self.sems)
        run = [nums[0], nums[0]]
        for n in nums[1:] + [None]:
            if n == run[1] + 1:
                run[1] = n
                continue
            self.nc.sync.sem_clear(range(run[0], run[1] + 1))
            run = [n, n]

    def fresh(self):
        self.clear()
        self.nc.all_engine_barrier()


class Chip:
    pass


def rsqrt_small(act, S, src, dst, ready, done):
    act.wait_ge(S[ready], 1)
    act.activation(dst, src, ACT.Ln)
    act.drain()
    act.activation(dst, dst, ACT.Exp, scale=-0.5)
    act.drain().then_inc(S[done], 1)


def layernorm_T(nc, C, S, b, xT, w=None):
    x, xn, ps = C.x, C.xn, C.ps
    with nc.Block() as blk:
        @blk.vector
        def _(dve):
            for j in range(TJ):
                dve.bn_stats(C.st[:, j, :], x[:, TJ * b + j, :])
            dve.drain()
            for j in range(TJ):
                dve.bn_aggr(C.mv[:, j, :], C.st[:, j, :])
            dve.drain()
            dve.tensor_scalar(C.var[:, :], C.mv[:, :, 1], 1e-5, None, ALU.add)
            dve.drain().then_inc(S["ln_var"], 1)
            dve.wait_ge(S["ln_rstd"], 1)
            for j in range(TJ):
                dve.tensor_scalar(xn[:, j, :], x[:, TJ * b + j, :], C.mv[:, j, 0:1], C.rstd[:, j:j + 1],
                                  ALU.subtract, ALU.mult).then_inc(S["ln_xn"], 1)

        @blk.scalar
        def _(act):
            rsqrt_small(act, S, C.var[:, :], C.rstd[:, :], "ln_var", "ln_rstd")
            if w is None:
                for k in range(KD):
                    act.wait_ge(S["ln_tr"], k + 1)
                    act.copy(xT[:, k, :], ps[:, k, :])

        @blk.tensor
        def _(pe):
            if w is None:
                pe.wait_ge(S["ln_xn"], TJ)
                for k in range(KD):
                    for j in range(TJ):
                        mm = pe.transpose(ps[:, k, P * j:P * j + P], xn[:, j, P * k:P * k + P], C.ident[:, :])
                    mm.then_inc(S["ln_tr"], 1)
    if w is not None:
        rmsnorm_T(nc, C, S, xn, xT, w, "r1")


def rmsnorm_T(nc, C, S, src, xT, w, tag):
    ps = C.ps
    with nc.Block() as blk:
        @blk.scalar
        def _(act):
            for j in range(TJ):
                act.activation(C.xr[:, j, :], src[:, j, :], ACT.Square, accum_out=C.ss[:, j:j + 1])
            act.drain()
            act.activation(C.var[:, :], C.ss[:, :], ACT.Ln, scale=1.0 / D, bias=C.eps5[:, 0:1])
            act.drain()
            act.activation(C.rstd[:, :], C.var[:, :], ACT.Exp, scale=-0.5).then_inc(S[tag + "_rstd"], 1)
            for k in range(KD):
                act.wait_ge(S[tag + "_tr"], k + 1)
                act.activation(xT[:, k, :], ps[:, k, :], ACT.Copy, scale=w[:, k:k + 1])

        @blk.vector
        def _(dve):
            dve.wait_ge(S[tag + "_rstd"], 1)
            for j in range(TJ):
                dve.tensor_scalar(C.xr[:, j, :], src[:, j, :], C.rstd[:, j:j + 1], None,
                                  ALU.mult).then_inc(S[tag + "_xr"], 1)

        @blk.tensor
        def _(pe):
            pe.wait_ge(S[tag + "_xr"], TJ)
            for k in range(KD):
                for j in range(TJ):
                    mm = pe.transpose(ps[:, k, P * j:P * j + P], C.xr[:, j, P * k:P * k + P], C.ident[:, :])
                mm.then_inc(S[tag + "_tr"], 1)


def halves(ap, h):
    v = ap.rearrange("p (n a r) -> p n a r", a=2, r=h)
    return v[:, :, 0, :], v[:, :, 1, :]


LN_SIGNALS = ["ln_var", "ln_rstd", "ln_xn", "ln_tr"]


def load_all(nc, S, pairs, name):
    with nc.Block() as blk:
        @blk.sync
        def _(sp):
            for dst, src in pairs[0::2]:
                sp.dma_start(dst, src).then_inc(S[name], 16)
            sp.wait_ge(S[name], 16 * len(pairs))

        @blk.scalar
        def _(act):
            for dst, src in pairs[1::2]:
                act.dma_start(dst, src).then_inc(S[name], 16)


def rows(ap):
    return ap.rearrange("(k p) n -> p k n", p=P)


def everywhere(ap, p=P):
    return ap.rearrange("(a n) -> a n", a=1).broadcast_to((p, ap.shape[0]))


TILE_SIGNALS = ["gp", "qk", "qk_sb", "abs", "softplus", "summed", "decay", "products", "diag", "diag_sb",
                "q_scaled", "k_scaled", "spread", "pairs", "masked", "kt", "kt_sb", "dstate", "state", "o", "o_sb"]


def gla_layer(nc, C, W):
    H, KH, VH, F = 16, 16, 32, 1408
    FM = F // P
    x, ps, ident = C.x, C.ps, C.ident
    with ExitStack() as ctx:
        def sb(name, shape, dt=F32):
            return ctx.enter_context(nc.sbuf_tensor("g_" + name, shape, dt))

        S = Signals(nc, ctx, ["g_ld"])
        Sb = Signals(nc, ctx, LN_SIGNALS + ["r1_rstd", "r1_tr", "r1_xr", "r2_rstd", "r2_tr", "r2_xr", "m_h", "m_s",
                                            "m_g", "m_y", "m_x"])
        Sc = Signals(nc, ctx, ["c_gp", "c_p", "c_v", "c_vb"])
        St_ = [Signals(nc, ctx, [f"t{u}_{n}" for n in TILE_SIGNALS], TILE_SIGNALS) for u in range(2)]
        Sn = Signals(nc, ctx, ["n_sq", "n_rs", "n_sg", "n_o", "n_tr", "n_trc", "n_y", "n_g"])
        xa = sb("xa", [P, TJ, D])
        C.xn = xa
        C.xr = sb("xr", [P, TJ, D])
        ln1 = sb("ln1", [P, KD])
        ln2 = sb("ln2", [P, KD])
        xT = sb("xT", [P, KD, L])
        ctx2 = ExitStack()

        def sa(name, shape, dt=F32):
            return ctx2.enter_context(nc.sbuf_tensor("ga_" + name, shape, dt))
        o_all = sb("o_all", [P, NT, D])
        with ctx2:
            wq = sa("wq", [P, KD, D])
            wk = sa("wk", [P, KD, D])
            wkg1 = sa("wkg1", [P, KD, KH])
            wkg2 = sa("wkg2", [KH, D])
            bkg = sa("bkg", [P, KD])
            bkgn = sa("bkgn", [P, KD])
            wv = sa("wv", [P, KD, D])
            wg = sa("wg", [P, KD, D])
            bg = sa("bg", [P, D])
            wo = sa("wo", [P, KD, D])
            masku = sa("masku", [P, 7, 64], U32)
            bdm = sa("bdm", [P, P])
            lr = sa("lr", [KH, L])
            kS = sa("kS", [P, 2, L])
            qS = sa("qS", [P, 2, L])
            dec = sa("dec", [P, 2, L])
            dec2 = sa("dec2", [P, 2, L])
            v = sa("v", [P, TJ, D])
            g = sa("g", [P, TJ, D])
            A_ = sa("A", [P, 2, 16, P])
            o = sa("o", [P, TJ, D])
            kt = sa("kt", [P, 2, TJ, P])
            qb = sa("qb", [P, 2, TJ, 4, 64])
            work = C.xr[:, :, :].rearrange("p (a u) (c s) -> p a u c s", u=2, s=P)
            tmp, state = work[:, 0], work[:, 1]
            mom = sa("mom", [P, 2, TJ * H])

            pad = lambda t: t.rearrange("p k (h c) -> p k h c", c=32)
            S.fresh()
            with nc.Block() as blk:
                @blk.vector
                def _(dve):
                    dve.memset(wq[:, :, :], 0.0)
                    dve.memset(wk[:, :, :], 0.0)
                    dve.memset(wkg2[:, :], 0.0)
                    dve.memset(qb[:, :, :, :, :], 0.0)
                    dve.memset(bkg[:, :], 0.0)
            pairs = [(pad(w[:, :, :])[:, k, :, 0:KH],
                      W[n].rearrange("(k p) (h c) -> p k h c", p=P, c=KH)[:, k])
                     for w, n in ((wq, "L0_attn_Wq"), (wk, "L0_attn_Wk")) for k in range(KD)]
            pairs += [(wkg2[:, :].rearrange("p (h c) -> p h c", c=32)[:, :, 0:KH],
                       W["L0_attn_Wkg2"].rearrange("p (h c) -> p h c", c=KH))]
            pairs += [(bkg[32 * i:32 * i + KH, :], W["L0_attn_bkg2"][i]) for i in range(4)]
            pairs += [(wkg1[:, :, :], rows(W["L0_attn_Wkg1"])), (wv[:, :, :], rows(W["L0_attn_Wv"])),
                      (wg[:, :, :], rows(W["L0_attn_Wg"])), (wo[:, :, :], rows(W["L0_attn_Wo"])),
                      (bg[:, :], everywhere(W["L0_attn_bg"])), (ln1[:, :], W["L0_attn_ln1_w"]),
                      (ln2[:, :], W["L0_attn_ln2_w"]), 
                      (masku[:, :, :], W["c_masku"]), (bdm[:, :], W["c_heads"])]
            load_all(nc, S, pairs, "g_ld")
            with nc.Block() as blk:
                @blk.vector
                def _(dve):
                    dve.tensor_scalar(bkgn[:, :], bkg[:, :], -1.0, None, ALU.mult)

            with nc.Fori(0, B) as b:
                Sb.fresh()
                layernorm_T(nc, C, Sb, b, xT, ln1)
                Sc.fresh()
                with nc.Block() as blk:
                    @blk.tensor
                    def _(pe):
                        for k in range(KD):
                            mm = pe.matmul(ps[0:KH, 7, :], wkg1[:, k, :], xT[:, k, :], start=(k == 0),
                                           stop=(k == KD - 1))
                        mm.then_inc(Sc["c_gp"], 1)
                        for j in range(TJ):
                            for n, w in ((2 * (j % 2), wv), (2 * (j % 2) + 1, wg)):
                                if j >= 2:
                                    pe.wait_ge(Sc["c_v" if w is wv else "c_vb"], j - 1)
                                for k in range(KD):
                                    mm = pe.matmul(ps[:, n, :], xT[:, k, P * j:P * j + P], w[:, k, :],
                                                   start=(k == 0), stop=(k == KD - 1))
                                mm.then_inc(Sc["c_p"], 1)

                    @blk.scalar
                    def _(act):
                        act.wait_ge(Sc["c_gp"], 1)
                        act.copy(lr[:, :], ps[0:KH, 7, :])
                        for j in range(TJ):
                            act.wait_ge(Sc["c_p"], 2 * j + 1)
                            act.copy(v[:, j, :], ps[:, 2 * (j % 2), :]).then_inc(Sc["c_v"], 1)
                        for j in range(TJ):
                            act.wait_ge(Sc["c_vb"], j + 1)
                            act.activation(g[:, j, :], g[:, j, :], ACT.Silu)

                    @blk.vector
                    def _(dve):
                        for j in range(TJ):
                            dve.wait_ge(Sc["c_p"], 2 * j + 2)
                            dve.tensor_tensor(g[:, j, :], ps[:, 2 * (j % 2) + 1, :], bg[:, :], ALU.add
                                              ).then_inc(Sc["c_vb"], 1)
                for t0 in range(0, KD, 2):
                    for s in St_:
                        s.clear()
                    nc.all_engine_barrier()
                    with nc.Block() as blk:
                        def hs(u):
                            return slice(P * (t0 + u), P * (t0 + u) + P)

                        def pair_bank(u, l, m):
                            return 4 * u + 2 * (l % 2) + m

                        @blk.tensor
                        def _(pe):
                            for u in range(2):
                                s = St_[u]
                                pe.matmul(ps[:, 4 * u, :], wkg2[:, hs(u)], lr[:, :], start=True, stop=True
                                          ).then_inc(s["gp"], 1)
                                for n, w in ((1, wq), (2, wk)):
                                    for k in range(KD):
                                        mm = pe.matmul(ps[:, 4 * u + n, :], w[:, k, hs(u)], xT[:, k, :],
                                                       start=(k == 0), stop=(k == KD - 1))
                                    mm.then_inc(s["qk"], 1)
                            for u in range(2):
                                s = St_[u]
                                pe.wait_ge(s["products"], 1)
                                for c in range(TJ):
                                    mm = pe.matmul(ps[:, 4 * u + 3, 4 * c:4 * c + 4], tmp[:, u, c, :],
                                                   bdm[:, 0:P:32], start=True, stop=True)
                                mm.then_inc(s["diag"], 1)
                            for l, w in enumerate(LEVELS):
                                for u in range(2):
                                    s = St_[u]
                                    pe.wait_ge(s["spread"], l + 1)
                                    if l == 0:
                                        pe.wait_ge(s["summed"], 1)
                                        pe.wait_ge(s["qk_sb"], 2)
                                    else:
                                        pe.wait_ge(s["k_scaled"], l)
                                    if l == 1:
                                        pe.wait_ge(s["diag_sb"], 1)
                                    if l >= 2:
                                        pe.wait_ge(s["masked"], 2 * (l - 1))
                                    for c in range(TJ):
                                        a = 256 * (c % 2)
                                        mm = pe.matmul(ps[:, pair_bank(u, l, c // 2), a:a + 256],
                                                       kS[:, u, P * c:P * c + P],
                                                       qb[:, u, c, :, :].rearrange("p i t -> p (i t)"),
                                                       start=True, stop=True)
                                    mm.then_inc(s["pairs"], 1)
                            for u in range(2):
                                s = St_[u]
                                pe.wait_ge(s["k_scaled"], len(LEVELS))
                                pe.wait_ge(s["q_scaled"], len(LEVELS) + 1)
                                pe.wait_ge(s["masked"], 2 * len(LEVELS))
                                for c in range(TJ):
                                    mm = pe.transpose(ps[:, 4 * u, P * c:P * c + P], kS[:, u, P * c:P * c + P],
                                                      ident[:, :])
                                mm.then_inc(s["kt"], 1)
                            for c in range(TJ):
                                for u in range(2):
                                    s = St_[u]
                                    if c == 0:
                                        pe.wait_ge(s["kt_sb"], 1)
                                    if c < TJ - 1:
                                        if c >= 1:
                                            pe.wait_ge(s["state"], c)
                                        pe.matmul(ps[:, 4 * u + 3, 0:P], kt[:, u, c, :], v[:, c, hs(u)],
                                                  start=True, stop=True).then_inc(s["dstate"], 1)
                                    oc = ps[:, 4 * u + 1 + c % 2, 0:P]
                                    if c >= 2:
                                        pe.wait_ge(s["o_sb"], c - 1)
                                    if c >= 1:
                                        pe.wait_ge(s["state"], c)
                                        pe.matmul(oc, qS[:, u, P * c:P * c + P], state[:, u, c - 1, :], start=True,
                                                  stop=False, skip_group_check=True)
                                    for i in range(4):
                                        a = P * (t0 + u) + VH * i
                                        mm = pe.matmul(oc[:, VH * i:VH * i + VH], A_[:, u, 4 * c + i, :],
                                                       v[:, c, a:a + VH], start=(c == 0), stop=(i == 3),
                                                       skip_group_check=True)
                                    mm.then_inc(s["o"], 1)

                        @blk.scalar
                        def _(act):
                            for u in range(2):
                                act.wait_ge(St_[u]["gp"], 1)
                                act.activation(dec2[:, u, :], ps[:, 4 * u, :], ACT.Abs, bias=bkg[:, t0 + u:t0 + u + 1])
                                act.drain().then_inc(St_[u]["abs"], 1)
                                act.activation(dec2[:, u, :], dec2[:, u, :], ACT.Exp, scale=-1.0)
                            act.drain()
                            for u in range(2):
                                act.activation(dec2[:, u, :], dec2[:, u, :], ACT.Ln, bias=1.0
                                               ).then_inc(St_[u]["softplus"], 1)
                            for u in range(2):
                                s = St_[u]
                                act.wait_ge(s["qk"], 1)
                                act.copy(qS[:, u, :], ps[:, 4 * u + 1, :]).then_inc(s["qk_sb"], 1)
                                act.wait_ge(s["qk"], 2)
                                act.mul(kS[:, u, :], ps[:, 4 * u + 2, :], float(VH) ** -0.5).then_inc(s["qk_sb"], 1)
                            for u in range(2):
                                act.wait_ge(St_[u]["summed"], 1)
                                act.activation(dec[:, u, :], dec[:, u, :], ACT.Exp, scale=-1.0 / 16.0
                                               ).then_inc(St_[u]["decay"], 1)
                            for l, w in enumerate(LEVELS):
                                for u in range(2):
                                    s = St_[u]
                                    act.wait_ge(s["q_scaled"], l + 1)
                                    if l:
                                        act.wait_ge(s["pairs"], l)
                                    for i in range(4):
                                        r = slice(32 * i, 32 * i + 32)
                                        act.copy(qb[r, u, :, i, :].rearrange("p c (n r) -> p c n r", r=w),
                                                 halves(qS[r, u, :], w)[1].rearrange("p (c n) r -> p c n r", c=TJ))
                                    act.drain().then_inc(s["spread"], 1)
                            for u in range(2):
                                act.wait_ge(St_[u]["kt"], 1)
                                act.copy(kt[:, u, :, :].rearrange("p c s -> p (c s)"), ps[:, 4 * u, :]
                                         ).then_inc(St_[u]["kt_sb"], 1)
                            for c in range(TJ):
                                for u in range(2):
                                    act.wait_ge(St_[u]["o"], c + 1)
                                    act.copy(o[:, c, hs(u)], ps[:, 4 * u + 1 + c % 2, 0:P]).then_inc(St_[u]["o_sb"], 1)

                        @blk.vector
                        def _(dve):
                            for u in range(2):
                                dve.wait_ge(St_[u]["abs"], 1)
                                dve.tensor_scalar(dec[:, u, :], ps[:, 4 * u, :], -1.0, bkgn[:, t0 + u:t0 + u + 1],
                                                  ALU.mult, ALU.add)
                                dve.drain()
                                dve.tensor_scalar(dec[:, u, :], dec[:, u, :], 0.0, None, ALU.max)
                            dve.drain()
                            for u in range(2):
                                dve.wait_ge(St_[u]["softplus"], 1)
                                dve.tensor_tensor(dec[:, u, :], dec[:, u, :], dec2[:, u, :], ALU.add
                                                  ).then_inc(St_[u]["summed"], 1)
                            for u in range(2):
                                dve.wait_ge(St_[u]["qk_sb"], 2)
                                dve.tensor_tensor(tmp[:, u, :, :].rearrange("p c s -> p (c s)"), qS[:, u, :],
                                                  kS[:, u, :], ALU.mult).then_inc(St_[u]["products"], 1)
                            for u in range(2):
                                dve.wait_ge(St_[u]["diag"], 1)
                                dve.tensor_tensor(A_[:, u, :, :],
                                                  ps[:, 4 * u + 3, 0:16].unsqueeze(2).broadcast_to((P, 16, P)),
                                                  ident[:, :].unsqueeze(1).broadcast_to((P, 16, P)), ALU.mult
                                                  ).then_inc(St_[u]["diag_sb"], 1)
                            dve.drain()
                            for l, w in enumerate(LEVELS):
                                for u in range(2):
                                    dve.wait_ge(St_[u]["pairs"], l + 1)
                                    for m in range(2):
                                        Av = A_[:, u, 8 * m:8 * m + 8, :].rearrange("p c (n a r) -> p c n a r",
                                                                                    a=2, r=w)
                                        dve.copy_predicated(
                                            Av[:, :, :, 1, :],
                                            masku[:, l, :].unsqueeze(1).broadcast_to((P, 8, 64)).rearrange(
                                                "p c (n r) -> p c n r", r=w),
                                            ps[:, pair_bank(u, l, m), :].rearrange("p (c n r) -> p c n r", c=8, r=w)
                                        ).then_inc(St_[u]["masked"], 1)
                                dve.drain()
                            Dc = dec2 if len(LEVELS) % 2 else dec
                            for c in range(TJ - 1):
                                for u in range(2):
                                    s = St_[u]
                                    dve.wait_ge(s["dstate"], c + 1)
                                    to = state[:, u, c, :]
                                    if c == 0:
                                        dve.tensor_tensor(to, ps[:, 4 * u + 3, 0:P], bdm[:, :], ALU.mult)
                                    else:
                                        dve.tensor_tensor(tmp[:, u, c, :], ps[:, 4 * u + 3, 0:P], bdm[:, :], ALU.mult)
                                        dve.drain()
                                        dve.scalar_tensor_tensor(to, state[:, u, c - 1, :], Dc[:, u, c:c + 1],
                                                                 tmp[:, u, c, :], ALU.mult, ALU.add)
                                    dve.drain().then_inc(s["state"], 1)

                        @blk.gpsimd
                        def _(pool):
                            for u in range(2):
                                pool.wait_ge(St_[u]["decay"], 1)
                                pool.wait_ge(St_[u]["products"], 1)
                                pool.tensor_tensor(qS[:, u, :], qS[:, u, :], dec[:, u, :], ALU.mult)
                                pool.drain().then_inc(St_[u]["q_scaled"], 1)
                            src = dec
                            for l, w in enumerate(LEVELS):
                                dst = dec2 if l % 2 == 0 else dec
                                nblk = L // (2 * w)
                                for u in range(2):
                                    pr = src[:, u, 0:2 * nblk].rearrange("p (n a) -> p n a", a=2)
                                    q2 = halves(qS[:, u, :], w)[1]
                                    pool.wait_ge(St_[u]["spread"], l + 1)
                                    pool.tensor_tensor(q2, q2, pr[:, :, 0:1].broadcast_to((P, nblk, w)), ALU.mult)
                                    pool.tensor_tensor(dst[:, u, 0:nblk], pr[:, :, 0], pr[:, :, 1], ALU.mult)
                                    pool.drain().then_inc(St_[u]["q_scaled"], 1)
                                for u in range(2):
                                    pr = src[:, u, 0:2 * nblk].rearrange("p (n a) -> p n a", a=2)
                                    k1 = halves(kS[:, u, :], w)[0]
                                    pool.wait_ge(St_[u]["pairs"], l + 1)
                                    pool.tensor_tensor(k1, k1, pr[:, :, 1:2].broadcast_to((P, nblk, w)), ALU.mult)
                                    pool.drain().then_inc(St_[u]["k_scaled"], 1)
                                src = dst
                Sn.fresh()
                with nc.Block() as blk:
                    ov = o[:, :, :].rearrange("p j (h d) -> p (j h) d", d=VH)
                    rv = C.xr[:, :, :].rearrange("p j (h d) -> p (j h) d", d=VH)

                    def each(m):
                        return mom[:, m, :].unsqueeze(2).broadcast_to((P, TJ * H, VH))

                    @blk.vector
                    def _(dve):
                        dve.tensor_reduce(mom[:, 0, :], ov, AX_X, ALU.add)
                        dve.drain()
                        dve.tensor_scalar(mom[:, 0, :], mom[:, 0, :], 1.0 / VH, None, ALU.mult)
                        dve.drain()
                        dve.tensor_tensor(ov, ov, each(0), ALU.subtract)
                        dve.drain()
                        dve.tensor_tensor(rv, ov, ov, ALU.mult)
                        dve.drain()
                        dve.tensor_reduce(mom[:, 1, :], rv, AX_X, ALU.add)
                        dve.drain().then_inc(Sn["n_sq"], 1)
                        dve.wait_ge(Sn["n_rs"], 1)
                        dve.tensor_tensor(ov, ov, each(1), ALU.mult)
                        dve.drain()
                        dve.tensor_tensor(o[:, :, :], o[:, :, :], g[:, :, :], ALU.mult)
                        dve.drain().then_inc(Sn["n_o"], 1)
                        for j in range(TJ):
                            dve.wait_ge(Sn["n_y"], j + 1)
                            dve.tensor_tensor(o_all[:, bass.ds(TJ * b + j, 1), :].rearrange("p a d -> p (a d)"),
                                              xa[:, j, :], ps[:, 4 + j, :], ALU.add)

                    @blk.scalar
                    def _(act):
                        act.wait_ge(Sn["n_sq"], 1)
                        act.activation(mom[:, 1, :], mom[:, 1, :], ACT.Ln, scale=1.0 / VH, bias=C.eps5[:, 0:1])
                        act.drain()
                        act.activation(mom[:, 1, :], mom[:, 1, :], ACT.Exp, scale=-0.5)
                        act.drain().then_inc(Sn["n_rs"], 1)
                        for k in range(KD):
                            act.wait_ge(Sn["n_tr"], k + 1)
                            act.copy(xT[:, k, :], ps[:, k, :]).then_inc(Sn["n_trc"], 1)

                    @blk.tensor
                    def _(pe):
                        pe.wait_ge(Sn["n_o"], 1)
                        for k in range(KD):
                            for j in range(TJ):
                                mm = pe.transpose(ps[:, k, P * j:P * j + P], o[:, j, P * k:P * k + P], ident[:, :])
                            mm.then_inc(Sn["n_tr"], 1)
                        pe.wait_ge(Sn["n_trc"], KD)
                        for j in range(TJ):
                            for k in range(KD):
                                mm = pe.matmul(ps[:, 4 + j, :], xT[:, k, P * j:P * j + P], wo[:, k, :],
                                               start=(k == 0), stop=(k == KD - 1))
                            mm.then_inc(Sn["n_y"], 1)

        w1 = sb("w1", [P, KD, F])
        w3 = sb("w3", [P, KD, F])
        w2 = sb("w2", [P, FM, D])
        sl = sb("sl", [P, 2, L])
        hT = sb("hT", [P, FM, L])
        S.fresh()
        load_all(nc, S, [(w1[:, :, :], rows(W["L0_attn_W1"])), (w3[:, :, :], rows(W["L0_attn_W3"])),
                         (w2[:, :, :], rows(W["L0_attn_W2"]))], "g_ld")
        with nc.Fori(0, B) as b:
            Sb.fresh()
            with nc.Block() as blk:
                @blk.vector
                def _(dve):
                    dve.tensor_copy(xa[:, :, :], o_all[:, bass.ds(TJ * b, TJ), :])
                    for j in range(TJ):
                        xj = x[:, bass.ds(TJ * b + j, 1), :]
                        dve.tensor_tensor(xj, xj, o_all[:, bass.ds(TJ * b + j, 1), :], ALU.add)
            rmsnorm_T(nc, C, Sb, xa, xT, ln2, "r2")
            with nc.Block() as blk:
                @blk.tensor
                def _(pe):
                    for m in range(FM):
                        for n, w in ((0, w1), (1, w3)):
                            if m >= 2:
                                pe.wait_ge(Sb["m_g" if n else "m_s"], m - 1)
                            for k in range(KD):
                                mm = pe.matmul(ps[:, 2 * (m % 2) + n, :], w[:, k, P * m:P * m + P], xT[:, k, :],
                                               start=(k == 0), stop=(k == KD - 1))
                            mm.then_inc(Sb["m_h"], 1)
                    pe.wait_ge(Sb["m_g"], FM)
                    for j in range(TJ):
                        for m in range(FM):
                            mm = pe.matmul(ps[:, 4 + j, :], hT[:, m, P * j:P * j + P], w2[:, m, :],
                                           start=(m == 0), stop=(m == FM - 1))
                        mm.then_inc(Sb["m_y"], 1)

                @blk.scalar
                def _(act):
                    for m in range(FM):
                        act.wait_ge(Sb["m_h"], 2 * m + 1)
                        if m >= 2:
                            act.wait_ge(Sb["m_g"], m - 1)
                        act.activation(sl[:, m % 2, :], ps[:, 2 * (m % 2), :], ACT.Silu).then_inc(Sb["m_s"], 1)

                @blk.vector
                def _(dve):
                    for m in range(FM):
                        dve.wait_ge(Sb["m_h"], 2 * m + 2)
                        dve.wait_ge(Sb["m_s"], m + 1)
                        dve.tensor_tensor(hT[:, m, :], sl[:, m % 2, :], ps[:, 2 * (m % 2) + 1, :], ALU.mult
                                          ).then_inc(Sb["m_g"], 1)
                    for j in range(TJ):
                        dve.wait_ge(Sb["m_y"], j + 1)
                        xj = x[:, bass.ds(TJ * b + j, 1), :].rearrange("p a d -> p (a d)")
                        dve.tensor_tensor(xj, xj, ps[:, 4 + j, :], ALU.add)


def context_mix(nc, C, W):
    CK = 2
    x, ps, ident = C.x, C.ps, C.ident
    with ExitStack() as ctx:
        def sb(name, shape, dt=F32):
            return ctx.enter_context(nc.sbuf_tensor("m_" + name, shape, dt))

        S = Signals(nc, ctx, ["m_ld"])
        Sb = Signals(nc, ctx, LN_SIGNALS + ["m_ctx", "m_qk", "m_qkc", "m_e", "m_max", "m_exp", "m_p", "m_at", "m_atc",
                                            "m_yy"])
        C.xn = sb("xn", [P, TJ, D])
        xT = sb("xT", [P, KD, L])
        wq = sb("wq", [P, CK, P])
        wk = sb("wk", [P, CK, P])
        bq = sb("bq", [P, 1])
        bk = sb("bk", [P, 1])
        cT = sb("cT", [P, CK, L])
        qT = sb("qT", [P, L])
        kT = sb("kT", [P, L])
        att = sb("att", [P, TJ, L])
        attT = sb("attT", [P, TJ, L])
        mx = sb("mx", [P, TJ])
        sm = sb("sm", [P, TJ])
        S.fresh()
        load_all(nc, S, [(wq[:, :, :], rows(W["L0_xattn_Wq"])), (wk[:, :, :], rows(W["L0_xattn_Wk"])),
                         (bq[:, :], W["L0_xattn_bq"]), (bk[:, :], W["L0_xattn_bk"])], "m_ld")
        with nc.Fori(0, B) as b:
            Sb.fresh()
            layernorm_T(nc, C, Sb, b, xT)
            with nc.Block() as blk:
                @blk.sync
                def _(sp):
                    sp.dma_start(cT[:, :, :], W["ctx_1024"].rearrange("b (k p) n -> b p k n", p=P)[
                        bass.ds(b, 1)].rearrange("a p k n -> (a p) k n")).then_inc(Sb["m_ctx"], 16)

                @blk.tensor
                def _(pe):
                    pe.wait_ge(Sb["m_ctx"], 16)
                    for n, w in ((4, wq), (5, wk)):
                        for k in range(CK):
                            mm = pe.matmul(ps[:, n, :], w[:, k, :], cT[:, k, :], start=(k == 0), stop=(k == CK - 1))
                        mm.then_inc(Sb["m_qk"], 1)
                    pe.wait_ge(Sb["m_qkc"], 2)
                    for m in range(TJ):
                        pe.matmul(ps[:, m, :], qT[:, P * m:P * m + P], kT[:, :], start=True, stop=True
                                  ).then_inc(Sb["m_e"], 1)
                    pe.wait_ge(Sb["m_p"], TJ)
                    for n in range(TJ):
                        for m in range(TJ):
                            mm = pe.transpose(ps[:, 4 + n, P * m:P * m + P], att[:, m, P * n:P * n + P], ident[:, :])
                        mm.then_inc(Sb["m_at"], 1)
                    pe.wait_ge(Sb["m_atc"], TJ)
                    for j in range(TJ):
                        for n in range(TJ):
                            mm = pe.matmul(ps[:, j, :], xT[:, n, P * j:P * j + P], attT[:, n, :],
                                           start=(n == 0), stop=(n == TJ - 1))
                        mm.then_inc(Sb["m_yy"], 1)

                @blk.scalar
                def _(act):
                    act.wait_ge(Sb["m_qk"], 1)
                    act.activation(qT[:, :], ps[:, 4, :], ACT.Identity, bias=bq[:, 0:1]).then_inc(Sb["m_qkc"], 1)
                    act.wait_ge(Sb["m_qk"], 2)
                    act.activation(kT[:, :], ps[:, 5, :], ACT.Identity, bias=bk[:, 0:1]).then_inc(Sb["m_qkc"], 1)
                    for m in range(TJ):
                        act.wait_ge(Sb["m_max"], m + 1)
                        act.activation(att[:, m, :], ps[:, m, :], ACT.Exp, bias=mx[:, m:m + 1],
                                       accum_out=sm[:, m:m + 1])
                        act.drain().then_inc(Sb["m_exp"], 1)
                    for n in range(TJ):
                        act.wait_ge(Sb["m_at"], n + 1)
                        act.copy(attT[:, n, :], ps[:, 4 + n, :]).then_inc(Sb["m_atc"], 1)

                @blk.vector
                def _(dve):
                    for m in range(TJ):
                        dve.wait_ge(Sb["m_e"], m + 1)
                        dve.tensor_reduce(mx[:, m:m + 1], ps[:, m, :], AX_X, ALU.max, negate=True)
                        dve.drain().then_inc(Sb["m_max"], 1)
                    for m in range(TJ):
                        dve.wait_ge(Sb["m_exp"], m + 1)
                        dve.reciprocal(sm[:, m:m + 1], sm[:, m:m + 1])
                        dve.drain()
                        dve.tensor_scalar(att[:, m, :], att[:, m, :], sm[:, m:m + 1], None, ALU.mult
                                          ).then_inc(Sb["m_p"], 1)
                    for j in range(TJ):
                        dve.wait_ge(Sb["m_yy"], j + 1)
                        xj = x[:, bass.ds(TJ * b + j, 1), :].rearrange("p a d -> p (a d)")
                        dve.tensor_tensor(xj, xj, ps[:, j, :], ALU.add)


def top_two(dve, vals, top, idx, idxf, iota, sel, n):
    dve.max(top, vals)
    dve.drain()
    dve.max_index(idx, top, vals)
    dve.drain()
    dve.tensor_copy(idxf, idx[:, 0:2])
    dve.drain()
    dve.tensor_scalar(sel, iota[:, 0:n], idxf[:, 0:1], None, ALU.is_equal)
    dve.drain()
    dve.scalar_tensor_tensor(sel, iota[:, 0:n], idxf[:, 1:2], sel, ALU.is_equal, ALU.add)
    dve.drain()


def low_rank_ffn(nc, C, W):
    NS, R, AD = 32, 16, 32
    x, ps, ident = C.x, C.ps, C.ident
    with ExitStack() as ctx:
        def sb(name, shape, dt=F32):
            return ctx.enter_context(nc.sbuf_tensor("f_" + name, shape, dt))

        S = Signals(nc, ctx, ["f_ld", "f_aw"])
        Sb = Signals(nc, ctx, LN_SIGNALS + ["f_sc", "f_scc", "f_max", "f_exp", "f_hu", "f_hg", "f_tr", "f_trc", "f_y"])
        C.xn = sb("xn", [P, TJ, D])
        xT = sb("xT", [P, KD, L])
        wr = sb("wr", [P, KD, NS])
        U = sb("U", [P, KD, NS * R])
        V = sb("V", [P, KD, D])
        attr = sb("attr", [P, NS, AD])
        wa = sb("wa", [P, AD])
        aw = sb("aw", [P, NS])
        iota = sb("iota", [P, NS])
        sc = sb("sc", [P, TJ, NS])
        top = sb("top", [P, TJ, 8])
        idx = sb("idx", [P, TJ, 8], U32)
        idxf = sb("idxf", [P, TJ, 2])
        sel = sb("sel", [P, TJ, NS])
        e = sb("e", [P, TJ, NS])
        nmx = sb("nmx", [P, TJ])
        sm = sb("sm", [P, TJ])
        gs = sb("gs", [P, TJ])
        gate = sb("gate", [P, TJ])
        hg = sb("hg", [P, TJ, NS * R])
        hgT = sb("hgT", [P, KD, L])
        S.fresh()
        load_all(nc, S, [(wr[:, :, :], rows(W["L0_ffn_Wr"])), (U[:, :, :], rows(W["L0_ffn_U"])),
                         (V[:, :, :], rows(W["L0_ffn_V"])),
                         (attr[:, :, :].rearrange("p s a -> p (s a)"), everywhere(W["L0_ffn_attr"].rearrange("s a -> (s a)"))),
                         (wa[:, :], everywhere(W["L0_ffn_Wa"].rearrange("o a -> (o a)"))),
                         (iota[:, :], everywhere(W["c_iota"]))], "f_ld")
        with nc.Block() as blk:
            @blk.vector
            def _(dve):
                dve.tensor_tensor(attr[:, :, :], attr[:, :, :], wa[:, :].unsqueeze(1).broadcast_to((P, NS, AD)), ALU.mult)
                dve.drain()
                dve.tensor_reduce(aw[:, :], attr[:, :, :], AX_X, ALU.add)
                dve.drain().then_inc(S["f_aw"], 1)

            @blk.scalar
            def _(act):
                act.wait_ge(S["f_aw"], 1)
                act.activation(aw[:, :], aw[:, :], ACT.Sigmoid)
        with nc.Fori(0, B) as b:
            Sb.fresh()
            layernorm_T(nc, C, Sb, b, xT)
            with nc.Block() as blk:
                @blk.tensor
                def _(pe):
                    for j in range(TJ):
                        for k in range(KD):
                            mm = pe.matmul(ps[:, 0, NS * j:NS * j + NS], xT[:, k, P * j:P * j + P], wr[:, k, :],
                                           start=(k == 0), stop=(k == KD - 1))
                    mm.then_inc(Sb["f_sc"], 1)
                    for j in range(TJ):
                        for k in range(KD):
                            mm = pe.matmul(ps[:, 4 + j, :], xT[:, k, P * j:P * j + P], U[:, k, :],
                                           start=(k == 0), stop=(k == KD - 1))
                        mm.then_inc(Sb["f_hu"], 1)
                    pe.wait_ge(Sb["f_hg"], TJ)
                    for k in range(KD):
                        for j in range(TJ):
                            mm = pe.transpose(ps[:, k, P * j:P * j + P], hg[:, j, P * k:P * k + P], ident[:, :])
                        mm.then_inc(Sb["f_tr"], 1)
                    pe.wait_ge(Sb["f_trc"], KD)
                    for j in range(TJ):
                        for k in range(KD):
                            mm = pe.matmul(ps[:, 4 + j, :], hgT[:, k, P * j:P * j + P], V[:, k, :],
                                           start=(k == 0), stop=(k == KD - 1))
                        mm.then_inc(Sb["f_y"], 1)

                @blk.scalar
                def _(act):
                    act.wait_ge(Sb["f_sc"], 1)
                    act.copy(sc[:, :, :], ps[:, 0, 0:TJ * NS].rearrange("p (j s) -> p j s", s=NS)
                             ).then_inc(Sb["f_scc"], 1)
                    act.wait_ge(Sb["f_max"], 1)
                    for j in range(TJ):
                        act.activation(e[:, j, :], sc[:, j, :], ACT.Exp, bias=nmx[:, j:j + 1], accum_out=sm[:, j:j + 1])
                    act.drain().then_inc(Sb["f_exp"], 1)
                    for k in range(KD):
                        act.wait_ge(Sb["f_tr"], k + 1)
                        act.copy(hgT[:, k, :], ps[:, k, :]).then_inc(Sb["f_trc"], 1)

                @blk.vector
                def _(dve):
                    dve.wait_ge(Sb["f_scc"], 1)
                    dve.tensor_reduce(nmx[:, :], sc[:, :, :], AX_X, ALU.max, negate=True)
                    dve.drain().then_inc(Sb["f_max"], 1)
                    for j in range(TJ):
                        top_two(dve, sc[:, j, :], top[:, j, :], idx[:, j, :], idxf[:, j, :], iota, sel[:, j, :], NS)
                    dve.wait_ge(Sb["f_exp"], 1)
                    dve.reciprocal(sm[:, :], sm[:, :])
                    dve.drain()
                    dve.tensor_tensor(e[:, :, :], e[:, :, :], sm[:, :].unsqueeze(2).broadcast_to((P, TJ, NS)), ALU.mult)
                    dve.drain()
                    dve.tensor_tensor(e[:, :, :], e[:, :, :], sel[:, :, :], ALU.mult)
                    dve.drain()
                    dve.tensor_reduce(gs[:, :], e[:, :, :], AX_X, ALU.add)
                    dve.drain()
                    dve.tensor_scalar(gs[:, :], gs[:, :], 1e-8, None, ALU.add)
                    dve.drain()
                    dve.reciprocal(gs[:, :], gs[:, :])
                    dve.drain()
                    dve.tensor_tensor(e[:, :, :], e[:, :, :], gs[:, :].unsqueeze(2).broadcast_to((P, TJ, NS)), ALU.mult)
                    dve.drain()
                    for j in range(TJ):
                        dve.wait_ge(Sb["f_hu"], j + 1)
                        dve.tensor_tensor(hg[:, j, :].rearrange("p (s r) -> p s r", r=R),
                                          ps[:, 4 + j, :].rearrange("p (s r) -> p s r", r=R),
                                          e[:, j, :].unsqueeze(2).broadcast_to((P, NS, R)), ALU.mult
                                          ).then_inc(Sb["f_hg"], 1)
                    dve.tensor_tensor(sel[:, :, :], e[:, :, :], aw[:, :].unsqueeze(1).broadcast_to((P, TJ, NS)), ALU.mult)
                    dve.drain()
                    dve.tensor_reduce(gate[:, :], sel[:, :, :], AX_X, ALU.add)
                    dve.drain()
                    dve.tensor_scalar(gate[:, :], gate[:, :], 0.2, 0.9, ALU.mult, ALU.add)
                    dve.drain()
                    for j in range(TJ):
                        dve.wait_ge(Sb["f_y"], j + 1)
                        xj = x[:, bass.ds(TJ * b + j, 1), :].rearrange("p a d -> p (a d)")
                        dve.scalar_tensor_tensor(xj, ps[:, 4 + j, :], gate[:, j:j + 1], xj, ALU.mult, ALU.add)


def delta_attention(nc, C, W):
    LAST = len(LEVELS) - 1
    H, NCH = 16, NT
    TOK = B * L
    x, ps, ident = C.x, C.ps, C.ident
    with ExitStack() as ctx:
        def sb(name, shape, dt=F32):
            return ctx.enter_context(nc.sbuf_tensor("d_" + name, shape, dt))

        S = Signals(nc, ctx, ["d_ld", "d_scr"] + LN_SIGNALS)
        Sp = Signals(nc, ctx, ["p_wo", "p_max", "p_ln", "p_q2", "p_vt", "p_raw", "p_pad", "p_conv", "p_silu", "p_sq", "p_ss", "p_nk", "p_gate",
                               "p_abs", "p_sp", "p_sum", "p_dec", "p_go", "p_th", "p_beta", "p_kn", "p_vb", "p_dg",
                               "p_dgm"])
        Sl = Signals(nc, ctx, ["l_pairs", "l_masked", "l_scaled", "l_y", "l_yc", "l_upd", "l_new", "l_tr", "l_trc",
                               "l_kt", "l_next"])
        Sr = Signals(nc, ctx, ["r_ks", "r_w", "r_u", "r_uc", "r_o", "r_oc", "r_st", "r_new", "r_ms", "r_var",
                               "r_rs", "r_ot", "r_og", "r_y", "r_yx", "r_nxt"])
        xT = sb("xT", [P, KD, TOK])
        f1T = sb("f1T", [P, TOK])
        g1T = sb("g1T", [P, TOK])
        beta_t = sb("beta_t", [P, NCH, H])
        negA = sb("negA", [P, H])
        dtb = sb("dtb", [P, H])
        cw = sb("cw", [P, 3, H, 4])
        onw = sb("onw", [P, 1])
        load_all(nc, S, [
            (negA[:, :], everywhere(W["L1_attn_A_log"].rearrange("a b h d -> (a b h d)"))),
            (dtb[:, :], W["L1_attn_dt_bias"]),
            (cw[:, 0], rows(W["L1_attn_conv_q_w"])),
            (cw[:, 1], rows(W["L1_attn_conv_k_w"])),
            (cw[:, 2], rows(W["L1_attn_conv_v_w"])),
            (onw[:, :], W["L1_attn_o_norm_w"]),
        ], "d_ld")

        with ExitStack() as pre:
            xTb = pre.enter_context(nc.sbuf_tensor("d_xTb", [P, KD, L], F32))
            C.xn = pre.enter_context(nc.sbuf_tensor("d_xn", [P, TJ, D], F32))
            wfa = pre.enter_context(nc.sbuf_tensor("d_wfa", [P, KD, P], F32))
            wga = pre.enter_context(nc.sbuf_tensor("d_wga", [P, KD, P], F32))
            wb = pre.enter_context(nc.sbuf_tensor("d_wb", [P, KD, H], F32))
            betaT = pre.enter_context(nc.sbuf_tensor("d_betaT", [H, TOK], F32))
            S.fresh()
            load_all(nc, S, [(wfa[:, :, :], rows(W["L1_attn_Wfa"])), (wga[:, :, :], rows(W["L1_attn_Wga"])),
                             (wb[:, :, :], rows(W["L1_attn_Wb"]))], "d_ld")
            with nc.Fori(0, B) as b:
                S.fresh()
                layernorm_T(nc, C, S, b, xTb)
                with nc.Block() as blk:
                    @blk.tensor
                    def _(pe):
                        for n, (w, m) in enumerate(((wfa, P), (wga, P), (wb, H))):
                            for k in range(KD):
                                mm = pe.matmul(ps[0:m, n, :], w[:, k, :], xTb[:, k, :],
                                               start=(k == 0), stop=(k == KD - 1))
                        for j in range(TJ):
                            for k in range(KD):
                                mm = pe.matmul(ps[:, 3, H * j:H * j + H], xTb[:, k, P * j:P * j + P], wb[:, k, :],
                                               start=(k == 0), stop=(k == KD - 1))
                        mm.then_inc(S["ln_tr"], 1)

                    @blk.scalar
                    def _(act):
                        act.wait_ge(S["ln_tr"], KD + 1)
                        act.copy(f1T[:, bass.ds(L * b, L)], ps[:, 0, :])
                        act.copy(g1T[:, bass.ds(L * b, L)], ps[:, 1, :])
                        act.activation(betaT[:, bass.ds(L * b, L)], ps[0:H, 2, :], ACT.Sigmoid)
                        act.activation(beta_t[:, bass.ds(TJ * b, TJ), :],
                                       ps[:, 3, 0:TJ * H].rearrange("p (j h) -> p j h", h=H), ACT.Sigmoid)

                    @blk.vector
                    def _(dve):
                        for k in range(KD):
                            dve.tensor_copy(xT[:, k, bass.ds(L * b, L)], xTb[:, k, :])
            S.fresh()
            with nc.Block() as blk:
                @blk.sync
                def _(sp):
                    sp.dma_start(C.scratch[0:H, :], betaT[:, :]).then_inc(S["d_scr"], 16)
                    sp.wait_ge(S["d_scr"], 16)

                @blk.scalar
                def _(act):
                    act.activation(negA[:, :], negA[:, :], ACT.Exp)
                    act.drain().then_inc(S["ln_var"], 1)

                @blk.vector
                def _(dve):
                    dve.wait_ge(S["ln_var"], 1)
                    dve.tensor_scalar(negA[:, :], negA[:, :], -1.0, None, ALU.mult)

        wqkv = sb("wqkv", [P, 3, KD, P])
        wfg = sb("wfg", [P, 2, P])
        wo = sb("wo", [P, D])
        raw = sb("raw", [P, 3, 3 + L])
        conv = sb("conv", [P, 3, L])
        KQ = sb("KQ", [P, 2, TOK])
        kS = sb("kS", [P, TOK])
        vb = sb("vb", [P, TOK])
        sg = sb("sg", [P, TOK])
        dec = sb("dec", [P, TOK])
        N_ = sb("N", [P, NCH, P])
        T_ = sb("T", [P, NCH, P])
        A_ = sb("A", [P, NCH, P])
        M_ = sb("M", [P, NCH, P])
        Y_ = sb("Y", [P, NCH, P])
        dec2 = sb("dec2", [P, TOK // 2])
        maskf = sb("maskf", [P, 7, 64])
        masku = sb("masku", [P, 7, 64], U32)
        rowm = sb("rowm", [P, 7])
        sumq = sb("sumq", [P, NCH])
        fac = sb("fac", [P, 3, NCH])

        def load_head(queue, h, done):
            for n, w in enumerate(("Wq", "Wk", "Wv")):
                queue.dma_start(wqkv[:, n], rows(W["L1_attn_" + w])[:, :, bass.ds(P * h, P)]).then_inc(done, 16)
            for n, w in enumerate(("Wfb", "Wgb")):
                queue.dma_start(wfg[:, n, :], W["L1_attn_" + w][:, bass.ds(P * h, P)]).then_inc(done, 16)

        S.fresh()
        load_all(nc, S, [(maskf[:, :, :], W["c_mask"]), (masku[:, :, :], W["c_masku"]), (rowm[:, :], W["c_rowm"])],
                 "d_ld")
        S.fresh()
        with nc.Block() as blk:
            @blk.sync
            def _(sp):
                load_head(sp, H - 1, S["d_ld"])
                sp.wait_ge(S["d_ld"], 5 * 16)

            @blk.vector
            def _(dve):
                dve.memset(raw[:, :, 0:3], 0.0)
        with nc.Fori(0, H) as h:
            Sp.fresh()
            with nc.Block() as blk:
                UNITS = [(n, b) for n in (1, 0, 2) for b in range(B)]
                LU = len(UNITS)

                def seq(t, b):
                    return (t if len(t.shape) == 2 else t[:, :, :].rearrange("p c s -> p (c s)"))[
                        :, L * b:L * b + L]

                @blk.sync
                def _(sp):
                    sp.dma_start(M_[:, :, :].rearrange("p c s -> p (c s)"),
                                 C.scratch[bass.ds(h, 1), :].broadcast_to((P, TOK))).then_inc(Sp["p_beta"], 16)
                    sp.dma_start(wo[:, :], W["L1_attn_Wo"][bass.ds(P * h, P), :]).then_inc(Sp["p_wo"], 16)
                    sp.wait_ge(Sp["p_beta"], 16)
                    sp.wait_ge(Sp["p_wo"], 16)

                @blk.tensor
                def _(pe):
                    def project(u):
                        n, b = UNITS[u]
                        if u >= 3:
                            pe.wait_ge(Sp["p_raw"], u - 2)
                        for k in range(KD):
                            mm = pe.matmul(ps[:, u % 3, :], wqkv[:, n, k, :], xT[:, k, L * b:L * b + L],
                                           start=(k == 0), stop=(k == KD - 1))
                        mm.then_inc(Sp["p_pad"], 1)

                    def out_gate(b):
                        if b >= 1:
                            pe.wait_ge(Sp["p_th"], b)
                        pe.matmul(ps[:, 3, :], wfg[:, 1, :], g1T[:, L * b:L * b + L],
                                  start=True, stop=True).then_inc(Sp["p_go"], 1)

                    def k_squares(b):
                        pe.wait_ge(Sp["p_sq"], b + 1)
                        pe.wait_ge(Sp["p_max"], b + 1)
                        pe.matmul(ps[:, 4 + b, :], C.ones[:, :], seq(N_, b), start=True, stop=True
                                  ).then_inc(Sp["p_ss"], 1)

                    def diagonal(b):
                        pe.wait_ge(Sp["p_kn"], b + 1)
                        pe.wait_ge(Sp["p_silu"], 2 * B)
                        pe.wait_ge(Sp["p_ln"], b + 1)
                        for c in range(TJ):
                            a = P * (TJ * b + c)
                            mm = pe.matmul(ps[:, 4 + b, P * c:P * c + P], kS[:, a:a + P], KQ[:, 1, a:a + P],
                                           start=True, stop=True)
                        mm.then_inc(Sp["p_dg"], 1)

                    def v_turned(b):
                        pe.wait_ge(Sp["p_silu"], 2 * B + b + 1)
                        if b < 3:
                            pe.wait_ge(Sp["p_raw"], LU - 2 + b)
                        else:
                            pe.wait_ge(Sp["p_q2"], B + 1)
                        for c in range(TJ):
                            a = P * (TJ * b + c)
                            mm = pe.transpose(ps[:, b, P * c:P * c + P], vb[:, a:a + P], ident[:, :])
                        mm.then_inc(Sp["p_vt"], 1)

                    for b in range(B):
                        pe.matmul(ps[:, 4 + b, :], wfg[:, 0, :], f1T[:, L * b:L * b + L],
                                  start=True, stop=True).then_inc(Sp["p_gate"], 1)
                    for u in range(LU):
                        project(u)
                        if B <= u < 2 * B:
                            out_gate(u - B)
                        if u == B + 2:
                            for b in range(B):
                                k_squares(b)
                        if u == 2 * B + 1:
                            pe.wait_ge(Sp["p_q2"], B)
                            pe.wait_ge(Sp["p_th"], B)
                            for c in range(NCH):
                                mm = pe.matmul(ps[:, 3, 2 * c:2 * c + 2], T_[:, c, :], C.ones[:, 0:2],
                                               start=True, stop=True)
                            mm.then_inc(Sp["p_ss"], 1)
                        if u >= LU - 2:
                            for b in (0, 1) if u == LU - 2 else (2, 3):
                                diagonal(b)
                    for b in range(B):
                        v_turned(b)

                @blk.scalar
                def _(act):
                    def copy_raw(u):
                        act.wait_ge(Sp["p_pad"], u + 1)
                        if u >= 3:
                            act.wait_ge(Sp["p_conv"], u - 2)
                        act.copy(raw[:, u % 3, 3:3 + L], ps[:, u % 3, :]).then_inc(Sp["p_raw"], 1)

                    def silu(u):
                        n, b = UNITS[u]
                        dst = (KQ[:, 1, L * b:L * b + L], seq(kS, b), seq(vb, b))[n]
                        act.wait_ge(Sp["p_conv"], u + 1)
                        act.activation(dst, conv[:, u % 3, :], ACT.Silu)
                        act.drain().then_inc(Sp["p_silu"], 1)
                        if n == 1:
                            act.activation(seq(N_, b), dst, ACT.Square).then_inc(Sp["p_sq"], 1)
                        if n == 0:
                            act.activation(seq(T_, b), dst, ACT.Square).then_inc(Sp["p_q2"], 1)

                    for b in range(B):
                        act.wait_ge(Sp["p_gate"], b + 1)
                        act.activation(seq(dec, b), ps[:, 4 + b, :], ACT.Abs, bias=dtb[:, bass.ds(h, 1)]
                                       ).then_inc(Sp["p_abs"], 1)
                    act.drain()
                    act.activation(dec[:, :], dec[:, :], ACT.Exp, scale=-1.0)
                    copy_raw(0)
                    act.drain()
                    for b in range(B):
                        act.activation(seq(dec, b), seq(dec, b), ACT.Ln, bias=1.0).then_inc(Sp["p_sp"], 1)
                    copy_raw(1)
                    for b in range(B):
                        act.wait_ge(Sp["p_sum"], b + 1)
                        act.activation(seq(dec, b), seq(dec, b), ACT.Exp, scale=negA[:, bass.ds(h, 1)]
                                       ).then_inc(Sp["p_dec"], 1)
                    silu(0)
                    for u in range(2, LU):
                        copy_raw(u)
                        silu(u - 1)
                        if B <= u < 2 * B:
                            b = u - B
                            act.wait_ge(Sp["p_go"], b + 1)
                            act.activation(sg[:, L * b:L * b + L], ps[:, 3, :], ACT.Tanh, scale=0.5
                                           ).then_inc(Sp["p_th"], 1)
                        if u == 2 * B:
                            for b in range(B):
                                act.wait_ge(Sp["p_ss"], b + 1)
                                act.activation(seq(Y_, b), ps[:, 4 + b, :], ACT.Ln, bias=C.eps6[:, 0:1]
                                               ).then_inc(Sp["p_ln"], 1)
                            act.drain()
                            for b in range(B):
                                act.activation(seq(Y_, b), seq(Y_, b), ACT.Exp, scale=-0.5
                                               ).then_inc(Sp["p_nk"], 1)
                    silu(LU - 1)
                    act.wait_ge(Sp["p_ss"], B + 1)
                    act.copy(sumq[:, :], ps[:, 3, 0:2 * NCH].rearrange("p (c a) -> p c a", a=2)[:, :, 0]
                             ).then_inc(Sp["p_q2"], 1)
                    for b in range(B):
                        act.wait_ge(Sp["p_vt"], b + 1)
                        for c in range(TJ):
                            a = P * (TJ * b + c)
                            act.activation(vb[:, a:a + P], ps[:, b, P * c:P * c + P], ACT.Copy,
                                           scale=beta_t[:, TJ * b + c, bass.ds(h, 1)])

                @blk.vector
                def _(dve):
                    def convolve(u):
                        n, b = UNITS[u]
                        dve.wait_ge(Sp["p_raw"], u + 1)
                        if u >= 3:
                            dve.wait_ge(Sp["p_silu"], u - 2)
                        out = conv[:, u % 3, :]
                        dve.tensor_scalar(out, raw[:, u % 3, 3:3 + L], cw[:, n, bass.ds(h, 1), 3], None, ALU.mult)
                        for t in range(3):
                            dve.drain()
                            dve.scalar_tensor_tensor(out, raw[:, u % 3, t:t + L], cw[:, n, bass.ds(h, 1), t], out,
                                                     ALU.mult, ALU.add)
                        dve.drain().then_inc(Sp["p_conv"], 1)

                    for b in range(B):
                        dve.wait_ge(Sp["p_abs"], b + 1)
                        dve.tensor_scalar(seq(A_, b), ps[:, 4 + b, :], dtb[:, bass.ds(h, 1)], 0.0, ALU.add, ALU.max
                                          ).then_inc(Sp["p_max"], 1)
                    convolve(0)
                    for b in range(B):
                        dve.wait_ge(Sp["p_sp"], b + 1)
                        dve.tensor_tensor(seq(dec, b), seq(A_, b), seq(dec, b), ALU.add).then_inc(Sp["p_sum"], 1)
                    for u in range(1, LU):
                        convolve(u)
                    for b in range(B):
                        dve.wait_ge(Sp["p_dg"], b + 1)
                        dve.tensor_tensor(A_[:, TJ * b:TJ * b + TJ, :],
                                          ps[:, 4 + b, :].rearrange("p (c s) -> p c s", s=P),
                                          ident[:, :].unsqueeze(1).broadcast_to((P, TJ, P)), ALU.mult)

                @blk.gpsimd
                def _(pool):
                    pool.wait_ge(Sp["p_beta"], 16)
                    for b in range(B):
                        pool.wait_ge(Sp["p_dec"], b + 1)
                        pool.tensor_tensor(seq(M_, b), seq(M_, b), seq(dec, b), ALU.mult)
                    pool.wait_ge(Sp["p_th"], B)
                    pool.tensor_scalar(sg[:, :], sg[:, :], 0.5, 0.5, ALU.mult, ALU.add)
                    pool.wait_ge(Sp["p_sq"], B)
                    for b in range(B):
                        pool.wait_ge(Sp["p_nk"], b + 1)
                        pool.tensor_tensor(seq(kS, b), seq(kS, b), seq(Y_, b), ALU.mult)
                        pool.drain().then_inc(Sp["p_kn"], 1)
                    for b in range(B):
                        pool.tensor_tensor(KQ[:, 0, L * b:L * b + L], seq(kS, b), seq(M_, b), ALU.mult)
                    pool.drain()
                    pool.memset(M_[:, :, :], 0.0)
                    pool.memset(Y_[:, :, :], 0.0)
                    pool.wait_ge(Sp["p_q2"], B)
                    for b in range(B):
                        pool.wait_ge(Sp["p_dg"], b + 1)
                        pool.tensor_tensor(KQ[:, 1, L * b:L * b + L], KQ[:, 1, L * b:L * b + L], seq(dec, b),
                                           ALU.mult)

            Sl.fresh()
            with nc.Block() as blk:
                def second(ap, w):
                    return ap.rearrange("p c (n a r) -> p c n a r", a=2, r=w)[:, :, :, 1, :]

                def packed(ap, w):
                    return ap.rearrange("p c (n r) -> p c n r", r=w)

                @blk.sync
                def _(sp):
                    load_head(sp, h, Sl["l_next"])
                    sp.wait_ge(Sl["l_next"], 5 * 16)

                def blocks(w):
                    return range(0, P, 2 * w)

                def of(t, b):
                    return t[:, TJ * b:TJ * b + TJ, :].rearrange("p c s -> p (c s)")

                @blk.tensor
                def _(pe):
                    def strips(w):
                        g = P // 2 if 4 <= w <= 16 else P
                        return [slice(n, n + g) for n in range(0, P, g)]

                    def pairs(l, w):
                        for b in range(B):
                            if l >= 1:
                                pe.wait_ge(Sl["l_scaled"], B * (l - 1) + b + 1)
                                pe.wait_ge(Sl["l_masked"], B * (l - 1) + b + 1)
                            if l >= 3:
                                pe.wait_ge(Sl["l_trc"], B * (l - 3) + b + 1)
                            for c in range(TJ):
                                cc = P * (TJ * b + c)
                                bank = ps[:, b, P * c:P * c + P].rearrange("p (q s) -> p q s", q=2)
                                for r in strips(w):
                                    t2 = KQ[:, :, cc + r.start:cc + r.stop].rearrange(
                                        "p q (n a r) -> p q n a r", a=2, r=w)[:, :, :, 1, :]
                                    mm = pe.matmul(bank[r, :, r.start // 2:r.stop // 2],
                                                   kS[:, cc + r.start:cc + r.stop], t2, start=True, stop=True)
                            mm.then_inc(Sl["l_pairs"], 1)

                    pairs(0, LEVELS[0])
                    for b in range(B):
                        pe.wait_ge(Sl["l_masked"], b + 1)
                        for c in range(TJ):
                            mm = pe.transpose(ps[:, 4 + b, P * c:P * c + P], M_[:, TJ * b + c, :], ident[:, :])
                        mm.then_inc(Sl["l_y"], 1)
                    pairs(1, LEVELS[1])
                    for l in range(1, LAST + 1):
                        w = LEVELS[l]
                        for b in range(B):
                            pe.wait_ge(Sl["l_masked"], B * l + b + 1)
                            pe.wait_ge(Sl["l_new"], B * (l - 1) + b + 1)
                            for c in range(TJ):
                                cc, a = TJ * b + c, P * c
                                if w < 32:
                                    for r in strips(w):
                                        mm = pe.matmul(ps[r, 4 + b, a + r.start:a + r.stop], M_[r, cc, r],
                                                       T_[r, cc, r], start=True, stop=True)
                                else:
                                    for n in blocks(w):
                                        one, two = slice(n, n + w), slice(n + w, n + 2 * w)
                                        mm = pe.matmul(ps[two, 4 + b, a + n:a + n + w], M_[one, cc, two],
                                                       T_[one, cc, one], start=True, stop=True)
                            mm.then_inc(Sl["l_y"], 1)
                        if l >= 2:
                            for b in range(B):
                                for c in range(TJ):
                                    mm = pe.transpose(ps[:, b, P * c:P * c + P], T_[:, TJ * b + c, :], ident[:, :])
                                mm.then_inc(Sl["l_tr"], 1)
                        if l < LAST:
                            pairs(l + 1, LEVELS[l + 1])
                        else:
                            for b in range(B):
                                pe.wait_ge(Sl["l_scaled"], B * l + b + 1)
                                pe.wait_ge(Sl["l_trc"], B * (l - 2) + b + 1)
                                for c in range(TJ):
                                    cc = TJ * b + c
                                    mm = pe.transpose(ps[:, b, P * c:P * c + P], kS[:, P * cc:P * cc + P],
                                                      ident[:, :])
                                mm.then_inc(Sl["l_kt"], 1)
                        for b in range(B):
                            pe.wait_ge(Sl["l_yc"], B * (l - 1) + b + 1)
                            if l >= 2:
                                pe.wait_ge(Sl["l_trc"], B * (l - 2) + b + 1)
                            for c in range(TJ):
                                cc, a = TJ * b + c, P * c
                                if w < 32:
                                    for r in strips(w):
                                        mm = pe.matmul(ps[r, 4 + b, a + r.start:a + r.stop], N_[r, cc, r],
                                                       Y_[r, cc, r], start=True, stop=True)
                                elif l < LAST:
                                    for n in blocks(w):
                                        one, two = slice(n, n + w), slice(n + w, n + 2 * w)
                                        mm = pe.matmul(ps[two, 4 + b, a + n:a + n + w], N_[two, cc, two],
                                                       Y_[two, cc, one], start=True, stop=True)
                                else:
                                    mm = pe.matmul(ps[0:w, 4 + b, a + w:a + 2 * w], Y_[w:, cc, 0:w],
                                                   N_[w:, cc, w:], start=True, stop=True)
                            mm.then_inc(Sl["l_upd"], 1)

                @blk.vector
                def _(dve):
                    def mask(l, w):
                        for b in range(B):
                            cs = slice(TJ * b, TJ * b + TJ)
                            bank = ps[:, b, :].rearrange("p (c q s) -> p c q s", c=TJ, q=2)
                            dve.wait_ge(Sl["l_pairs"], B * l + b + 1)
                            if l >= 1:
                                dve.wait_ge(Sl["l_y"], B * (l - 1) + b + 1)
                            dve.tensor_tensor(second(M_[:, cs, :], w), packed(bank[:, :, 0, :], w),
                                              packed(maskf[:, l, :].unsqueeze(1).broadcast_to((P, TJ, 64)), w),
                                              ALU.mult)
                            dve.copy_predicated(second(A_[:, cs, :], w),
                                                packed(masku[:, l, :].unsqueeze(1).broadcast_to((P, TJ, 64)), w),
                                                packed(bank[:, :, 1, :], w)).then_inc(Sl["l_masked"], 1)

                    mask(0, LEVELS[0])
                    dve.drain()
                    eye = ident[:, :].unsqueeze(1).broadcast_to((P, TJ, P))
                    for b in range(B):
                        cs = slice(TJ * b, TJ * b + TJ)
                        dve.tensor_tensor(N_[:, cs, :], eye, M_[:, cs, :], ALU.subtract)
                        dve.wait_ge(Sl["l_y"], b + 1)
                        dve.tensor_tensor(T_[:, cs, :], eye, ps[:, 4 + b, :].rearrange("p (c s) -> p c s", c=TJ),
                                          ALU.subtract).then_inc(Sl["l_new"], 1)
                    dve.drain()
                    mask(1, LEVELS[1])
                    for l in range(1, LAST + 1):
                        w = LEVELS[l]
                        if l < LAST:
                            dve.drain()
                            mask(l + 1, LEVELS[l + 1])
                        for b in range(B):
                            cs = slice(TJ * b, TJ * b + TJ)
                            bank = ps[:, 4 + b, :].rearrange("p (c s) -> p c s", c=TJ)
                            dve.wait_ge(Sl["l_upd"], B * (l - 1) + b + 1)
                            if w < 32:
                                Tf = halves(of(T_, b), w)[0]
                                op = dve.tensor_tensor(Tf, Tf, halves(ps[:, 4 + b, :], w)[0], ALU.subtract)
                            elif l < LAST:
                                for n in blocks(w):
                                    two = slice(n + w, n + 2 * w)
                                    op = dve.tensor_scalar(T_[two, cs, n:n + w], bank[two, :, n:n + w], -1.0, None,
                                                           ALU.mult)
                            else:
                                op = dve.tensor_scalar(N_[0:w, cs, w:], bank[0:w, :, w:], -1.0, None, ALU.mult)
                            op.then_inc(Sl["l_new"], 1)
                        dve.drain()

                @blk.scalar
                def _(act):
                    act.activation(fac[:, 2, :], sumq[:, :], ACT.Ln, bias=C.eps6[:, 0:1])
                    act.drain()
                    act.activation(fac[:, 0, :], fac[:, 2, :], ACT.Exp, scale=-0.5, bias=C.lnsd[:, 0:1])
                    for l in range(1, LAST + 1):
                        w = LEVELS[l]
                        for b in range(B):
                            cs = slice(TJ * b, TJ * b + TJ)
                            bank = ps[:, 4 + b, :].rearrange("p (c s) -> p c s", c=TJ)
                            act.wait_ge(Sl["l_y"], B * l + b + 1)
                            if w < 32:
                                op = act.activation(halves(of(Y_, b), w)[0], halves(ps[:, 4 + b, :], w)[0], ACT.Copy,
                                                    scale=rowm[:, l:l + 1])
                            else:
                                for n in blocks(w):
                                    two = slice(n + w, n + 2 * w)
                                    op = act.copy(Y_[two, cs, n:n + w], bank[two, :, n:n + w])
                            op.then_inc(Sl["l_yc"], 1)
                        if l >= 2:
                            h = LEVELS[l - 1]
                            for b in range(B):
                                act.wait_ge(Sl["l_tr"], B * (l - 2) + b + 1)
                                act.copy(halves(of(N_, b), h)[1], halves(ps[:, b, :], h)[1]
                                         ).then_inc(Sl["l_trc"], 1)
                    for b in range(B):
                        act.wait_ge(Sl["l_kt"], b + 1)
                        act.copy(M_[:, TJ * b:TJ * b + TJ, :].rearrange("p c s -> p (c s)"), ps[:, b, :])

                @blk.gpsimd
                def _(pool):
                    src = dec
                    for l, w in enumerate(LEVELS):
                        dst = dec2 if l % 2 == 0 else dec
                        nblk = L // (2 * w)
                        for b in range(B):
                            sl = slice(L * b, L * b + L)
                            n0 = b * 2 * nblk
                            pr = src[:, n0:n0 + 2 * nblk].rearrange("p (n a) -> p n a", a=2)
                            D1, D2 = pr[:, :, 0:1], pr[:, :, 1:2]
                            kq2 = KQ[:, :, sl].rearrange("p q (n a r) -> p q n a r", a=2, r=w)[:, :, :, 1, :]
                            kf = halves(kS[:, sl], w)[0]
                            pool.wait_ge(Sl["l_pairs"], B * l + b + 1)
                            for q in range(2):
                                pool.tensor_tensor(kq2[:, q], kq2[:, q], D1.broadcast_to((P, nblk, w)), ALU.mult)
                            pool.tensor_tensor(kf, kf, D2.broadcast_to((P, nblk, w)), ALU.mult)
                            pool.tensor_tensor(dst[:, b * nblk:b * nblk + nblk], pr[:, :, 0], pr[:, :, 1], ALU.mult)
                            pool.drain().then_inc(Sl["l_scaled"], 1)
                        src = dst
            Dc = dec2 if len(LEVELS) % 2 else dec

            Sr.fresh()
            St = dec[:, 2 * L:2 * L + B * P] if Dc is dec2 else dec2[:, 0:B * P]
            with nc.Block() as blk:
                def W_(b):
                    return conv[:, 0, P * b:P * b + P]

                def U_(b):
                    return conv[:, 1, P * b:P * b + P]

                def tokens(b, c):
                    return slice(P * (TJ * b + c), P * (TJ * b + c) + P)

                @blk.tensor
                def _(pe):
                    def turn(c):
                        for b in range(B):
                            pe.wait_ge(Sr["r_oc"], B * c + b + 1)
                            pe.transpose(ps[:, 4 + b, P:2 * P], Y_[:, TJ * b + c, :], ident[:, :]
                                         ).then_inc(Sr["r_ot"], 1)

                    for c in range(TJ):
                        if c >= 1:
                            for b in range(B):
                                pe.wait_ge(Sr["r_new"], B * (c - 1) + b + 1)
                                pe.matmul(ps[:, b, 0:P], KQ[:, 0, tokens(b, c)], St[:, P * b:P * b + P],
                                          start=True, stop=True).then_inc(Sr["r_ks"], 1)
                            turn(c - 1)
                        for b in range(B):
                            if c >= 1:
                                pe.wait_ge(Sr["r_w"], B * (c - 1) + b + 1)
                            pe.matmul(ps[:, b, P:2 * P], N_[:, TJ * b + c, :], W_(b) if c else vb[:, tokens(b, c)],
                                      start=True, stop=True).then_inc(Sr["r_u"], 1)
                        for b in range(B):
                            cc = TJ * b + c
                            o = ps[:, 4 + b, 0:P]
                            if c >= 1:
                                pe.wait_ge(Sr["r_og"], B * (c - 1) + b + 1)
                                pe.matmul(o, KQ[:, 1, tokens(b, c)], St[:, P * b:P * b + P],
                                          start=True, stop=False)
                            pe.wait_ge(Sr["r_uc"], B * c + b + 1)
                            if c < TJ - 1:
                                pe.matmul(ps[:, b, 2 * P:3 * P], M_[:, cc, :], U_(b), start=True, stop=True
                                          ).then_inc(Sr["r_st"], 1)
                            pe.matmul(o, A_[:, cc, :], U_(b), start=(c == 0), stop=True).then_inc(Sr["r_o"], 1)
                    turn(TJ - 1)
                    for n in range(NCH):
                        if n == 0:
                            pe.wait_ge(Sr["r_og"], NCH)
                        if n >= 8:
                            pe.wait_ge(Sr["r_yx"], n - 7)
                        pe.matmul(ps[:, n % 8, :], kS[:, P * n:P * n + P], wo[:, :], start=True, stop=True
                                  ).then_inc(Sr["r_y"], 1)

                @blk.vector
                def _(dve):
                    def gate(c):
                        for b in range(B):
                            t = tokens(b, c)
                            dve.wait_ge(Sr["r_ot"], B * c + b + 1)
                            dve.scalar_tensor_tensor(kS[:, t], ps[:, 4 + b, P:2 * P], onw[:, 0:1], sg[:, t],
                                                     ALU.mult, ALU.mult).then_inc(Sr["r_og"], 1)

                    for c in range(TJ):
                        if c >= 1:
                            for b in range(B):
                                dve.wait_ge(Sr["r_u"], B * (c - 1) + b + 1)
                                dve.wait_ge(Sr["r_ks"], B * (c - 1) + b + 1)
                                dve.tensor_tensor(W_(b), vb[:, tokens(b, c)], ps[:, b, 0:P],
                                                  ALU.subtract).then_inc(Sr["r_w"], 1)
                            gate(c - 1)
                        if c < TJ - 1:
                            for b in range(B):
                                cc = TJ * b + c
                                s = St[:, P * b:P * b + P]
                                dve.wait_ge(Sr["r_st"], B * c + b + 1)
                                if c >= 1:
                                    dve.scalar_tensor_tensor(s, s, Dc[:, cc:cc + 1], ps[:, b, 2 * P:3 * P],
                                                             ALU.mult, ALU.add).then_inc(Sr["r_new"], 1)
                                else:
                                    dve.tensor_copy(s, ps[:, b, 2 * P:3 * P]).then_inc(Sr["r_new"], 1)
                    gate(TJ - 1)
                    dve.wait_ge(Sr["r_ms"], 1)
                    dve.tensor_tensor(fac[:, 1, :], fac[:, 1, :], fac[:, 0, :], ALU.mult)
                    dve.drain()
                    dve.tensor_tensor(fac[:, 1, :], fac[:, 1, :], fac[:, 0, :], ALU.mult)
                    dve.drain().then_inc(Sr["r_var"], 1)
                    dve.wait_ge(Sr["r_rs"], 1)
                    dve.tensor_tensor(fac[:, 1, :], fac[:, 1, :], fac[:, 0, :], ALU.mult)
                    dve.drain()
                    for n in range(NCH):
                        dve.wait_ge(Sr["r_y"], n + 1)
                        dve.scalar_tensor_tensor(x[:, n, :], ps[:, n % 8, :], fac[:, 1, n:n + 1], x[:, n, :],
                                                 ALU.mult, ALU.add).then_inc(Sr["r_yx"], 1)

                @blk.scalar
                def _(act):
                    for c in range(TJ):
                        for b in range(B):
                            act.wait_ge(Sr["r_u"], B * c + b + 1)
                            if c >= 1:
                                act.wait_ge(Sr["r_o"], B * (c - 1) + b + 1)
                                act.wait_ge(Sr["r_st"], B * (c - 1) + b + 1)
                            act.copy(U_(b), ps[:, b, P:2 * P]).then_inc(Sr["r_uc"], 1)
                        for b in range(B):
                            act.wait_ge(Sr["r_o"], B * c + b + 1)
                            act.copy(Y_[:, TJ * b + c, :], ps[:, 4 + b, 0:P]).then_inc(Sr["r_oc"], 1)
                        act.drain()
                        for b in range(B):
                            cc = TJ * b + c
                            act.activation(A_[:, cc, :], Y_[:, cc, :], ACT.Square, accum_out=fac[:, 1, cc:cc + 1])
                    act.drain().then_inc(Sr["r_ms"], 1)
                    act.wait_ge(Sr["r_var"], 1)
                    act.activation(fac[:, 2, :], fac[:, 1, :], ACT.Ln, scale=1.0 / P, bias=C.eps6[:, 0:1])
                    act.drain()
                    act.activation(fac[:, 1, :], fac[:, 2, :], ACT.Exp, scale=-0.5)
                    act.drain().then_inc(Sr["r_rs"], 1)




def cross_attention(nc, C, W):
    H, HD, DCA, CK, NM = 16, 32, 16, 2, L - 16
    G = TJ * H
    N = TJ * H
    x, ps, ident = C.x, C.ps, C.ident
    with ExitStack() as ctx:
        def sb(name, shape, dt=F32):
            return ctx.enter_context(nc.sbuf_tensor("a_" + name, shape, dt))

        S = Signals(nc, ctx, ["a_ld"])
        Sb = Signals(nc, ctx, LN_SIGNALS + ["a_ctx", "a_q", "a_qb", "a_k", "a_kb", "a_d", "a_sq", "a_rs",
                                            "a_n", "a_tr", "a_trc"])
        Sh = Signals(nc, ctx, ["h_s", "h_max", "h_exp", "h_pt", "h_ptc", "h_o", "h_half", "h_bo", "h_on", "h_ot", "h_otc",
                               "h_y", "h_x"])
        C.xn = sb("xn", [P, TJ, D])
        xT = sb("xT", [P, KD, L])
        wq = sb("wq", [P, KD, D])
        wkv = sb("wkv", [P, CK, 2 * D])
        wdc = sb("wdc", [P, CK, 2 * D])
        wo = sb("wo", [P, KD, D])
        bq = sb("bq", [P, D])
        bkv = sb("bkv", [P, 2 * D])
        bdc = sb("bdc", [P, 2 * D])
        bo = sb("bo", [P, D])
        nw = sb("nw", [P, 6])
        isd = sb("isd", [P, 2])
        cT = sb("cT", [P, CK, L])
        q = sb("q", [P, TJ, D])
        k = sb("k", [P, TJ, D])
        v = sb("v", [P, TJ, D])
        v2 = sb("v2", [P, H, 2 * HD])
        kv3 = sb("kv3", [P, 2 * D])
        sq = sb("sq", [P, TJ, D])
        mom = sb("mom", [P, 2, 2, G])
        qT = sb("qT", [P, 4, KD, L])
        kT = sb("kT", [P, KD, L])
        nm = sb("nm", [P, 2, H, 2])
        sm = sb("sm", [P, 2, 2, H])
        pr = sb("pr", [P, 3, L])
        pT = sb("pT", [P, 2, L])
        o = sb("o", [P, TJ, D])
        S.fresh()
        load_all(nc, S, [
            (wq[:, :, :], rows(W["L1_xattn_Wq"])), (wo[:, :, :], rows(W["L1_xattn_Wo"])),
            (wkv[:, :, 0:D], rows(W["L1_xattn_Wk"])), (wkv[:, :, D:2 * D], rows(W["L1_xattn_Wv"])),
            (wdc[:, :, :], rows(W["L1_xattn_Wkv_dca"])), (bq[:, :], everywhere(W["L1_xattn_bq"])),
            (bkv[:, 0:D], everywhere(W["L1_xattn_bk"])), (bkv[:, D:2 * D], everywhere(W["L1_xattn_bv"])),
            (bdc[:, :], everywhere(W["L1_xattn_bkv_dca"])), (bo[:, :], everywhere(W["L1_xattn_bo"])),
            (isd[:, :], W["c_isd"])]
            + [(nw[HD * i:HD * i + HD, n:n + 1], W["L1_xattn_" + name])
               for n, name in enumerate(("qn_w", "qn_b", "kn_w", "kn_b", "kn_dca_w", "kn_dca_b"))
               for i in range(4)], "a_ld")
        with nc.Block() as blk:
            @blk.vector
            def _(dve):
                dve.memset(qT[:, :, :, :], 0.0)
        with nc.Fori(0, B) as b:
            Sb.fresh()
            layernorm_T(nc, C, Sb, b, xT)
            with nc.Block() as blk:
                def heads(ap):
                    return ap.rearrange("p j (h d) -> p (j h) d", d=HD)

                @blk.sync
                def _(sp):
                    sp.dma_start(cT[:, :, :], W["ctx_1024"].rearrange("b (k p) n -> b p k n", p=P)[
                        bass.ds(b, 1)].rearrange("a p k n -> (a p) k n")).then_inc(Sb["a_ctx"], 16)

                @blk.tensor
                def _(pe):
                    for j in range(TJ):
                        for kk in range(KD):
                            mm = pe.matmul(ps[:, j, :], xT[:, kk, P * j:P * j + P], wq[:, kk, :],
                                           start=(kk == 0), stop=(kk == KD - 1))
                        mm.then_inc(Sb["a_q"], 1)
                    pe.wait_ge(Sb["a_ctx"], 16)
                    for j in range(TJ):
                        if j >= 2:
                            pe.wait_ge(Sb["a_kb"], j - 1)
                        for n in range(2):
                            for kk in range(CK):
                                mm = pe.matmul(ps[:, 4 + 2 * (j % 2) + n, :], cT[:, kk, P * j:P * j + P],
                                               wkv[:, kk, D * n:D * n + D], start=(kk == 0), stop=(kk == CK - 1))
                        mm.then_inc(Sb["a_k"], 1)
                    pe.wait_ge(Sb["a_kb"], TJ - 1)
                    for n in range(2):
                        for kk in range(CK):
                            mm = pe.matmul(ps[:, 4 + n, :], cT[:, kk, P * (TJ - 1):L], wdc[:, kk, D * n:D * n + D],
                                           start=(kk == 0), stop=(kk == CK - 1))
                    mm.then_inc(Sb["a_d"], 1)
                    for n, src in enumerate((q, k)):
                        pe.wait_ge(Sb["a_n"], n + 1)
                        for kk in range(KD):
                            if n == 1:
                                pe.wait_ge(Sb["a_trc"], kk + 1)
                            for j in range(TJ):
                                mm = pe.transpose(ps[:, kk, P * j:P * j + P], src[:, j, P * kk:P * kk + P], ident[:, :])
                            mm.then_inc(Sb["a_tr"], 1)

                @blk.vector
                def _(dve):
                    for j in range(TJ):
                        dve.wait_ge(Sb["a_q"], j + 1)
                        dve.tensor_tensor(q[:, j, :], ps[:, j, :], bq[:, :], ALU.add).then_inc(Sb["a_qb"], 1)
                    def moments(n, t):
                        tv = heads(t[:, :, :])
                        dve.drain()
                        dve.tensor_reduce(mom[:, n, 0, :], tv, AX_X, ALU.add)
                        dve.drain()
                        dve.tensor_scalar(mom[:, n, 0, :], mom[:, n, 0, :], 1.0 / HD, None, ALU.mult)
                        dve.drain()
                        dve.tensor_tensor(tv, tv, each(n, 0), ALU.subtract)
                        dve.drain()
                        dve.tensor_tensor(heads(sq[:, :, :]), tv, tv, ALU.mult)
                        dve.drain()
                        dve.tensor_reduce(mom[:, n, 1, :], heads(sq[:, :, :]), AX_X, ALU.add)
                        dve.drain().then_inc(Sb["a_sq"], 1)

                    def each(n, i):
                        return mom[:, n, i, :].unsqueeze(2).broadcast_to((P, G, HD))

                    def scale(n, t):
                        dve.wait_ge(Sb["a_rs"], n + 1)
                        dve.tensor_tensor(heads(t[:, :, :]), heads(t[:, :, :]), each(n, 1), ALU.mult)
                        dve.drain().then_inc(Sb["a_n"], 1)

                    moments(0, q)
                    bh = bkv[:, :].rearrange("p (h e) -> p h e", e=2 * HD)
                    for j in range(TJ):
                        dve.wait_ge(Sb["a_k"], j + 1)
                        last = j == TJ - 1
                        kvp = ps[:, 4 + 2 * (j % 2):6 + 2 * (j % 2), :].rearrange("p n (h e) -> p (n h) e", e=2 * HD)
                        dve.tensor_tensor(k[:, j, :].rearrange("p (h d) -> p h d", d=HD), kvp[:, :, 0:HD],
                                          bh[:, :, 0:HD], ALU.add)
                        dst = v2[:, :, 0:HD] if last else v[:, j, :].rearrange("p (h d) -> p h d", d=HD)
                        dve.tensor_tensor(dst, kvp[:, :, HD:], bh[:, :, HD:], ALU.add).then_inc(Sb["a_kb"], 1)
                        if j == 0:
                            scale(0, q)
                    dve.wait_ge(Sb["a_d"], 1)
                    for n in range(2):
                        dve.tensor_tensor(kv3[:, D * n:D * n + D], ps[:, 4 + n, :], bdc[:, D * n:D * n + D],
                                          ALU.add)
                    dve.drain()
                    dve.tensor_scalar(kv3[:, :], kv3[:, :], isd[:, 1:2], None, ALU.mult)
                    dve.tensor_scalar(v2[:, :, 0:HD], v2[:, :, 0:HD], isd[:, 0:1], None, ALU.mult)
                    dve.drain()
                    dve.scalar_tensor_tensor(k[:, TJ - 1, :], k[:, TJ - 1, :], isd[:, 0:1], kv3[:, 0:D],
                                             ALU.mult, ALU.add)
                    dve.tensor_copy(v2[:, :, HD:], kv3[:, D:2 * D].rearrange("p (h d) -> p h d", d=HD))
                    moments(1, k)
                    scale(1, k)

                @blk.scalar
                def _(act):
                    for n in range(2):
                        act.wait_ge(Sb["a_sq"], n + 1)
                        act.activation(mom[:, n, 1, :], mom[:, n, 1, :], ACT.Ln, scale=1.0 / HD, bias=C.eps6[:, 0:1])
                        act.drain()
                        act.activation(mom[:, n, 1, :], mom[:, n, 1, :], ACT.Exp, scale=-0.5)
                        act.drain().then_inc(Sb["a_rs"], 1)
                        for kk in range(KD):
                            act.wait_ge(Sb["a_tr"], KD * n + kk + 1)
                            if n == 0:
                                for i in range(4):
                                    own = slice(HD * i, HD * i + HD)
                                    op = act.activation(qT[own, i, kk, :], ps[own, kk, :], ACT.Identity,
                                                        scale=nw[own, 0:1], bias=nw[own, 1:2])
                                op.then_inc(Sb["a_trc"], 1)
                            else:
                                act.activation(kT[:, kk, 0:NM], ps[:, kk, 0:NM], ACT.Identity, scale=nw[:, 2:3],
                                               bias=nw[:, 3:4])
                                act.activation(kT[:, kk, NM:L], ps[:, kk, NM:L], ACT.Identity, scale=nw[:, 4:5],
                                               bias=nw[:, 5:6])
            Sh.fresh()
            AT = dict(first=1 - H // 2, second=1, turn=3, project=5, add=6)
            with nc.Block() as blk:
                def tile_of(i, what):
                    j, rest = divmod(i + 1 - AT[what], H)
                    return j - 1 if rest == 0 and 1 <= j <= TJ else None

                UNITS = range(N + AT["add"])

                @blk.tensor
                def _(pe):
                    def scores(i):
                        j, h = divmod(i, H)
                        if i >= 3:
                            pe.wait_ge(Sh["h_exp"], i - 2)
                        pe.matmul(ps[:, i % 3, :], qT[:, h % 4, h // 4, P * j:P * j + P], kT[:, h // 4, :],
                                  start=True, stop=True).then_inc(Sh["h_s"], 1)

                    def turn(i):
                        pe.wait_ge(Sh["h_exp"], i + 1)
                        if i >= 2:
                            pe.wait_ge(Sh["h_ptc"], i - 1)
                        for t in range(TJ):
                            mm = pe.transpose(ps[:, 3 + i % 2, P * t:P * t + P], pr[:, i % 3, P * t:P * t + P],
                                              ident[:, :])
                        mm.then_inc(Sh["h_pt"], 1)

                    def mix(i):
                        j, h = divmod(i, H)
                        pe.wait_ge(Sh["h_ptc"], i + 1)
                        if j >= 1 and h % 8 == 0:
                            pe.wait_ge(Sh["h_half"], 2 * (j - 1) + h // 8 + 1)
                        bank = ps[:, 5 + h // 8, 64 * (h % 8):64 * (h % 8) + 64]
                        pe.matmul(bank, pT[:, i % 2, P * (TJ - 1):L], v2[:, h, :], start=True, stop=False,
                                  skip_group_check=True)
                        for t in range(TJ - 1):
                            mm = pe.matmul(bank[:, 0:HD], pT[:, i % 2, P * t:P * t + P],
                                           v[:, t, HD * h:HD * h + HD], start=False, stop=(t == TJ - 2),
                                           skip_group_check=True)
                        mm.then_inc(Sh["h_o"], 1)

                    scores(0)
                    scores(1)
                    for i in UNITS:
                        if i + 2 < N:
                            scores(i + 2)
                        if i < N:
                            turn(i)
                        if 1 <= i <= N:
                            mix(i - 1)
                        if (j := tile_of(i, "turn")) is not None:
                            pe.wait_ge(Sh["h_on"], j + 1)
                            if j >= 1:
                                pe.wait_ge(Sh["h_x"], j)
                            for kk in range(KD):
                                mm = pe.transpose(ps[:, 7, P * kk:P * kk + P], o[:, 0, P * kk:P * kk + P],
                                                  ident[:, :])
                            mm.then_inc(Sh["h_ot"], 1)
                        if (j := tile_of(i, "project")) is not None:
                            pe.wait_ge(Sh["h_otc"], j + 1)
                            for kk in range(KD):
                                mm = pe.matmul(ps[:, 7, :], o[:, 1, P * kk:P * kk + P], wo[:, kk, :],
                                               start=(kk == 0), stop=(kk == KD - 1))
                            mm.then_inc(Sh["h_y"], 1)

                @blk.vector
                def _(dve):
                    def half(j, n):
                        r = sm[:, j % 2, :, 8 * n:8 * n + 8]
                        dve.wait_ge(Sh["h_exp"], H * j + 8 * n + 8)
                        dve.reciprocal(r, r)
                        dve.drain()
                        dve.wait_ge(Sh["h_o"], H * j + 8 * n + 8)
                        if j >= 1 and n == 0:
                            dve.wait_ge(Sh["h_ot"], j)
                        ov = ps[:, 5 + n, :].rearrange("p (h s d) -> p h s d", s=2, d=HD)
                        for s in range(2):
                            dst = o[:, 2 * s, 256 * n:256 * n + 256].rearrange("p (h d) -> p h d", d=HD)
                            op = dve.tensor_tensor(dst, ov[:, :, s, :],
                                                   sm[:, j % 2, s, 8 * n:8 * n + 8].unsqueeze(2)
                                                   .broadcast_to((P, 8, HD)), ALU.mult)
                        op.then_inc(Sh["h_half"], 1)

                    def maxima(i):
                        m = nm[:, :, i % H, :]
                        dve.wait_ge(Sh["h_s"], i + 1)
                        dve.tensor_reduce(m[:, 0, 0:1], ps[:, i % 3, 0:NM], AX_X, ALU.max)
                        dve.tensor_reduce(m[:, 0, 1:2], ps[:, i % 3, NM:L], AX_X, ALU.max)
                        dve.drain()
                        dve.tensor_scalar(m[:, 1, :], m[:, 0, :], -float(HD) ** -0.5, None, ALU.mult)
                        dve.drain().then_inc(Sh["h_max"], 1)

                    maxima(0)
                    for i in UNITS:
                        if i + 1 < N:
                            maxima(i + 1)
                        if 1 <= i <= N:
                            dve.wait_ge(Sh["h_pt"], i)
                            if i >= 3:
                                dve.wait_ge(Sh["h_o"], i - 2)
                            dve.tensor_copy(pT[:, (i - 1) % 2, :], ps[:, 3 + (i - 1) % 2, :]
                                            ).then_inc(Sh["h_ptc"], 1)
                        if (j := tile_of(i, "first")) is not None:
                            half(j, 0)
                        if (j := tile_of(i, "second")) is not None:
                            half(j, 1)
                        if (j := tile_of(i, "add")) is not None:
                            xj = x[:, bass.ds(TJ * b + j, 1), :].rearrange("p a d -> p (a d)")
                            dve.wait_ge(Sh["h_bo"], j + 1)
                            dve.wait_ge(Sh["h_y"], j + 1)
                            dve.tensor_tensor(xj, xj, ps[:, 7, :], ALU.add).then_inc(Sh["h_x"], 1)

                @blk.gpsimd
                def _(pool):
                    for j in range(TJ):
                        pool.wait_ge(Sh["h_half"], 2 * j + 2)
                        pool.tensor_tensor(o[:, 0, :], o[:, 0, :], o[:, 2, :], ALU.add)
                        pool.drain().then_inc(Sh["h_on"], 1)
                        xj = x[:, bass.ds(TJ * b + j, 1), :].rearrange("p a d -> p (a d)")
                        pool.tensor_tensor(xj, xj, bo[:, :], ALU.add)
                        pool.drain().then_inc(Sh["h_bo"], 1)

                @blk.scalar
                def _(act):
                    for i in UNITS:
                        if i < N:
                            j, h = divmod(i, H)
                            act.wait_ge(Sh["h_max"], i + 1)
                            if i >= 3:
                                act.wait_ge(Sh["h_pt"], i - 2)
                            for s, (a, z) in enumerate(((0, NM), (NM, L))):
                                act.activation(pr[:, i % 3, a:z], ps[:, i % 3, a:z], ACT.Exp,
                                               bias=nm[:, 1, h, s:s + 1], scale=float(HD) ** -0.5,
                                               accum_out=sm[:, j % 2, s, h:h + 1])
                            act.drain().then_inc(Sh["h_exp"], 1)
                        if (j := tile_of(i, "turn")) is not None:
                            act.wait_ge(Sh["h_ot"], j + 1)
                            if j >= 1:
                                act.wait_ge(Sh["h_y"], j)
                            act.copy(o[:, 1, :], ps[:, 7, :]).then_inc(Sh["h_otc"], 1)


def expert_ffn(nc, C, W):
    E, F, TOK = 8, 448, B * L
    FM, FP = 4, 112
    x, ps, ident = C.x, C.ps, C.ident
    with ExitStack() as ctx:
        def sb(name, shape, dt=F32):
            return ctx.enter_context(nc.sbuf_tensor("e_" + name, shape, dt))

        S = Signals(nc, ctx, ["e_ld", "e_scr"])
        Sb = Signals(nc, ctx, LN_SIGNALS + ["e_sc", "e_scc", "e_max", "e_exp", "e_g", "e_gt"])
        Se = Signals(nc, ctx, ["ex_next", "ex_s", "ex_in", "ex_h", "ex_sl", "ex_g", "ex_y", "ex_yx"])
        C.xn = sb("xn", [P, TJ, D])
        xT = sb("xT", [P, KD, TOK])
        xTb = sb("xTb", [P, KD, L])
        gw = sb("gw", [P, KD, E])
        eb = sb("eb", [P, E])
        iota = sb("iota", [P, 32])
        sc = sb("sc", [P, TJ, E])
        top = sb("top", [P, TJ, 8])
        idx = sb("idx", [P, TJ, 8], U32)
        idxf = sb("idxf", [P, TJ, 2])
        sel = sb("sel", [P, TJ, E])
        e = sb("e", [P, TJ, E])
        bi = sb("bi", [P, TJ, E])
        nmx = sb("nmx", [P, TJ])
        sm = sb("sm", [P, TJ])
        gT = sb("gT", [E, TOK])
        w1 = [sb(f"w1_{n}", [P, KD, F]) for n in range(2)]
        w3 = [sb(f"w3_{n}", [P, KD, F]) for n in range(2)]
        w2 = [sb(f"w2_{n}", [FP, FM, D]) for n in range(2)]
        sbc = sb("sbc", [P, 2, TOK])
        sl = sb("sl", [FP, 2, L])
        hT = sb("hT", [FP, 2, FM, L])
        xs = sb("xs", [P, 2, KD, L])
        S.fresh()
        load_all(nc, S, [(gw[:, :, :], rows(W["L1_ffn_gate_w"])), (eb[:, :], everywhere(W["L1_ffn_expert_bias"])),
                         (iota[:, :], everywhere(W["c_iota"]))], "e_ld")
        with nc.Fori(0, B) as b:
            Sb.fresh()
            layernorm_T(nc, C, Sb, b, xTb)
            with nc.Block() as blk:
                @blk.tensor
                def _(pe):
                    for j in range(TJ):
                        for k in range(KD):
                            mm = pe.matmul(ps[:, 0, E * j:E * j + E], xTb[:, k, P * j:P * j + P], gw[:, k, :],
                                           start=(k == 0), stop=(k == KD - 1))
                    mm.then_inc(Sb["e_sc"], 1)
                    pe.wait_ge(Sb["e_g"], 1)
                    for j in range(TJ):
                        mm = pe.transpose(ps[0:E, 1, P * j:P * j + P], e[:, j, :], ident[:, :])
                    mm.then_inc(Sb["e_gt"], 1)

                @blk.scalar
                def _(act):
                    act.wait_ge(Sb["e_sc"], 1)
                    act.copy(sc[:, :, :], ps[:, 0, 0:TJ * E].rearrange("p (j s) -> p j s", s=E)
                             ).then_inc(Sb["e_scc"], 1)
                    act.wait_ge(Sb["e_max"], 1)
                    for j in range(TJ):
                        act.activation(e[:, j, :], sc[:, j, :], ACT.Exp, bias=nmx[:, j:j + 1], accum_out=sm[:, j:j + 1])
                    act.drain().then_inc(Sb["e_exp"], 1)
                    act.wait_ge(Sb["e_gt"], 1)
                    act.copy(gT[:, bass.ds(L * b, L)], ps[0:E, 1, :])

                @blk.vector
                def _(dve):
                    for k in range(KD):
                        dve.tensor_copy(xT[:, k, bass.ds(L * b, L)], xTb[:, k, :])
                    dve.wait_ge(Sb["e_scc"], 1)
                    dve.tensor_reduce(nmx[:, :], sc[:, :, :], AX_X, ALU.max, negate=True)
                    dve.drain().then_inc(Sb["e_max"], 1)
                    dve.wait_ge(Sb["e_exp"], 1)
                    dve.reciprocal(sm[:, :], sm[:, :])
                    dve.drain()
                    dve.tensor_tensor(e[:, :, :], e[:, :, :], sm[:, :].unsqueeze(2).broadcast_to((P, TJ, E)), ALU.mult)
                    dve.drain()
                    dve.tensor_tensor(bi[:, :, :], e[:, :, :], eb[:, :].unsqueeze(1).broadcast_to((P, TJ, E)), ALU.add)
                    dve.drain()
                    for j in range(TJ):
                        top_two(dve, bi[:, j, :], top[:, j, :], idx[:, j, :], idxf[:, j, :], iota, sel[:, j, :], E)
                    dve.tensor_tensor(e[:, :, :], e[:, :, :], sel[:, :, :], ALU.mult)
                    dve.drain().then_inc(Sb["e_g"], 1)
        def tall(ap):
            return ap.rearrange("(m p) n -> p m n", p=FP)

        def load_weights(queue, n, w1d, w3d, w2d, done):
            queue.dma_start(w1[n][:, :, :], rows(w1d)).then_inc(done, 16)
            queue.dma_start(w3[n][:, :, :], rows(w3d)).then_inc(done, 16)
            queue.dma_start(w2[n][:, :, :], tall(w2d)).then_inc(done, 16)

        def load_next(queue, n, i, done):
            load_weights(queue, n, *(W["L1_ffn_" + w][bass.ds(i, 1)].rearrange("a m n -> (a m) n")
                                     for w in ("w1", "w3", "w2")), done)

        S.fresh()
        with nc.Block() as blk:
            @blk.sync
            def _(sp):
                sp.dma_start(C.scratch[0:E, :], gT[:, :]).then_inc(S["e_scr"], 16)
                sp.dma_start(C.scratch[E:2 * E, :], gT[:, :]).then_inc(S["e_scr"], 16)
                sp.wait_ge(S["e_scr"], 32)

            @blk.scalar
            def _(act):
                load_weights(act, 1, W["L1_ffn_sw1"], W["L1_ffn_sw3"], W["L1_ffn_sw2"], S["e_ld"])
                act.wait_ge(S["e_ld"], 48)

        def expert(n, scored, nxt):
            Se.fresh()
            w1_, w3_, w2_ = w1[n], w3[n], w2[n]
            with nc.Block() as blk:
                @blk.sync
                def _(sp):
                    sp.dma_start(sbc[:, 1 - n, :], C.scratch[bass.ds(nxt + 1, 1), :].broadcast_to((P, TOK))
                                 ).then_inc(Se["ex_s"], 16)
                    load_next(sp, 1 - n, (nxt + E) % E if isinstance(nxt, int) else nxt, Se["ex_next"])
                    sp.wait_ge(Se["ex_s"], 16)
                    sp.wait_ge(Se["ex_next"], 48)

                @blk.gpsimd
                def _(pool):
                    if scored:
                        for b in range(1, B):
                            if b >= 2:
                                pool.wait_ge(Se["ex_h"], 2 * FM * (b - 1))
                            for k in range(KD):
                                pool.tensor_tensor(xs[:, b % 2, k, :], xT[:, k, L * b:L * b + L],
                                                   sbc[:, n, L * b:L * b + L], ALU.mult).then_inc(Se["ex_in"], 1)
                        pool.wait_ge(Se["ex_h"], 2 * FM * (B - 1))
                    pool.wait_ge(Se["ex_s"], 16)
                    for k in range(KD):
                        pool.tensor_tensor(xs[:, 0, k, :], xT[:, k, 0:L], sbc[:, 1 - n, 0:L], ALU.mult)

                @blk.tensor
                def _(pe):
                    def out(b):
                        pe.wait_ge(Se["ex_g"], FM * (b + 1))
                        for j in range(TJ):
                            if b >= 1:
                                pe.wait_ge(Se["ex_yx"], TJ * (b - 1) + j + 1)
                            for m in range(FM):
                                mm = pe.matmul(ps[:, 4 + j, :], hT[:, b % 2, m, P * j:P * j + P], w2_[:, m, :],
                                               start=(m == 0), stop=(m == FM - 1))
                            mm.then_inc(Se["ex_y"], 1)

                    for b in range(B):
                        for m in range(FM):
                            i = FM * b + m
                            for q, w in ((0, w1_), (1, w3_)):
                                if i >= 2:
                                    pe.wait_ge(Se["ex_g" if q else "ex_sl"], i - 1)
                                for k in range(KD):
                                    if scored:
                                        if b >= 1:
                                            pe.wait_ge(Se["ex_in"], KD * (b - 1) + k + 1)
                                        rhs = xs[:, b % 2, k, :]
                                    else:
                                        rhs = xT[:, k, L * b:L * b + L]
                                    mm = pe.matmul(ps[0:FP, 2 * (i % 2) + q, :], w[:, k, FP * m:FP * m + FP], rhs,
                                                   start=(k == 0), stop=(k == KD - 1))
                                mm.then_inc(Se["ex_h"], 1)
                        if b >= 1:
                            out(b - 1)
                    out(B - 1)

                @blk.scalar
                def _(act):
                    for i in range(FM * B):
                        act.wait_ge(Se["ex_h"], 2 * i + 1)
                        if i >= 2:
                            act.wait_ge(Se["ex_g"], i - 1)
                        act.activation(sl[:, i % 2, :], ps[0:FP, 2 * (i % 2), :], ACT.Silu).then_inc(Se["ex_sl"], 1)

                @blk.vector
                def _(dve):
                    def add(b):
                        for j in range(TJ):
                            dve.wait_ge(Se["ex_y"], TJ * b + j + 1)
                            dve.tensor_tensor(x[:, TJ * b + j, :], x[:, TJ * b + j, :], ps[:, 4 + j, :], ALU.add
                                              ).then_inc(Se["ex_yx"], 1)

                    for b in range(B):
                        for m in range(FM):
                            i = FM * b + m
                            dve.wait_ge(Se["ex_h"], 2 * i + 2)
                            dve.wait_ge(Se["ex_sl"], i + 1)
                            if m == 0 and b >= 2:
                                dve.wait_ge(Se["ex_y"], TJ * (b - 1))
                            dve.tensor_tensor(hT[:, b % 2, m, :], sl[:, i % 2, :], ps[0:FP, 2 * (i % 2) + 1, :],
                                              ALU.mult).then_inc(Se["ex_g"], 1)
                        if b >= 1:
                            add(b - 1)
                    add(B - 1)

        expert(1, False, -1)
        with nc.Fori(0, E // 2) as r:
            expert(0, True, 2 * r)
            expert(1, True, 2 * r + 1)


def program(nc, W, out, scratch, stages):
    with ExitStack() as ctx:
        C = Chip()
        sb = lambda name, shape: ctx.enter_context(nc.sbuf_tensor(name, shape, F32))
        C.x = sb("x", [P, NT, D])
        C.ident = sb("ident", [P, P])
        C.ones = sb("ones", [P, P])
        C.st = sb("st", [P, TJ, 6])
        C.mv = sb("mv", [P, TJ, 2])
        C.var = sb("var", [P, TJ])
        C.ss = sb("ss", [P, TJ])
        C.rstd = sb("rstd", [P, TJ])
        C.eps5 = sb("eps5", [P, 1])
        C.eps6 = sb("eps6", [P, 1])
        C.lnsd = sb("lnsd", [P, 1])
        C.ps = ctx.enter_context(nc.psum_tensor("ps", [P, 8, 512], F32))
        C.scratch = scratch
        S = Signals(nc, ctx, ["x_in", "x_out"])
        xv = W["x"].rearrange("b (j p) d -> p (b j) d", p=P)
        ov = out.rearrange("b (j p) d -> p (b j) d", p=P)
        with nc.Block() as blk:
            @blk.sync
            def _(sp):
                for b in range(B):
                    sp.dma_start(C.x[:, TJ * b:TJ * b + TJ, :], xv[:, TJ * b:TJ * b + TJ, :]).then_inc(S["x_in"], 16)
                sp.dma_start(C.ident[:, :], W["c_ident"]).then_inc(S["x_in"], 16)
                sp.wait_ge(S["x_in"], 16 * (B + 1))

            @blk.vector
            def _(dve):
                dve.memset(C.ones[:, :], 1.0)
                dve.memset(C.eps5[:, :], 1e-5)
                dve.memset(C.eps6[:, :], 1e-6)
                dve.memset(C.lnsd[:, :], LOG_RSQRT_P)
        for stage in stages:
            stage(nc, C, W)
        with nc.Block() as blk:
            @blk.sync
            def _(sp):
                for b in range(B):
                    sp.dma_start(ov[:, TJ * b:TJ * b + TJ, :], C.x[:, TJ * b:TJ * b + TJ, :]).then_inc(S["x_out"], 16)
                sp.wait_ge(S["x_out"], 16 * B)


def shape_constants():
    import numpy as np
    mask = np.zeros((P, len(LEVELS), P // 2), np.float32)
    second = np.zeros((P, len(LEVELS)), np.float32)
    for l, w in enumerate(LEVELS):
        second[:, l] = np.arange(P) // w % 2
        t = np.arange(P).reshape(-1, 2, w)[:, 1, :].reshape(-1)
        mask[:, l, :] = (np.arange(P)[:, None] // (2 * w) == t[None, :] // (2 * w)) & (second[:, l:l + 1] == 0)
    heads = np.kron(np.eye(4), np.ones((32, 32))).astype(np.float32)
    return {"c_heads": heads, "c_ident": np.eye(P, dtype=np.float32), "c_mask": mask, "c_masku": mask.astype(np.uint32),
            "c_rowm": second, "c_rown": second - 1, "c_iota": np.arange(32, dtype=np.float32),
            "c_isd": np.stack([np.arange(P) < P - 16, np.arange(P) >= P - 16], 1).astype(np.float32)}


def kernel(**inputs):
    import numpy as np
    import concourse.bacc as bacc
    from concourse.bass_utils import run_bass_kernel_spmd as run

    nc = bacc.Bacc("TRN2", target_bir_lowering=False, num_devices=1)
    arrays = {n: np.ascontiguousarray(layout(n, np.asarray(a))) for n, a in inputs.items()}
    arrays.update(shape_constants())
    W = {n: nc.dram_tensor("in_" + n, a.shape, mybir.dt.from_np(a.dtype), kind="ExternalInput").ap()
         for n, a in arrays.items()}
    out = nc.dram_tensor("out_0", (B, L, D), F32, kind="ExternalOutput").ap()
    scratch = nc.dram_tensor("scratch", (16, B * L), F32).ap()
    program(nc, W, out, scratch, STAGES)
    r = run(nc, [{"in_" + n: a for n, a in arrays.items()}], core_ids=[0])
    return r.results[0]["out_0"]


def layout(name, a):
    import numpy as np
    if name == "ctx_1024":
        return a.transpose(0, 2, 1)
    if name in ("L0_xattn_Wq", "L0_xattn_Wk", "L0_ffn_Wr"):
        return a.T
    if name in ("L1_attn_Wq", "L1_attn_Wk", "L1_attn_Wv", "L1_attn_Wfb", "L1_attn_Wgb"):
        return np.roll(a, -P, axis=1)
    if name in ("L1_ffn_w1", "L1_ffn_w2", "L1_ffn_w3"):
        return np.roll(a, -1, axis=0)
    if name in PER_CHANNEL:
        return a.reshape(-1, min(P, a.size)).T
    if name == "L0_attn_bkg2":
        return a.reshape(KD, 4, 16).transpose(1, 2, 0)
    if name == "L0_ffn_U":
        return a.transpose(1, 0, 2).reshape(D, -1)
    if name == "L0_ffn_V":
        return a.reshape(-1, D)
    return a


PER_CHANNEL = ("L0_attn_ln1_w", "L0_attn_ln2_w", "L0_xattn_bq", "L0_xattn_bk", "L1_attn_dt_bias", "L1_attn_o_norm_w",
               "L1_xattn_qn_w", "L1_xattn_qn_b", "L1_xattn_kn_w", "L1_xattn_kn_b", "L1_xattn_kn_dca_w",
               "L1_xattn_kn_dca_b")
LOG_RSQRT_P = -0.5 * math.log(P)
STAGES = [gla_layer, context_mix, low_rank_ffn, delta_attention, cross_attention, expert_ffn]
```
